# Optimizing a Trainium2 kernel written in Bass

```python
import numpy as np
import jax
import jax.numpy as jnp

def _softmax(x, axis=-1):
    return jax.nn.softmax(x, axis=axis)

def _gelu(x):
    return jax.nn.gelu(x, approximate=True)

def _silu(x):
    return jax.nn.silu(x)

def _sigmoid(x):
    return jax.nn.sigmoid(x)

def _layernorm(x, axis=-1, eps=1e-05):
    m = jnp.mean(x, axis=axis, keepdims=True)
    v = jnp.var(x, axis=axis, keepdims=True)
    return (x - m) / jnp.sqrt(v + eps)

def _scatter_add(tgt, idx, src, axis=0):
    return tgt.at[idx].add(src)

def _segment_sum(src, seg, n):
    return jax.ops.segment_sum(src, seg, n)
kernel_name = 'mk_cond_seq_d2_seqx_r2_fbd02a'

def setup_inputs(seed: int=0):
    np.random.seed(seed)
    _w = jnp.asarray

    def _rec_inputs():
        import jax
        import jax.numpy as jnp
        _rk = jax.random.key(seed)
        x = -0.0003929 + 0.9999 * jax.random.normal(jax.random.fold_in(_rk, 1), (32, 128, 512), jnp.float32)
        _lenS = 128 - jax.random.randint(jax.random.fold_in(_rk, 7), (32,), 0, max(1, 128 // 4) + 1, jnp.int32)
        _lenS2 = 128 - jax.random.randint(jax.random.fold_in(_rk, 8), (32,), 0, max(1, 128 // 4) + 1, jnp.int32)
        cond_2048 = 0.00782532 + 1.00527 * jax.random.normal(jax.random.fold_in(_rk, 11), (32, 1024), jnp.float32)
        _validS = jnp.arange(128)[None, :] < _lenS[:, None]
        _validS2 = jnp.arange(128)[None, :] < _lenS2[:, None]
        _causal = jnp.tril(jnp.ones((128, 128), dtype=bool))
        mask_BxS_ik0 = jnp.where(jnp.broadcast_to(_validS[:, :], (32, 128)), 0, 1).astype(jnp.int32)
        mask_BxS_ff1 = jnp.where(jnp.ones((32, 128), dtype=bool), 1.0, 0.0).astype(jnp.float32)
        return (x, cond_2048, mask_BxS_ik0, mask_BxS_ff1)
    x, cond_2048, mask_BxS_ik0, mask_BxS_ff1 = _rec_inputs()

    def _L0_cond_setup():
        import jax, jax.numpy as jnp
        import numpy as np
        H = 16
        LN_EPS = 1e-05

        def _layernorm(x, scale, bias):
            mu = jnp.mean(x, axis=-1, keepdims=True)
            var = jnp.var(x, axis=-1, keepdims=True)
            return (x - mu) * jax.lax.rsqrt(var + LN_EPS) * scale + bias
        key = jax.random.key(seed)
        ks = jax.random.split(key, 8)
        B, T, D, E = (4, 2048, 512, 1024)
        s = 0.02
        return {'x': jax.random.normal(ks[0], (B, T, D), jnp.float32), 'emb': jax.random.normal(ks[1], (B, E), jnp.float32), 'src_mask': jax.random.randint(ks[2], (B, T), 0, 2).astype(jnp.int32), 'norm_scale': jnp.ones((D,), jnp.float32), 'norm_bias': jnp.zeros((D,), jnp.float32), 'Wq': jax.random.normal(ks[3], (D, D), jnp.float32) * s, 'bq': jnp.zeros((D,), jnp.float32), 'Wk': jax.random.normal(ks[4], (D, D), jnp.float32) * s, 'bk': jnp.zeros((D,), jnp.float32), 'Wv': jax.random.normal(ks[5], (D, D), jnp.float32) * s, 'bv': jnp.zeros((D,), jnp.float32), 'film_emb_W': jax.random.normal(ks[6], (E, 2 * D), jnp.float32) * s, 'film_emb_b': jnp.zeros((2 * D,), jnp.float32), 'film_norm_scale': jnp.ones((D,), jnp.float32), 'film_norm_bias': jnp.zeros((D,), jnp.float32), 'film_out_W': jax.random.normal(ks[7], (D, D), jnp.float32) * s, 'film_out_b': jnp.zeros((D,), jnp.float32)}
    _L0_cond_all = _L0_cond_setup()
    _L0_cond_in = {k: v for k, v in _L0_cond_all.items() if k in ('norm_scale', 'norm_bias', 'Wq', 'bq', 'Wk', 'bk', 'Wv', 'bv', 'film_emb_W', 'film_emb_b', 'film_norm_scale', 'film_norm_bias', 'film_out_W', 'film_out_b')}
    del _L0_cond_all

    def _L1_cond_setup():
        import jax, jax.numpy as jnp
        import numpy as np
        B, T, D, H, TE = (8, 512, 512, 16, 1024)
        LN_EPS = 1e-05

        def layer_norm(x, w, b):
            m = jnp.mean(x, axis=-1, keepdims=True)
            v = jnp.var(x, axis=-1, keepdims=True)
            return (x - m) / jnp.sqrt(v + LN_EPS) * w + b
        key = jax.random.key(seed)
        ks = jax.random.split(key, 8)
        s = lambda k, sh: jax.random.normal(k, sh, jnp.float32) * 0.02
        return dict(x=jax.random.normal(ks[0], (B, T, D), jnp.float32), emb=jax.random.normal(ks[1], (B, TE), jnp.float32), src_mask=jnp.ones((B, T), jnp.float32), norm_w=jnp.ones((D,), jnp.float32), norm_b=jnp.zeros((D,), jnp.float32), q_w=s(ks[2], (D, D)), q_b=jnp.zeros((D,), jnp.float32), k_w=s(ks[3], (D, D)), k_b=jnp.zeros((D,), jnp.float32), v_w=s(ks[4], (D, D)), v_b=jnp.zeros((D,), jnp.float32), emb_w=s(ks[5], (TE, 2 * D)), emb_b=jnp.zeros((2 * D,), jnp.float32), sb_norm_w=jnp.ones((D,), jnp.float32), sb_norm_b=jnp.zeros((D,), jnp.float32), out_w=s(ks[6], (D, D)), out_b=jnp.zeros((D,), jnp.float32))
    _L1_cond_all = _L1_cond_setup()
    _L1_cond_in = {k: v for k, v in _L1_cond_all.items() if k in ('norm_w', 'norm_b', 'q_w', 'q_b', 'k_w', 'k_b', 'v_w', 'v_b', 'emb_w', 'emb_b', 'sb_norm_w', 'sb_norm_b', 'out_w', 'out_b')}
    del _L1_cond_all
    return {'x': x, 'cond_2048': cond_2048, 'mask_BxS_ik0': mask_BxS_ik0, 'mask_BxS_ff1': mask_BxS_ff1, 'L0_cond_norm_scale': _L0_cond_in['norm_scale'], 'L0_cond_norm_bias': _L0_cond_in['norm_bias'], 'L0_cond_Wq': _L0_cond_in['Wq'], 'L0_cond_bq': _L0_cond_in['bq'], 'L0_cond_Wk': _L0_cond_in['Wk'], 'L0_cond_bk': _L0_cond_in['bk'], 'L0_cond_Wv': _L0_cond_in['Wv'], 'L0_cond_bv': _L0_cond_in['bv'], 'L0_cond_film_emb_W': _L0_cond_in['film_emb_W'], 'L0_cond_film_emb_b': _L0_cond_in['film_emb_b'], 'L0_cond_film_norm_scale': _L0_cond_in['film_norm_scale'], 'L0_cond_film_norm_bias': _L0_cond_in['film_norm_bias'], 'L0_cond_film_out_W': _L0_cond_in['film_out_W'], 'L0_cond_film_out_b': _L0_cond_in['film_out_b'], 'L1_cond_norm_w': _L1_cond_in['norm_w'], 'L1_cond_norm_b': _L1_cond_in['norm_b'], 'L1_cond_q_w': _L1_cond_in['q_w'], 'L1_cond_q_b': _L1_cond_in['q_b'], 'L1_cond_k_w': _L1_cond_in['k_w'], 'L1_cond_k_b': _L1_cond_in['k_b'], 'L1_cond_v_w': _L1_cond_in['v_w'], 'L1_cond_v_b': _L1_cond_in['v_b'], 'L1_cond_emb_w': _L1_cond_in['emb_w'], 'L1_cond_emb_b': _L1_cond_in['emb_b'], 'L1_cond_sb_norm_w': _L1_cond_in['sb_norm_w'], 'L1_cond_sb_norm_b': _L1_cond_in['sb_norm_b'], 'L1_cond_out_w': _L1_cond_in['out_w'], 'L1_cond_out_b': _L1_cond_in['out_b']}

def reference(x, cond_2048, mask_BxS_ik0, mask_BxS_ff1, L0_cond_norm_scale, L0_cond_norm_bias, L0_cond_Wq, L0_cond_bq, L0_cond_Wk, L0_cond_bk, L0_cond_Wv, L0_cond_bv, L0_cond_film_emb_W, L0_cond_film_emb_b, L0_cond_film_norm_scale, L0_cond_film_norm_bias, L0_cond_film_out_W, L0_cond_film_out_b, L1_cond_norm_w, L1_cond_norm_b, L1_cond_q_w, L1_cond_q_b, L1_cond_k_w, L1_cond_k_b, L1_cond_v_w, L1_cond_v_b, L1_cond_emb_w, L1_cond_emb_b, L1_cond_sb_norm_w, L1_cond_sb_norm_b, L1_cond_out_w, L1_cond_out_b):
    import jax
    import jax.numpy as jnp

    def _L0_cond_ref(x, emb, src_mask, norm_scale, norm_bias, Wq, bq, Wk, bk, Wv, bv, film_emb_W, film_emb_b, film_norm_scale, film_norm_bias, film_out_W, film_out_b):
        import jax, jax.numpy as jnp
        import numpy as np
        H = 16
        LN_EPS = 1e-05

        def _layernorm(x, scale, bias):
            mu = jnp.mean(x, axis=-1, keepdims=True)
            var = jnp.var(x, axis=-1, keepdims=True)
            return (x - mu) * jax.lax.rsqrt(var + LN_EPS) * scale + bias
        B, T, D = x.shape
        dh = D // H
        xn = _layernorm(x, norm_scale, norm_bias)
        q = xn @ Wq + bq
        k = xn @ Wk + bk
        v = xn @ Wv + bv
        mask = (src_mask == 1)[:, :, None]
        k = jnp.where(mask, -jnp.inf, k)
        v = jnp.where(mask, 0.0, v)
        q = q.reshape(B, T, H, dh).transpose(0, 2, 1, 3)
        k = k.reshape(B, T, H, dh).transpose(0, 2, 1, 3)
        v = v.reshape(B, T, H, dh).transpose(0, 2, 1, 3)
        q = jax.nn.softmax(q, axis=-1)
        k = jax.nn.softmax(k, axis=2)
        attn = jnp.einsum('bhse,bhsd->bhed', k, v)
        y = jnp.einsum('bhtd,bhed->bhte', q, attn)
        y = y.transpose(0, 2, 1, 3).reshape(B, T, D)
        emb_out = jax.nn.silu(emb) @ film_emb_W + film_emb_b
        scale, shift = jnp.split(emb_out, 2, axis=-1)
        h = _layernorm(y, film_norm_scale, film_norm_bias) * (1.0 + scale[:, None, :]) + shift[:, None, :]
        h = jax.nn.silu(h) @ film_out_W + film_out_b
        return x + h

    def _L1_cond_ref(x, emb, src_mask, norm_w, norm_b, q_w, q_b, k_w, k_b, v_w, v_b, emb_w, emb_b, sb_norm_w, sb_norm_b, out_w, out_b):
        import jax, jax.numpy as jnp
        import numpy as np
        B, T, D, H, TE = (8, 512, 512, 16, 1024)
        LN_EPS = 1e-05

        def layer_norm(x, w, b):
            m = jnp.mean(x, axis=-1, keepdims=True)
            v = jnp.var(x, axis=-1, keepdims=True)
            return (x - m) / jnp.sqrt(v + LN_EPS) * w + b
        Bx, Tx, Dx = x.shape
        xn = layer_norm(x, norm_w, norm_b)
        q = (xn @ q_w + q_b).reshape(Bx, Tx, H, -1)
        k = (xn @ k_w + k_b).reshape(Bx, Tx, H, -1)
        att = jnp.einsum('bnhl,bmhl->bnmh', q, k)
        mask = src_mask.reshape(Bx, 1, Tx, 1)
        att = att + (1.0 - mask) * -1000000.0
        att = jax.nn.softmax(att, axis=2)
        v = ((xn @ v_w + v_b) * src_mask[:, :, None]).reshape(Bx, Tx, H, -1)
        y = jnp.einsum('bnmh,bmhl->bnhl', att, v).reshape(Bx, Tx, Dx)
        e = jax.nn.silu(emb) @ emb_w + emb_b
        scale, shift = jnp.split(e[:, None, :], 2, axis=2)
        h = layer_norm(y, sb_norm_w, sb_norm_b) * (1.0 + scale) + shift
        h = jax.nn.silu(h) @ out_w + out_b
        return x + h
    x = _L0_cond_ref(x, cond_2048, mask_BxS_ik0, L0_cond_norm_scale, L0_cond_norm_bias, L0_cond_Wq, L0_cond_bq, L0_cond_Wk, L0_cond_bk, L0_cond_Wv, L0_cond_bv, L0_cond_film_emb_W, L0_cond_film_emb_b, L0_cond_film_norm_scale, L0_cond_film_norm_bias, L0_cond_film_out_W, L0_cond_film_out_b)
    x = _L1_cond_ref(x, cond_2048, mask_BxS_ff1, L1_cond_norm_w, L1_cond_norm_b, L1_cond_q_w, L1_cond_q_b, L1_cond_k_w, L1_cond_k_b, L1_cond_v_w, L1_cond_v_b, L1_cond_emb_w, L1_cond_emb_b, L1_cond_sb_norm_w, L1_cond_sb_norm_b, L1_cond_out_w, L1_cond_out_b)
    return x

_drawn_inputs = setup_inputs


def setup_inputs(seed=0):
    import zlib

    import numpy as np

    out = dict(_drawn_inputs(seed))
    spreads = {'L0_cond_norm_scale': (1.0, 0.2),
     'L0_cond_norm_bias': (0.0, 0.1),
     'L0_cond_bq': (0.0, 0.1),
     'L0_cond_bk': (0.0, 0.8),
     'L0_cond_bv': (0.0, 0.1),
     'L0_cond_film_emb_b': (0.0, 0.1),
     'L0_cond_film_norm_scale': (1.0, 0.2),
     'L0_cond_film_norm_bias': (0.0, 0.1),
     'L0_cond_film_out_b': (0.0, 0.1),
     'L1_cond_norm_w': (1.0, 0.2),
     'L1_cond_norm_b': (0.0, 0.1),
     'L1_cond_q_b': (0.0, 0.274),
     'L1_cond_k_b': (0.0, 0.8),
     'L1_cond_v_b': (0.0, 0.1),
     'L1_cond_emb_b': (0.0, 0.1),
     'L1_cond_sb_norm_w': (1.0, 0.2),
     'L1_cond_sb_norm_b': (0.0, 0.1),
     'L1_cond_out_b': (0.0, 0.1)}
    factors = {}
    for name, (base, spread) in spreads.items():
        noise = np.random.default_rng([zlib.crc32(name.encode()), seed]).standard_normal(out[name].shape)
        drawn = base * np.exp(spread * noise) if base else spread * noise
        out[name] = jnp.asarray(drawn.astype(out[name].dtype))
    for name, factor in factors.items():
        out[name] = (out[name] * factor).astype(out[name].dtype)
    return out
```

```python
from contextlib import ExitStack

import concourse.bass as bass
from concourse import mybir

F32 = mybir.dt.float32
F32R = mybir.dt.float32r
BF16 = mybir.dt.bfloat16
I32 = mybir.dt.int32
ALU = mybir.AluOpType
ACT = mybir.ActivationFunctionType
AX = mybir.AxisListType

P = 128
B, T, D, E = 32, 128, 512, 1024
H, DH = 16, 32
C = D // P
HC = H // C
V1 = DH + 1
EC = E // P
FC = 2 * C
NP = B // 2
EPS = 1e-5
BIG = 1e30
SCORE_OFF = -1e6

NS, NB, FS, FB, EB = 0, 4, 8, 12, 16
ROWS = 24


class Pair:

    def __init__(self, i, j):
        self.i, self.j = i, j
        self.par = j % 2

    def plus(self, n):
        return Pair(self.i, self.j + n)

    def times(self, n, k=0):
        return self.i * (2 * n) + (self.j * n + k)

    def use(self):
        return self.i + (self.j // 2 + 1)


def at(t):
    return Pair(t // 2, t % 2)


def need(eng, sem, count):
    if not isinstance(count, int) or count > 0:
        eng.wait_ge(sem, count)


def slots(eng, slot):
    slot(at(0), True, True, True)
    slot(at(1), False, True, True)
    with eng.Fori(1, NP // 2 - 1) as i:
        slot(Pair(i, 0), False, True, True)
        slot(Pair(i, 1), False, True, True)
    slot(at(NP - 2), False, True, True)
    slot(at(NP - 1), False, True, False)
    slot(at(NP), False, False, False)


def pairs_of(x):
    return x.rearrange("(g s) t d -> g t s d", s=2)


def chained(eng, sem):
    count = [0]

    def link(ins):
        count[0] += 1
        ins.then_inc(sem, 1)
        eng.wait_ge(sem, count[0])

    return link


def prepare_shared(nc, a, g):
    with ExitStack() as ctx:
        def sb(name, shape, dt=F32):
            return ctx.enter_context(nc.sbuf_tensor(name, shape, dt))

        def ps(name, shape):
            return ctx.enter_context(nc.psum_tensor(name, shape, F32))

        def sem(name):
            return ctx.enter_context(nc.semaphore(name))

        rows = sb("rows", [2 * ROWS, P])
        cond = sb("cond", [B, E])
        cond_tanh = sb("cond_tanh", [B, E])
        keep_mask = sb("keep_mask", [B, T], I32)
        score_mask = sb("score_mask", [B, T])
        maskf = sb("maskf", [B, T])
        mask_b = sb("mask_b", [B, T], BF16)
        off = sb("off", [B, T])
        rest = sb("rest", [B, T])
        count = sb("count", [B, 1])
        part = sb("part", [B, 3, T], BF16)
        emb_w = sb("emb_w", [P, EC, E])
        one_plus = sb("one_plus", [P, C, B])
        shift = sb("shift", [P, C, B])
        turned = ps("turned", [P, 512])
        cond_t = ps("cond_t", [P, EC, B])
        emb = ps("emb", [P, FC, B])

        rows_in, cond_in, masks_in = sem("rows_in"), sem("cond_in"), sem("masks_in")
        emb_in = [sem("emb_in0"), sem("emb_in1")]
        ident_zero, ident_done, consts_done = sem("ident_zero"), sem("ident_done"), sem("consts_done")
        rows_zero, parts_done, rows_out = sem("rows_zero"), sem("parts_done"), sem("rows_out")
        tanh_done, silu_done, cond_turned = sem("tanh_done"), sem("silu_done"), sem("cond_turned")
        cond_copied, vec_turned, mask_turned = sem("cond_copied"), sem("vec_turned"), sem("mask_turned")
        emb_done, emb_read, chain = sem("emb_done"), sem("emb_read"), sem("chain")
        mask_ready = sem("mask_ready")

        block = ctx.enter_context(nc.Block())

        @block.sync
        def _(sp):
            for n, ins in enumerate(a["vectors"]):
                for x, r0 in ins:
                    r = x.rearrange("(c p) -> c p", p=P)
                    sp.dma_start(rows[n * ROWS + r0:n * ROWS + r0 + r.shape[0], :], r).then_inc(rows_in, 16)
            sp.dma_start(cond[:], a["cond"]).then_inc(cond_in, 16)
            sp.dma_start(keep_mask[:], a["mask0"]).then_inc(masks_in, 16)
            sp.dma_start(score_mask[:], a["mask1"]).then_inc(masks_in, 16)
            for n in range(2):
                if n == 1:
                    sp.wait_ge(emb_done, 1)
                sp.dma_start(emb_w[:], a["emb_w"][n].rearrange("(k p) f -> p k f", p=P)).then_inc(emb_in[n], 16)
                if n == 0:
                    sp.wait_ge(parts_done, 2)
                    sp.wait_ge(rows_zero, 4)
                    sp.dma_start(g["mask_rows"][3:4, :].rearrange("a (b t) -> a b t", b=B),
                                 mask_b[:]).then_inc(rows_out, 16)
                    for r in range(3):
                        sp.dma_start(g["off_rows"][r:r + 1, :].rearrange("a (b t) -> a b t", b=B),
                                     part[:, r, :]).then_inc(rows_out, 16)
            sp.wait_ge(rows_out, 64)

        @block.gpsimd
        def _(pool):
            ident, three = g["ident"], g["three"]
            nc.gpsimd.memset(ident[:], 0.0).then_inc(ident_zero, 1)
            nc.gpsimd.memset(three[:], 1.0).then_inc(ident_zero, 1)
            nc.gpsimd.memset(g["eps"][:], EPS).then_inc(consts_done, 1)
            nc.gpsimd.memset(g["power"][:], -0.5).then_inc(consts_done, 1)
            pool.wait_ge(ident_zero, 2)
            nc.gpsimd.affine_select(out=ident[:], in_=ident[:], compare_op=ALU.not_equal, fill=1.0,
                                    base=0, pattern=[[-1, P]], channel_multiplier=1).then_inc(ident_done, 1)
            nc.gpsimd.affine_select(out=three[:], in_=three[:], compare_op=ALU.is_ge, fill=0.0,
                                    base=2, pattern=[[0, P]], channel_multiplier=-1).then_inc(ident_done, 1)
            nc.gpsimd.memset(g["mask_rows"][:], 0.0).then_inc(rows_zero, 1)
            nc.gpsimd.memset(g["off_rows"][:], 0.0).then_inc(rows_zero, 1)
            pool.wait_ge(rows_zero, 2)
            nc.gpsimd.memset(g["mask_rows"][0:3, :], 1.0).then_inc(rows_zero, 2)

        @block.scalar
        def _(act):
            act.wait_ge(cond_in, 16)
            nc.scalar.activation(cond_tanh[:], cond[:], ACT.Tanh, scale=0.5).then_inc(tanh_done, 1)

        @block.tensor
        def _(pe):
            ident = g["ident"]
            pe.wait_ge(ident_done, 2)
            pe.wait_ge(rows_in, 16 * 2 * 5)
            nc.tensor.transpose(turned[:, 0:2 * ROWS], rows[:], ident[0:2 * ROWS, 0:2 * ROWS]).then_inc(vec_turned, 1)
            pe.wait_ge(mask_ready, 2)
            nc.tensor.transpose(turned[:, 64:64 + B], maskf[:], ident[0:B, 0:B]).then_inc(mask_turned, 1)
            nc.tensor.transpose(turned[:, 128:128 + B], off[:], ident[0:B, 0:B]).then_inc(mask_turned, 1)
            nc.tensor.transpose(turned[:, 192:192 + B], score_mask[:], ident[0:B, 0:B]).then_inc(mask_turned, 1)
            pe.wait_ge(silu_done, 1)
            for k in range(EC):
                last = nc.tensor.transpose(cond_t[:, k, :], cond[:, k * P:(k + 1) * P], ident[0:B, 0:B])
            last.then_inc(cond_turned, 1)
            pe.wait_ge(cond_copied, 1)
            for n in range(2):
                pe.wait_ge(emb_in[n], 16)
                if n == 1:
                    pe.wait_ge(emb_read, 1)
                for f in range(FC):
                    for k in range(EC):
                        last = nc.tensor.matmul(emb[:, f, :], emb_w[:, k, f * P:(f + 1) * P], g["condT"][:, k, :],
                                                start=(k == 0), stop=(k == EC - 1))
                last.then_inc(emb_done, 1)

        @block.vector
        def _(dve):
            link = chained(dve, chain)
            vec, film = g["vec"], g["film"]
            dve.wait_ge(masks_in, 32)
            link(nc.vector.tensor_scalar(maskf[:], keep_mask[:], 1.0, None, ALU.is_equal))
            nc.vector.tensor_copy(mask_b[:], maskf[:]).then_inc(parts_done, 1)
            dve.wait_ge(parts_done, 1)
            link(nc.vector.tensor_scalar(maskf[:], maskf[:], -1.0, 1.0, ALU.mult, ALU.add))
            link(nc.vector.tensor_reduce(count[:], maskf[:], AX.X, ALU.add))
            link(nc.vector.reciprocal(count[:], count[:]))
            link(nc.vector.tensor_scalar(count[:], count[:], 0.0, None, ALU.mult))
            link(nc.vector.tensor_scalar(maskf[:], maskf[:], count[:, 0:1], None, ALU.add))
            link(nc.vector.tensor_scalar(off[:], score_mask[:], 1.0, -SCORE_OFF, ALU.subtract, ALU.mult))
            nc.vector.tensor_copy(rest[:], off[:]).then_inc(mask_ready, 2)
            dve.wait_ge(mask_ready, 2)
            link(nc.vector.tensor_copy(part[:, 0, :], rest[:]))
            link(nc.vector.tensor_tensor(out=rest[:], in0=rest[:], in1=part[:, 0, :], op=ALU.subtract))
            link(nc.vector.tensor_copy(part[:, 1, :], rest[:]))
            link(nc.vector.tensor_tensor(out=rest[:], in0=rest[:], in1=part[:, 1, :], op=ALU.subtract))
            nc.vector.tensor_copy(part[:, 2, :], rest[:]).then_inc(parts_done, 1)
            dve.wait_ge(vec_turned, 1)
            dve.wait_ge(mask_turned, 3)
            link(nc.vector.tensor_copy(vec[:], turned[:, 0:2 * ROWS]))
            link(nc.vector.tensor_copy(g["valid"][:], turned[:, 64:64 + B]))
            link(nc.vector.tensor_copy(g["score_keep"][:], turned[:, 192:192 + B]))
            link(nc.vector.tensor_copy(g["score_off"][:], turned[:, 128:128 + B]))
            dve.wait_ge(tanh_done, 1)
            nc.vector.scalar_tensor_tensor(out=cond[:], in0=cond_tanh[:], scalar=1.0, in1=cond[:],
                                           op0=ALU.add, op1=ALU.mult).then_inc(silu_done, 1)
            dve.wait_ge(cond_turned, 1)
            nc.vector.tensor_scalar(g["condT"][:], cond_t[:], 0.5, None, ALU.mult).then_inc(cond_copied, 1)
            for n in range(2):
                v = n * ROWS
                dve.wait_ge(emb_done, n + 1)
                for c in range(C):
                    link(nc.vector.tensor_scalar(one_plus[:, c, :], emb[:, c, :], vec[:, v + EB + c:v + EB + c + 1], 1.0,
                                                 ALU.add, ALU.add))
                    last = nc.vector.tensor_scalar(shift[:, c, :], emb[:, C + c, :],
                                                   vec[:, v + EB + C + c:v + EB + C + c + 1], None, ALU.add)
                    link(last)
                    link(nc.vector.tensor_scalar(film[:, n, 0, :, c], one_plus[:, c, :],
                                                 vec[:, v + FS + c:v + FS + c + 1], None, ALU.mult))
                    link(nc.vector.scalar_tensor_tensor(out=film[:, n, 1, :, c], in0=one_plus[:, c, :],
                                                        scalar=vec[:, v + FB + c:v + FB + c + 1], in1=shift[:, c, :],
                                                        op0=ALU.mult, op1=ALU.add))
                nc.vector.memset(shift[:], 0.0).then_inc(emb_read, 1)
                dve.wait_ge(emb_read, n + 1)


def prepare_layer(nc, a, g, n):
    with ExitStack() as ctx:
        def sb(name, shape, dt=F32):
            return ctx.enter_context(nc.sbuf_tensor(f"{name}_{n}", shape, dt))

        def ps(name, shape):
            return ctx.enter_context(nc.psum_tensor(f"{name}_{n}", shape, F32))

        def sem(name):
            return ctx.enter_context(nc.semaphore(f"{name}_{n}"))

        raw = sb("raw", [P, 4, C, D])
        norm_bias = sb("norm_bias", [P, C, P])
        full = sb("full", [P, 2, D])
        piece = sb("piece", [P, D])
        piece_b = sb("piece_b", [P, 3, D], BF16)
        big = sb("big", [P, 1])
        through = [ps(f"through{m}", [P, D]) for m in range(3)]
        turned = ps("turned", [P, C, P])

        raw_in = [sem(f"raw_in{m}") for m in range(4)]
        bias_in, bias_wide, through_done = sem("bias_in"), sem("bias_wide"), sem("through_done")
        full_done, full_turned, columns_done = sem("full_done"), sem("full_turned"), sem("columns_done")
        upper_done, lower_done, chain = sem("upper_done"), sem("lower_done"), sem("chain")

        block = ctx.enter_context(nc.Block())

        def wide(x):
            return x.rearrange("(a d) -> a d", a=1).broadcast_to([P, D])

        @block.sync
        def _(sp):
            for m in range(4):
                sp.dma_start(raw[:, m], a["w"][n][m].rearrange("(c p) f -> p c f", p=P)).then_inc(raw_in[m], 16)
                if m == 0:
                    sp.dma_start(full[:, 0, :], wide(a["b"][n][0])).then_inc(bias_in, 16)
                    sp.dma_start(full[:, 1, :], wide(a["b"][n][1])).then_inc(bias_in, 16)
                    sp.dma_start(g["bv"][:, n, :], wide(a["b"][n][2])).then_inc(bias_in, 16)
                    sp.dma_start(g["bo"][:, n, :], wide(a["b"][n][3])).then_inc(bias_in, 16)
            sp.wait_ge(bias_in, 64)

        @block.tensor
        def _(pe):
            pe.wait_ge(bias_wide, 1)
            for m in range(3):
                pe.wait_ge(raw_in[m], 16)
                for c in range(C):
                    last = nc.tensor.matmul(through[m][:], norm_bias[:, c, :], raw[:, m, c, :],
                                            start=(c == 0), stop=(c == C - 1))
                last.then_inc(through_done, 1)
            if n == 1:
                for m in range(2):
                    pe.wait_ge(full_done, m + 1)
                    if m == 1:
                        pe.wait_ge(columns_done, 1)
                    for c in range(C):
                        last = nc.tensor.transpose(turned[:, c, :], full[:, m, c * P:(c + 1) * P], g["ident"][:])
                    last.then_inc(full_turned, 1)

        @block.scalar
        def _(act):
            for m in range(4):
                act.wait_ge(raw_in[m], 16)
                for c in range(C):
                    s = 0.5 if m == 3 else g["vec"][:, n * ROWS + NS + c:n * ROWS + NS + c + 1]
                    nc.scalar.activation(g["w_hi"][:, m, c, :], raw[:, m, c, :], ACT.Copy,
                                         scale=s).then_inc(upper_done, 1)

        @block.vector
        def _(dve):
            link = chained(dve, chain)
            vec = g["vec"]
            nb = n * ROWS + NB
            nc.vector.tensor_copy(norm_bias[:], vec[:, nb:nb + C].unsqueeze(2).broadcast_to([P, C, P])).then_inc(bias_wide, 1)
            dve.wait_ge(bias_wide, 1)
            dve.wait_ge(bias_in, 64)
            for m in range(2):
                dve.wait_ge(through_done, m + 1)
                nc.vector.tensor_tensor(out=full[:, m, :], in0=through[m][:], in1=full[:, m, :],
                                        op=ALU.add).then_inc(full_done, 1)
            dve.wait_ge(through_done, 3)
            dve.wait_ge(full_done, 2)
            link(nc.vector.tensor_tensor(out=g["bv"][:, n, :], in0=through[2][:], in1=g["bv"][:, n, :], op=ALU.add))
            if n == 0:
                ident = g["ident"]
                for m, row in enumerate((g["row_q"], g["row_k"])):
                    link(nc.vector.tensor_copy(piece_b[:, 0, :], full[:, m, :]))
                    link(nc.vector.tensor_tensor(out=piece[:], in0=full[:, m, :], in1=piece_b[:, 0, :], op=ALU.subtract))
                    link(nc.vector.tensor_copy(piece_b[:, 1, :], piece[:]))
                    link(nc.vector.tensor_tensor(out=piece[:], in0=piece[:], in1=piece_b[:, 1, :], op=ALU.subtract))
                    link(nc.vector.tensor_copy(piece_b[:, 2, :], piece[:]))
                    link(nc.vector.tensor_scalar(row[:], piece_b[:, 0, :], ident[:, 0:1], None, ALU.mult))
                    for r in (1, 2):
                        link(nc.vector.scalar_tensor_tensor(out=row[:], in0=piece_b[:, r, :], scalar=ident[:, r:r + 1],
                                                            in1=row[:], op0=ALU.mult, op1=ALU.add))
                link(nc.vector.tensor_scalar(big[:], ident[:, 3:4], -BIG, None, ALU.mult))
                link(nc.vector.tensor_scalar(g["row_k"][:], g["row_k"][:], big[:, 0:1], None, ALU.add))
            else:
                for m in range(2):
                    dve.wait_ge(full_turned, m + 1)
                    nc.vector.tensor_copy(g["bqk"][:, m, :], turned[:, :, 0]).then_inc(columns_done, 1)
            for m in range(4):
                for c in range(C):
                    s = 0.5 if m == 3 else vec[:, n * ROWS + NS + c:n * ROWS + NS + c + 1]
                    dve.wait_ge(upper_done, m * C + c + 1)
                    nc.vector.scalar_tensor_tensor(out=g["w_lo"][:, m, c, :], in0=raw[:, m, c, :], scalar=s,
                                                   in1=g["w_hi"][:, m, c, :].bitcast(F32),
                                                   op0=ALU.mult, op1=ALU.subtract).then_inc(lower_done, 1)
            dve.wait_ge(lower_done, 4 * C)


def layer0(nc, a, g, mid):
    with ExitStack() as ctx:
        def sb(name, shape, dt=F32):
            return ctx.enter_context(nc.sbuf_tensor(name + "_l0", shape, dt))

        def ps(name, shape):
            return ctx.enter_context(nc.psum_tensor(name + "_l0", shape, F32))

        def sem(name):
            return ctx.enter_context(nc.semaphore(name + "_l0"))

        w_hi, w_lo, ident = g["w_hi"], g["w_lo"], g["ident"]
        x = sb("x", [P, 2, 2, D])
        stats = sb("stats", [P, 2, 6])
        moments = sb("moments", [P, 2, 2])
        rstd = sb("rstd", [P, 2])
        xT_hi = sb("xT_hi", [P, C, 2, T], F32R)
        xT_lo = sb("xT_lo", [P, C, 2, T], F32R)
        k_max = sb("k_max", [P, 2 * C])
        k_exp = sb("k_exp", [P, C, 2, T])
        kx = sb("kx", [P, 2, D])
        q_max = sb("q_max", [P, 2, H])
        q_exp = sb("q_exp", [P, 2, D])
        qT = sb("qT", [P, 2, C, T])
        v = sb("v", [P, 2, D])
        k_sum = sb("k_sum", [P, 2 * C])
        k_inv = sb("k_inv", [P, 2 * C])
        attn = sb("attn", [P, 2, C, HC, V1])
        q_sum = sb("q_sum", [P, 2, H])
        y = sb("y", [P, 2, D])
        y_stats = sb("y_stats", [P, 2, 6])
        y_moments = sb("y_moments", [P, 2, 2])
        y_rstd = sb("y_rstd", [P, 2])
        factor = sb("factor", [P, 2, 2, C])
        shift = sb("shift", [P, 2, 2, C])
        kept = sb("kept", [P, 2, 2])
        z = sb("z", [P, 2, C, T])
        z_tanh = sb("z_tanh", [P, 2, C, T])
        u_hi = sb("u_hi", [P, 2, C, T], F32R)
        u_lo = sb("u_lo", [P, 2, C, T], F32R)
        idle = sb("idle", [P, 1])
        res = sb("res", [P, 2, 2, D])

        bank_a = ps("bank_a", [P, 2, D])
        bank_b = ps("bank_b", [P, 2, D])
        bank_t = ps("bank_t", [P, 2, D])
        bank_y = ps("bank_y", [P, 2, D])

        x_in = [sem("x_in0"), sem("x_in1")]
        res_in = [sem("res_in0"), sem("res_in1")]
        stored = [sem("stored0"), sem("stored1")]
        (ones_set, stats_done, moments_done, eps_added, rstd_done, x_normed, x_turned, xhi_done, xlo_done,
         kT_done, k_maxed, k_shifted, k_exped, k_scaled, k_turned, kx_done, q_done, q_maxed, q_shifted, q_exped, q_turned,
         qT_done, v_done, v_read, kv_done, k_summed, k_inverted, attn_done, y_done, q_summed, y_read, y_stats_done,
         y_moments_done, y_eps, y_rstd_done, y_normed, y_turned, z_scaled, z_done, tanh_done, u_done, uhi_done,
         ulo_done, out_done, out_read, res_biased, columns_done) = [sem(x) for x in (
             "ones_set stats_done moments_done eps_added rstd_done x_normed x_turned xhi_done xlo_done "
             "kT_done k_maxed k_shifted k_exped k_scaled k_turned kx_done q_done q_maxed q_shifted q_exped q_turned "
             "qT_done v_done v_read kv_done k_summed k_inverted attn_done y_done q_summed y_read y_stats_done "
             "y_moments_done y_eps y_rstd_done y_normed y_turned z_scaled z_done tanh_done u_done uhi_done "
             "ulo_done out_done out_read res_biased columns_done").split()]

        x_dram, mid_dram = pairs_of(a["x"]), pairs_of(mid)
        block = ctx.enter_context(nc.Block())

        @block.sync
        def _(sp):
            def load_x(t):
                need(sp, x_turned, t.times(1, -1))
                sp.dma_start(x[:, t.par], x_dram[t.times(1)]).then_inc(x_in[t.par], 16)

            def slot(t, first, live, more):
                if more:
                    load_x(t.plus(1))
                if live:
                    need(sp, stored[t.par], 16 * (t.use() - 1))
                    sp.dma_start(res[:, t.par], x_dram[t.times(1)]).then_inc(res_in[t.par], 16)
                if not first:
                    before = t.plus(-1)
                    sp.wait_ge(out_read, before.times(2, 2))
                    sp.dma_start(mid_dram[before.times(1)], res[:, before.par]).then_inc(stored[before.par], 16)

            load_x(at(0))
            slots(sp, slot)
            for n in range(2):
                sp.wait_ge(stored[n], 16 * NP // 2)

        @block.gpsimd
        def _(pool):
            def root(t):
                need(pool, x_normed, t.times(2, 0))
                pool.wait_ge(moments_done, t.times(1, 1))
                nc.gpsimd.tensor_tensor(out=rstd[:], in0=moments[:, :, 1], in1=g["eps"][:], op=ALU.add).then_inc(eps_added, 1)
                pool.wait_ge(eps_added, t.times(1, 1))
                nc.gpsimd.tensor_tensor(out=rstd[:], in0=rstd[:], in1=g["power"][:], op=ALU.pow).then_inc(rstd_done, 1)

            def y_root(t, s):
                need(pool, y_normed, t.times(2, s - 1))
                pool.wait_ge(y_moments_done, t.times(2, s + 1))
                nc.gpsimd.tensor_tensor(out=y_rstd[:, s:s + 1], in0=y_moments[:, s, 1:2], in1=g["eps"][:, 0:1],
                                        op=ALU.add).then_inc(y_eps, 1)
                pool.wait_ge(y_eps, t.times(2, s + 1))
                nc.gpsimd.tensor_tensor(out=y_rstd[:, s:s + 1], in0=y_rstd[:, s:s + 1], in1=g["power"][:, 0:1],
                                        op=ALU.pow).then_inc(y_rstd_done, 1)

            def z_shift(t, s):
                pool.wait_ge(z_scaled, t.times(2, s + 1))
                nc.gpsimd.tensor_tensor(out=z[:, s], in0=z[:, s],
                                        in1=shift[:, t.par, s, :].unsqueeze(2).broadcast_to([P, C, T]),
                                        op=ALU.add).then_inc(z_done, 1)

            def bias_res(t):
                pool.wait_ge(res_in[t.par], 16 * t.use())
                nc.gpsimd.tensor_tensor(out=res[:, t.par], in0=res[:, t.par],
                                        in1=g["bo"][:, 0:1, :].broadcast_to([P, 2, D]),
                                        op=ALU.add).then_inc(res_biased, 1)

            def k_scale(t, h):
                pool.wait_ge(k_inverted, t.times(2, h + 1))
                nc.gpsimd.tensor_tensor(out=k_exp[:, 2 * h:2 * h + 2].rearrange("p c s t -> p (c s) t"),
                                        in0=k_exp[:, 2 * h:2 * h + 2].rearrange("p c s t -> p (c s) t"),
                                        in1=k_inv[:, 4 * h:4 * h + 4].unsqueeze(2).broadcast_to([P, 4, T]),
                                        op=ALU.mult).then_inc(k_scaled, 1)

            def slot(t, first, live, more):
                before = t.plus(-1)
                if more:
                    root(t.plus(1))
                if not first:
                    y_root(before, 0)
                if live:
                    k_scale(t, 0)
                if not first:
                    y_root(before, 1)
                if live:
                    k_scale(t, 1)
                if not first:
                    z_shift(before, 0)
                    z_shift(before, 1)
                if live:
                    bias_res(t)

            root(at(0))
            slots(pool, slot)

        @block.scalar
        def _(act):
            def k_expose(t, h):
                act.wait_ge(k_shifted, t.times(2, h + 1))
                nc.scalar.activation(k_exp[:, 2 * h:2 * h + 2], k_exp[:, 2 * h:2 * h + 2], ACT.Exp).then_inc(k_exped, 1)

            def q_expose(t, s):
                act.wait_ge(q_shifted, t.times(2, s + 1))
                nc.scalar.activation(q_exp[:, s], q_exp[:, s], ACT.Exp).then_inc(q_exped, 1)

            def tanh(t, s):
                act.wait_ge(z_done, t.times(2, s + 1))
                need(act, u_done, t.times(2, s - 1))
                nc.scalar.activation(z_tanh[:, s], z[:, s], ACT.Tanh, scale=0.5).then_inc(tanh_done, 1)

            def u_upper(t, s):
                need(act, out_done, t.times(2, s - 1))
                act.wait_ge(u_done, t.times(2, s + 1))
                nc.scalar.copy(u_hi[:, s], z[:, s]).then_inc(uhi_done, 1)

            def k_read(t):
                act.wait_ge(columns_done, t.times(1, 1))
                need(act, kv_done, t.times(2, 0))
                act.wait_ge(k_turned, t.times(1, 1))
                for s in range(2):
                    nc.scalar.activation(kx[:, s], bank_y[:, s], ACT.Copy,
                                         scale=kept[:, t.par, s:s + 1]).then_inc(kx_done, 1)

            def x_upper(t):
                act.wait_ge(x_turned, t.times(1, 1))
                nc.scalar.copy(xT_hi[:].rearrange("p c s t -> p s c t"),
                               bank_t[:].rearrange("p s (c t) -> p s c t", c=C)).then_inc(xhi_done, 1)

            def q_read(t):
                act.wait_ge(q_turned, t.times(1, 1))
                need(act, y_done, t.times(2, 0))
                nc.scalar.copy(qT[:].rearrange("p s c t -> p (s c t)"),
                               bank_a[:].rearrange("p s d -> p (s d)")).then_inc(qT_done, 1)

            def slot(t, first, live, more):
                before = t.plus(-1)
                if live:
                    k_expose(t, 0)
                    k_expose(t, 1)
                    q_expose(t, 0)
                    q_expose(t, 1)
                if not first:
                    tanh(before, 0)
                    u_upper(before, 0)
                    tanh(before, 1)
                if more:
                    x_upper(t.plus(1))
                if not first:
                    u_upper(before, 1)
                if live:
                    k_read(t)
                    q_read(t)

            x_upper(at(0))
            slots(act, slot)

        @block.tensor
        def _(pe):
            def project(out, m, s, row=None):
                for c in range(C):
                    for hi, lo in ((xT_hi, w_hi), (xT_hi, w_lo), (xT_lo, w_hi)):
                        last = nc.tensor.matmul(out, hi[:, c, s, :], lo[:, m, c, :],
                                                start=(c == 0 and lo is w_hi and hi is xT_hi),
                                                stop=(row is None and c == C - 1 and hi is xT_lo))
                if row is not None:
                    last = nc.tensor.matmul(out, g["three"][:], row[:], start=False, stop=True)
                return last

            def turn_x(t):
                pe.wait_ge(x_normed, t.times(2, 2))
                for s in range(2):
                    for c in range(C):
                        last = nc.tensor.transpose(bank_t[:, s, c * T:(c + 1) * T],
                                                   x[:, t.par, s, c * P:(c + 1) * P], ident[:])
                last.then_inc(x_turned, 1)

            def k_transposed(t, h):
                if h == 0:
                    pe.wait_ge(xhi_done, t.times(1, 1))
                    pe.wait_ge(xlo_done, t.times(1, 1))
                    need(pe, qT_done, t.times(1, 0))
                for f in (2 * h, 2 * h + 1):
                    out = bank_a[:, h, (f % 2) * 2 * T:(f % 2 + 1) * 2 * T]
                    for c in range(C):
                        for w, xs in ((w_hi, xT_hi), (w_lo, xT_hi), (w_hi, xT_lo)):
                            nc.tensor.matmul(out, w[:, 1, c, f * P:(f + 1) * P],
                                             xs[:, c].rearrange("p s t -> p (s t)"),
                                             start=(c == 0 and w is w_hi and xs is xT_hi), stop=False)
                    last = nc.tensor.matmul(out, g["row_k"][:, f * P:(f + 1) * P],
                                            g["mask_rows"][:, bass.ds(t.times(2 * T), 2 * T)],
                                            start=False, stop=True)
                last.then_inc(kT_done, 1)

            def q_rows(t, s):
                need(pe, out_read, t.times(2, -3 + s))
                project(bank_b[:, s], 0, s, g["row_q"]).then_inc(q_done, 1)

            def v_rows(t, s):
                pe.wait_ge(k_shifted, t.times(2, s + 1))
                project(bank_a[:, s], 2, s).then_inc(v_done, 1)

            def turn_k(t):
                pe.wait_ge(k_scaled, t.times(2, 2))
                need(pe, y_read, t.times(2, 0))
                for s in range(2):
                    for c in range(C):
                        last = nc.tensor.transpose(bank_y[:, s, c * P:(c + 1) * P], k_exp[:, c, s, :], ident[:])
                last.then_inc(k_turned, 1)

            def turn_q(t):
                pe.wait_ge(q_exped, t.times(2, 2))
                pe.wait_ge(v_read, t.times(2, 2))
                for s in range(2):
                    for c in range(C):
                        last = nc.tensor.transpose(bank_a[:, s, c * T:(c + 1) * T],
                                                   q_exp[:, s, c * P:(c + 1) * P], ident[:])
                last.then_inc(q_turned, 1)

            def v_times_k(t, s):
                if s == 0:
                    pe.wait_ge(kx_done, t.times(2, 2))
                    pe.wait_ge(v_read, t.times(2, 2))
                for c in range(C):
                    last = nc.tensor.matmul(bank_y[:, s, c * P:(c + 1) * P], v[:, s, c * P:(c + 1) * P],
                                            kx[:, s, c * P:(c + 1) * P], start=True, stop=True)
                last.then_inc(kv_done, 1)

            def q_times_attn(t, s):
                pe.wait_ge(attn_done, t.times(2, 2))
                if s == 0:
                    pe.wait_ge(qT_done, t.times(1, 1))
                else:
                    pe.wait_ge(y_read, t.times(2, 1))
                for c in range(C):
                    last = nc.tensor.matmul(bank_y[:, c // 2, (c % 2) * HC * V1:(c % 2 + 1) * HC * V1],
                                            qT[:, s, c, :], attn[:, s, c].rearrange("p h d -> p (h d)"),
                                            start=True, stop=True)
                last.then_inc(y_done, 1)

            def turn_y(t, s):
                pe.wait_ge(y_normed, t.times(2, s + 1))
                for c in range(C):
                    last = nc.tensor.transpose(bank_t[:, s, c * T:(c + 1) * T], y[:, s, c * P:(c + 1) * P], ident[:])
                last.then_inc(y_turned, 1)

            def out_rows(t, s, after):
                if after is not None:
                    pe.wait_ge(q_shifted, after.times(2, s + 1))
                pe.wait_ge(uhi_done, t.times(2, s + 1))
                pe.wait_ge(ulo_done, t.times(2, s + 1))
                for c in range(C):
                    for us, w in ((u_hi, w_hi), (u_hi, w_lo), (u_lo, w_hi)):
                        last = nc.tensor.matmul(bank_b[:, s], us[:, s, c, :], w[:, 3, c, :],
                                                start=(c == 0 and us is u_hi and w is w_hi),
                                                stop=(c == C - 1 and us is u_lo))
                last.then_inc(out_done, 1)

            def slot(t, first, live, more):
                before = t.plus(-1)
                if live:
                    k_transposed(t, 0)
                    k_transposed(t, 1)
                if not first:
                    q_times_attn(before, 0)
                if live:
                    q_rows(t, 0)
                if not first:
                    q_times_attn(before, 1)
                if live:
                    q_rows(t, 1)
                if not first:
                    turn_y(before, 0)
                if live:
                    v_rows(t, 0)
                    v_rows(t, 1)
                if not first:
                    turn_y(before, 1)
                if live:
                    turn_k(t)
                    turn_q(t)
                if more:
                    if not first:
                        pe.wait_ge(z_scaled, before.times(2, 2))
                    turn_x(t.plus(1))
                if not first:
                    out_rows(before, 0, t if live else None)
                    out_rows(before, 1, t if live else None)
                if live:
                    v_times_k(t, 0)
                    v_times_k(t, 1)

            turn_x(at(0))
            slots(pe, slot)

        @block.vector
        def _(dve):
            def x_stats(t):
                dve.wait_ge(x_in[t.par], 16 * t.use())
                for s in range(2):
                    nc.vector.bn_stats(stats[:, s, :], x[:, t.par, s, :]).then_inc(stats_done, 1)
                dve.wait_ge(stats_done, t.times(2, 2))
                nc.vector.memset(idle[:], 0.0)
                for s in range(2):
                    last = nc.vector.bn_aggr(moments[:, s, :], stats[:, s, :])
                last.then_inc(moments_done, 1)

            def x_norm(t):
                dve.wait_ge(rstd_done, t.times(1, 1))
                for s in range(2):
                    nc.vector.tensor_scalar(x[:, t.par, s, :], x[:, t.par, s, :], moments[:, s, 0:1], rstd[:, s:s + 1],
                                            ALU.subtract, ALU.mult).then_inc(x_normed, 1)

            def x_lower(t):
                dve.wait_ge(xhi_done, t.times(1, 1))
                nc.vector.tensor_tensor(out=xT_lo[:].rearrange("p c s t -> p s c t"),
                                        in0=bank_t[:].rearrange("p s (c t) -> p s c t", c=C),
                                        in1=xT_hi[:].bitcast(F32).rearrange("p c s t -> p s c t"),
                                        op=ALU.subtract).then_inc(xlo_done, 1)

            def k_shift(t, h):
                src = bank_a[:, h].rearrange("p (f t) -> p f t", t=T)
                dve.wait_ge(kT_done, t.times(2, h + 1))
                nc.vector.tensor_reduce(k_max[:, 4 * h:4 * h + 4], src, AX.X, ALU.max).then_inc(k_maxed, 1)
                need(dve, k_turned, t.times(1, 0))
                dve.wait_ge(k_maxed, t.times(2, h + 1))
                nc.vector.tensor_tensor(out=k_exp[:, 2 * h:2 * h + 2].rearrange("p c s t -> p (c s) t"), in0=src,
                                        in1=k_max[:, 4 * h:4 * h + 4].unsqueeze(2).broadcast_to([P, 4, T]),
                                        op=ALU.subtract).then_inc(k_shifted, 1)

            def q_shift(t, s):
                src = bank_b[:, s].rearrange("p (h d) -> p h d", h=H)
                dve.wait_ge(q_done, t.times(2, s + 1))
                nc.vector.tensor_reduce(q_max[:, s, :], src, AX.X, ALU.max).then_inc(q_maxed, 1)
                need(dve, q_turned, t.times(1, 0))
                dve.wait_ge(q_maxed, t.times(2, s + 1))
                nc.vector.tensor_tensor(out=q_exp[:, s].rearrange("p (h d) -> p h d", h=H), in0=src,
                                        in1=q_max[:, s, :].unsqueeze(2).broadcast_to([P, H, DH]),
                                        op=ALU.subtract).then_inc(q_shifted, 1)

            def v_read_out(t, s):
                need(dve, kv_done, t.times(2, s - 1))
                dve.wait_ge(v_done, t.times(2, s + 1))
                nc.vector.tensor_tensor(out=v[:, s], in0=bank_a[:, s], in1=g["bv"][:, 0, :],
                                        op=ALU.add).then_inc(v_read, 1)

            def k_sums(t, h):
                dve.wait_ge(k_exped, t.times(2, h + 1))
                nc.vector.tensor_reduce(k_sum[:, 4 * h:4 * h + 4],
                                        k_exp[:, 2 * h:2 * h + 2].rearrange("p c s t -> p (c s) t"),
                                        AX.X, ALU.add).then_inc(k_summed, 1)
                need(dve, k_scaled, t.times(2, h - 1))
                dve.wait_ge(k_summed, t.times(2, h + 1))
                nc.vector.reciprocal(k_inv[:, 4 * h:4 * h + 4], k_sum[:, 4 * h:4 * h + 4]).then_inc(k_inverted, 1)

            def attn_blocks(t, s):
                dve.wait_ge(kv_done, t.times(2, s + 1))
                need(dve, y_done, t.times(2, s - 1))
                for j in range(HC):
                    rows = slice(DH * j, DH * j + DH)
                    last = nc.vector.tensor_copy(
                        attn[rows, s, :, j, 0:DH],
                        bank_y[rows, s].rearrange("p (c h e) -> p c h e", c=C, h=HC)[:, :, j, :])
                last.then_inc(attn_done, 1)

            def y_read_out(t, s):
                src = bank_y[:, :, 0:2 * HC * V1].rearrange("p b (h d) -> p b h d", d=V1)
                dve.wait_ge(y_done, t.times(2, s + 1))
                nc.vector.reciprocal(q_sum[:, s, :].rearrange("p (b h) -> p b h", b=2),
                                     src[:, :, :, DH]).then_inc(q_summed, 1)
                need(dve, y_turned, t.times(2, s - 1))
                dve.wait_ge(q_summed, t.times(2, s + 1))
                nc.vector.tensor_tensor(
                    out=y[:, s].rearrange("p (b h d) -> p b h d", b=2, d=DH), in0=src[:, :, :, 0:DH],
                    in1=q_sum[:, s, :].rearrange("p (b h) -> p b h", b=2).unsqueeze(3).broadcast_to([P, 2, H // 2, DH]),
                    op=ALU.mult).then_inc(y_read, 1)
                dve.wait_ge(y_read, t.times(2, s + 1))
                nc.vector.bn_stats(y_stats[:, s, :], y[:, s]).then_inc(y_stats_done, 1)
                dve.wait_ge(y_stats_done, t.times(2, s + 1))
                nc.vector.memset(idle[:], 0.0)
                nc.vector.bn_aggr(y_moments[:, s, :], y_stats[:, s, :]).then_inc(y_moments_done, 1)

            def y_norm(t, s):
                dve.wait_ge(y_rstd_done, t.times(2, s + 1))
                nc.vector.tensor_scalar(y[:, s], y[:, s], y_moments[:, s, 0:1], y_rstd[:, s:s + 1],
                                        ALU.subtract, ALU.mult).then_inc(y_normed, 1)

            def z_scale(t, s):
                need(dve, ulo_done, t.times(2, s - 1))
                need(dve, uhi_done, t.times(2, s - 1))
                dve.wait_ge(y_turned, t.times(2, s + 1))
                nc.vector.tensor_tensor(out=z[:, s], in0=bank_t[:, s].rearrange("p (c t) -> p c t", c=C),
                                        in1=factor[:, t.par, s, :].unsqueeze(2).broadcast_to([P, C, T]),
                                        op=ALU.mult).then_inc(z_scaled, 1)

            def u_form(t, s):
                dve.wait_ge(tanh_done, t.times(2, s + 1))
                nc.vector.scalar_tensor_tensor(out=z[:, s], in0=z_tanh[:, s], scalar=1.0, in1=z[:, s],
                                               op0=ALU.add, op1=ALU.mult).then_inc(u_done, 1)

            def u_lower(t, s):
                need(dve, out_done, t.times(2, s - 1))
                dve.wait_ge(uhi_done, t.times(2, s + 1))
                nc.vector.tensor_tensor(out=u_lo[:, s], in0=z[:, s], in1=u_hi[:, s].bitcast(F32),
                                        op=ALU.subtract).then_inc(ulo_done, 1)

            def out_add(t, s):
                dve.wait_ge(res_biased, t.times(1, 1))
                dve.wait_ge(out_done, t.times(2, s + 1))
                nc.vector.tensor_tensor(out=res[:, t.par, s, :], in0=bank_b[:, s], in1=res[:, t.par, s, :],
                                        op=ALU.add).then_inc(out_read, 1)

            def columns(t):
                need(dve, z_done, t.times(2, -2))
                need(dve, kx_done, t.times(2, -2))
                both = bass.ds(t.times(2), 2)
                nc.vector.tensor_copy(factor[:, t.par], g["film"][:, 0, 0, both, :])
                nc.vector.tensor_copy(shift[:, t.par], g["film"][:, 0, 1, both, :])
                nc.vector.tensor_copy(kept[:, t.par], g["valid"][:, both]).then_inc(columns_done, 1)

            def slot(t, first, live, more):
                before = t.plus(-1)
                if not first:
                    attn_blocks(before, 0)
                    attn_blocks(before, 1)
                if live:
                    k_shift(t, 0)
                    columns(t)
                if more:
                    x_stats(t.plus(1))
                if live:
                    k_shift(t, 1)
                if not first:
                    y_read_out(before, 0)
                if live:
                    k_sums(t, 0)
                    q_shift(t, 0)
                if not first:
                    y_norm(before, 0)
                    y_read_out(before, 1)
                if live:
                    k_sums(t, 1)
                    q_shift(t, 1)
                if not first:
                    y_norm(before, 1)
                    z_scale(before, 0)
                if more:
                    x_norm(t.plus(1))
                if live:
                    v_read_out(t, 0)
                    v_read_out(t, 1)
                if not first:
                    z_scale(before, 1)
                if not first:
                    u_form(before, 0)
                    u_lower(before, 0)
                    u_form(before, 1)
                if more:
                    x_lower(t.plus(1))
                if not first:
                    u_lower(before, 1)
                    out_add(before, 0)
                    out_add(before, 1)

            nc.vector.memset(attn[:], 0.0).then_inc(ones_set, 1)
            dve.wait_ge(ones_set, 1)
            for j in range(HC):
                nc.vector.memset(attn[DH * j:DH * j + DH, :, :, j, DH:V1], 1.0).then_inc(ones_set, 1)
            dve.wait_ge(ones_set, 1 + HC)
            x_stats(at(0))
            x_norm(at(0))
            x_lower(at(0))
            slots(dve, slot)


def layer1(nc, a, g, mid, out):
    with ExitStack() as ctx:
        def sb(name, shape, dt=F32):
            return ctx.enter_context(nc.sbuf_tensor(name + "_l1", shape, dt))

        def ps(name, shape):
            return ctx.enter_context(nc.psum_tensor(name + "_l1", shape, F32))

        def sem(name):
            return ctx.enter_context(nc.semaphore(name + "_l1"))

        w_hi, w_lo, ident = g["w_hi"], g["w_lo"], g["ident"]
        x = sb("x", [P, 2, 2, D])
        stats = sb("stats", [P, 2, 6])
        moments = sb("moments", [P, 2, 2])
        rstd = sb("rstd", [P, 2])
        xT_hi = sb("xT_hi", [P, C, 2, T], F32R)
        xT_lo = sb("xT_lo", [P, C, 2, T], F32R)
        qT = sb("qT", [P, 2, C, 2, T], F32R)
        kT = sb("kT", [P, 2, C, 2, T], F32R)
        q_wide = sb("q_wide", [P, 2, C, 2, HC, T], F32R)
        v = sb("v", [P, 2, H, V1])
        shift_q = sb("shift_q", [P, 2 * H])
        shift_rows = sb("shift_rows", [P, P], BF16)
        pick = sb("pick", [P, 2 * H, P], BF16)
        pick_col = sb("pick_col", [P, 2 * H])
        prob = sb("prob", [P, 4, HC, T])
        y_sum = sb("y_sum", [P, 2, H])
        y = sb("y", [P, 2, D])
        y_stats = sb("y_stats", [P, 2, 6])
        y_moments = sb("y_moments", [P, 2, 2])
        y_rstd = sb("y_rstd", [P, 2])
        factor = sb("factor", [P, 2, 2, C])
        shift = sb("shift", [P, 2, 2, C])
        off = sb("off", [P, 2, 2])
        keep = sb("keep", [P, 2, 2])
        z = sb("z", [P, 2, C, T])
        z_tanh = sb("z_tanh", [P, 2, C, T])
        u_hi = sb("u_hi", [P, 2, C, T], F32R)
        u_lo = sb("u_lo", [P, 2, C, T], F32R)
        idle = sb("idle", [P, 1])
        res = sb("res", [P, 2, 2, D])

        bank_a = ps("bank_a", [P, 2, D])
        bank_b = ps("bank_b", [P, 2, D])
        bank_t = ps("bank_t", [P, 2, D])
        bank_y = ps("bank_y", [P, 2, D])
        chunk_bank = [bank_a[:, 0], bank_a[:, 1], bank_b[:, 0], bank_b[:, 1]]

        x_in = [sem("x_in0"), sem("x_in1")]
        res_in = [sem("res_in0"), sem("res_in1")]
        stored = [sem("stored0"), sem("stored1")]
        names = ("ready wide_cleared stats_done moments_done eps_added rstd_done x_normed x_turned xhi_done xlo_done "
                 "q_done qhi_done qlo_done spread_in k_done khi_done klo_done v_done v_read v_masked "
                 "rough_done max_done max_turned shift_split score_done exp_done pv_done "
                 "y_summed y_read y_stats_done y_moments_done y_eps y_rstd_done y_normed y_turned "
                 "z_scaled z_done tanh_done u_done uhi_done ulo_done out_done out_read res_biased columns_done picked")
        (ready, wide_cleared, stats_done, moments_done, eps_added, rstd_done, x_normed, x_turned, xhi_done, xlo_done,
         q_done, qhi_done, qlo_done, spread_in, k_done, khi_done, klo_done, v_done, v_read, v_masked,
         rough_done, max_done, max_turned, shift_split, score_done, exp_done, pv_done,
         y_summed, y_read, y_stats_done, y_moments_done, y_eps, y_rstd_done, y_normed, y_turned,
         z_scaled, z_done, tanh_done, u_done, uhi_done, ulo_done, out_done, out_read, res_biased,
         columns_done, picked) = [sem(n) for n in names.split()]

        mid_dram, out_dram = pairs_of(mid), pairs_of(out)
        block = ctx.enter_context(nc.Block())

        @block.sync
        def _(sp):
            def load_x(t):
                need(sp, x_turned, t.times(1, -1))
                sp.dma_start(x[:, t.par], mid_dram[t.times(1)]).then_inc(x_in[t.par], 16)

            def slot(t, first, live, more):
                if more:
                    load_x(t.plus(1))
                if live:
                    need(sp, stored[t.par], 16 * (t.use() - 1))
                    sp.dma_start(res[:, t.par], mid_dram[t.times(1)]).then_inc(res_in[t.par], 16)
                    sp.wait_ge(qlo_done, t.times(C, C))
                    for j in range(HC):
                        rows = slice(DH * j, DH * j + DH)
                        sp.dma_start(q_wide[rows, :, :, :, j, :].bitcast(F32).rearrange("p a c s t -> p (a c s) t"),
                                     qT[rows].bitcast(F32).rearrange("p a c s t -> p (a c s) t")).then_inc(spread_in, 16)
                if not first:
                    before = t.plus(-1)
                    sp.wait_ge(out_read, before.times(2, 2))
                    sp.dma_start(out_dram[before.times(1)], res[:, before.par]).then_inc(stored[before.par], 16)

            sp.wait_ge(wide_cleared, 1)
            load_x(at(0))
            slots(sp, slot)
            for n in range(2):
                sp.wait_ge(stored[n], 16 * NP // 2)

        @block.gpsimd
        def _(pool):
            def root(t):
                need(pool, x_normed, t.times(2, 0))
                pool.wait_ge(moments_done, t.times(1, 1))
                nc.gpsimd.tensor_tensor(out=rstd[:], in0=moments[:, :, 1], in1=g["eps"][:], op=ALU.add).then_inc(eps_added, 1)
                pool.wait_ge(eps_added, t.times(1, 1))
                nc.gpsimd.tensor_tensor(out=rstd[:], in0=rstd[:], in1=g["power"][:], op=ALU.pow).then_inc(rstd_done, 1)

            def y_root(t, s):
                need(pool, y_normed, t.times(2, s - 1))
                pool.wait_ge(y_moments_done, t.times(2, s + 1))
                nc.gpsimd.tensor_tensor(out=y_rstd[:, s:s + 1], in0=y_moments[:, s, 1:2], in1=g["eps"][:, 0:1],
                                        op=ALU.add).then_inc(y_eps, 1)
                pool.wait_ge(y_eps, t.times(2, s + 1))
                nc.gpsimd.tensor_tensor(out=y_rstd[:, s:s + 1], in0=y_rstd[:, s:s + 1], in1=g["power"][:, 0:1],
                                        op=ALU.pow).then_inc(y_rstd_done, 1)

            def z_shift(t, s):
                pool.wait_ge(z_scaled, t.times(2, s + 1))
                nc.gpsimd.tensor_tensor(out=z[:, s], in0=z[:, s],
                                        in1=shift[:, t.par, s, :].unsqueeze(2).broadcast_to([P, C, T]),
                                        op=ALU.add).then_inc(z_done, 1)

            def v_mask(t, s):
                pool.wait_ge(v_read, t.times(2, s + 1))
                nc.gpsimd.tensor_tensor(out=v[:, s, :, 0:DH], in0=v[:, s, :, 0:DH],
                                        in1=keep[:, t.par, s:s + 1].unsqueeze(2).broadcast_to([P, H, DH]),
                                        op=ALU.mult).then_inc(v_masked, 1)

            def bias_res(t):
                pool.wait_ge(res_in[t.par], 16 * t.use())
                nc.gpsimd.tensor_tensor(out=res[:, t.par], in0=res[:, t.par],
                                        in1=g["bo"][:, 1:2, :].broadcast_to([P, 2, D]),
                                        op=ALU.add).then_inc(res_biased, 1)

            def slot(t, first, live, more):
                before = t.plus(-1)
                if not first:
                    y_root(before, 1)
                if more:
                    root(t.plus(1))
                if not first:
                    z_shift(before, 0)
                    z_shift(before, 1)
                if live:
                    v_mask(t, 0)
                    v_mask(t, 1)
                    bias_res(t)
                    y_root(t, 0)

            nc.gpsimd.memset(q_wide[:].bitcast(F32), 0.0).then_inc(wide_cleared, 1)
            root(at(0))
            slots(pool, slot)

        @block.scalar
        def _(act):
            def upper(t, dst, banks, m, h, done, signal):
                act.wait_ge(done, t.times(2, h + 1))
                for f in (2 * h, 2 * h + 1):
                    nc.scalar.activation(dst[:, 0, f].rearrange("p s t -> p (s t)"),
                                         banks[:, f // 2, (f % 2) * 2 * T:(f % 2 + 1) * 2 * T], ACT.Identity,
                                         bias=g["bqk"][:, m, f:f + 1]).then_inc(signal, 1)

            def tanh(t, s):
                act.wait_ge(z_done, t.times(2, s + 1))
                need(act, u_done, t.times(2, s - 1))
                nc.scalar.activation(z_tanh[:, s], z[:, s], ACT.Tanh, scale=0.5).then_inc(tanh_done, 1)

            def u_upper(t, s):
                need(act, out_done, t.times(2, s - 1))
                act.wait_ge(u_done, t.times(2, s + 1))
                nc.scalar.copy(u_hi[:, s], z[:, s]).then_inc(uhi_done, 1)

            def x_upper(t):
                act.wait_ge(x_turned, t.times(1, 1))
                nc.scalar.copy(xT_hi[:].rearrange("p c s t -> p s c t"),
                               bank_t[:].rearrange("p s (c t) -> p s c t", c=C)).then_inc(xhi_done, 1)

            def expose(t, n):
                need(act, pv_done, t.times(8, n - 3))
                act.wait_ge(score_done, t.times(8, n + 1))
                nc.scalar.activation(prob[:, n % 4].rearrange("p h t -> p (h t)"), chunk_bank[n % 4], ACT.Exp,
                                     bias=off[:, t.par, n // C:n // C + 1]).then_inc(exp_done, 1)

            def slot(t, first, live, more):
                before = t.plus(-1)
                if live:
                    need(act, spread_in, t.times(64, 0))
                    upper(t, qT, bank_a, 0, 0, q_done, qhi_done)
                    upper(t, qT, bank_a, 0, 1, q_done, qhi_done)
                    need(act, score_done, t.times(8, 0))
                    upper(t, kT, bank_b, 1, 0, k_done, khi_done)
                if not first:
                    tanh(before, 0)
                    tanh(before, 1)
                if live:
                    upper(t, kT, bank_b, 1, 1, k_done, khi_done)
                if not first:
                    u_upper(before, 0)
                    u_upper(before, 1)
                if more:
                    x_upper(t.plus(1))
                if live:
                    act.wait_ge(columns_done, t.times(1, 1))
                    for n in range(2 * C):
                        expose(t, n)

            x_upper(at(0))
            slots(act, slot)

        @block.tensor
        def _(pe):
            def turn_x(t):
                pe.wait_ge(x_normed, t.times(2, 2))
                for s in range(2):
                    for c in range(C):
                        last = nc.tensor.transpose(bank_t[:, s, c * T:(c + 1) * T],
                                                   x[:, t.par, s, c * P:(c + 1) * P], ident[:])
                last.then_inc(x_turned, 1)

            def transposed(bank, m, h, signal):
                for f in (2 * h, 2 * h + 1):
                    for c in range(C):
                        for w, xs in ((w_hi, xT_hi), (w_lo, xT_hi), (w_hi, xT_lo)):
                            last = nc.tensor.matmul(bank[:, h, (f % 2) * 2 * T:(f % 2 + 1) * 2 * T],
                                                    w[:, m, c, f * P:(f + 1) * P],
                                                    xs[:, c].rearrange("p s t -> p (s t)"),
                                                    start=(c == 0 and w is w_hi and xs is xT_hi),
                                                    stop=(c == C - 1 and xs is xT_lo))
                last.then_inc(signal, 1)

            def q_transposed(t, h):
                if h == 0:
                    pe.wait_ge(xhi_done, t.times(1, 1))
                    pe.wait_ge(xlo_done, t.times(1, 1))
                need(pe, exp_done, t.times(8, h - 3))
                transposed(bank_a, 0, h, q_done)

            def k_transposed(t, h):
                need(pe, exp_done, t.times(8, h - 1))
                transposed(bank_b, 1, h, k_done)

            def v_rows(t, s):
                pe.wait_ge(qlo_done, t.times(C, 2 * s + 2))
                for c in range(C):
                    for xs, w in ((xT_hi, w_hi), (xT_hi, w_lo), (xT_lo, w_hi)):
                        last = nc.tensor.matmul(bank_a[:, s], xs[:, c, s, :], w[:, 2, c, :],
                                                start=(c == 0 and w is w_hi and xs is xT_hi),
                                                stop=(c == C - 1 and xs is xT_lo))
                last.then_inc(v_done, 1)

            def turn_y(t, s):
                pe.wait_ge(y_normed, t.times(2, 2))
                for c in range(C):
                    last = nc.tensor.transpose(bank_t[:, s, c * T:(c + 1) * T], y[:, s, c * P:(c + 1) * P], ident[:])
                last.then_inc(y_turned, 1)

            def rough(t, n):
                s, c, bank = n // C, n % C, chunk_bank[(n + 2) % 4]
                if n == 0:
                    pe.wait_ge(spread_in, t.times(64, 64))
                if n < 2:
                    pe.wait_ge(klo_done, t.times(C, 2 * n + 2))
                elif n < 4:
                    if n == 2:
                        pe.wait_ge(klo_done, t.times(C, C))
                    pe.wait_ge(v_read, t.times(2, n - 1))
                else:
                    pe.wait_ge(max_done, t.times(8, n - 3))
                nc.tensor.matmul(bank, g["three"][:],
                                 g["off_rows"][:, bass.ds(t.times(2 * T, s * T), T)].unsqueeze(1).broadcast_to([P, HC, T]),
                                 start=True, stop=False)
                for h in range(HC):
                    last = nc.tensor.matmul(bank[:, h * T:(h + 1) * T], q_wide[:, 0, c, s, h, :], kT[:, 0, c, s, :],
                                            start=False, stop=(h == HC - 1))
                last.then_inc(rough_done, 1)

            def turn_max(t):
                pe.wait_ge(max_done, t.times(8, 8))
                need(pe, y_read, t.times(2, 0))
                nc.tensor.transpose(bank_y[0:2 * H, 0, 0:P], shift_q[:], ident[:]).then_inc(max_turned, 1)

            def scores(t, n):
                s, c, bank = n // C, n % C, chunk_bank[n % 4]
                if n < 2:
                    if n == 0:
                        pe.wait_ge(shift_split, t.times(1, 1))
                elif n < 4:
                    need(pe, out_read, t.times(2, n - 3))
                else:
                    pe.wait_ge(exp_done, t.times(8, n - 3))
                for k, (ks, qs) in enumerate(((0, 0), (0, 1), (1, 0))):
                    nc.tensor.matmul(bank, kT[:, ks, c, s, :], q_wide[:, qs, c, s].rearrange("p h t -> p (h t)"),
                                     start=(k == 0), stop=False)
                for h in range(HC):
                    last = nc.tensor.matmul(bank[:, h * T:(h + 1) * T], pick[:, s * H + c * HC + h, :], shift_rows[:],
                                            start=False, stop=(h == HC - 1))
                last.then_inc(score_done, 1)

            def times_v(t, n, more=True):
                s, c = n // C, n % C
                bank = (bank_y, bank_t)[s]
                if n == 0:
                    pe.wait_ge(v_masked, t.times(2, 2))
                if n == C:
                    if more:
                        pe.wait_ge(xhi_done, t.times(1, 2))
                        pe.wait_ge(xlo_done, t.times(1, 2))
                    else:
                        pe.wait_ge(z_scaled, t.times(2, 0))
                pe.wait_ge(exp_done, t.times(8, n + 1))
                for h in range(HC):
                    k = (c % 2) * HC + h
                    last = nc.tensor.matmul(bank[:, c // 2, k * V1:(k + 1) * V1], prob[:, n % 4, h, :],
                                            v[:, s, c * HC + h, :], start=True, stop=True)
                last.then_inc(pv_done, 1)

            def out_rows(t, s, after):
                if after is not None:
                    pe.wait_ge(max_done, after.times(8, C + s + 1))
                pe.wait_ge(uhi_done, t.times(2, s + 1))
                pe.wait_ge(ulo_done, t.times(2, s + 1))
                for c in range(C):
                    for us, w in ((u_hi, w_hi), (u_hi, w_lo), (u_lo, w_hi)):
                        last = nc.tensor.matmul(bank_b[:, s], us[:, s, c, :], w[:, 3, c, :],
                                                start=(c == 0 and us is u_hi and w is w_hi),
                                                stop=(c == C - 1 and us is u_lo))
                last.then_inc(out_done, 1)

            def slot(t, first, live, more):
                before = t.plus(-1)
                if live:
                    q_transposed(t, 0)
                if not first:
                    times_v(before, 2 * C - 2)
                    times_v(before, 2 * C - 1)
                if live:
                    q_transposed(t, 1)
                    k_transposed(t, 0)
                if not first:
                    turn_y(before, 0)
                    turn_y(before, 1)
                if live:
                    k_transposed(t, 1)
                    v_rows(t, 0)
                    v_rows(t, 1)
                    for n in range(C):
                        rough(t, n)
                if more:
                    if not first:
                        pe.wait_ge(z_scaled, before.times(2, 2))
                    turn_x(t.plus(1))
                if live:
                    for n in range(C, 2 * C):
                        rough(t, n)
                if not first:
                    out_rows(before, 0, t if live else None)
                if live:
                    turn_max(t)
                if not first:
                    out_rows(before, 1, t if live else None)
                if live:
                    for n in range(2 * C):
                        scores(t, n)
                        if n >= 2:
                            times_v(t, n - 2, more)

            pe.wait_ge(ready, 2)
            turn_x(at(0))
            slots(pe, slot)

        @block.vector
        def _(dve):
            def x_stats(t):
                dve.wait_ge(x_in[t.par], 16 * t.use())
                for s in range(2):
                    nc.vector.bn_stats(stats[:, s, :], x[:, t.par, s, :]).then_inc(stats_done, 1)
                dve.wait_ge(stats_done, t.times(2, 2))
                nc.vector.memset(idle[:], 0.0)
                for s in range(2):
                    last = nc.vector.bn_aggr(moments[:, s, :], stats[:, s, :])
                last.then_inc(moments_done, 1)

            def x_norm(t):
                dve.wait_ge(rstd_done, t.times(1, 1))
                for s in range(2):
                    nc.vector.tensor_scalar(x[:, t.par, s, :], x[:, t.par, s, :], moments[:, s, 0:1], rstd[:, s:s + 1],
                                            ALU.subtract, ALU.mult).then_inc(x_normed, 1)

            def x_lower(t):
                dve.wait_ge(xhi_done, t.times(1, 1))
                nc.vector.tensor_tensor(out=xT_lo[:].rearrange("p c s t -> p s c t"),
                                        in0=bank_t[:].rearrange("p s (c t) -> p s c t", c=C),
                                        in1=xT_hi[:].bitcast(F32).rearrange("p c s t -> p s c t"),
                                        op=ALU.subtract).then_inc(xlo_done, 1)

            def lower(t, dst, banks, m, h, hi_done, signal):
                dve.wait_ge(hi_done, t.times(C, 2 * h + 2))
                for f in (2 * h, 2 * h + 1):
                    nc.vector.scalar_tensor_tensor(
                        out=dst[:, 1, f].rearrange("p s t -> p (s t)"),
                        in0=banks[:, f // 2, (f % 2) * 2 * T:(f % 2 + 1) * 2 * T], scalar=g["bqk"][:, m, f:f + 1],
                        in1=dst[:, 0, f].bitcast(F32).rearrange("p s t -> p (s t)"),
                        op0=ALU.add, op1=ALU.subtract).then_inc(signal, 1)

            def v_read_out(t, s):
                need(dve, pv_done, t.times(8, 0))
                dve.wait_ge(v_done, t.times(2, s + 1))
                nc.vector.tensor_tensor(out=v[:, s, :, 0:DH], in0=bank_a[:, s].rearrange("p (h d) -> p h d", h=H),
                                        in1=g["bv"][:, 1, :].rearrange("p (h d) -> p h d", h=H),
                                        op=ALU.add).then_inc(v_read, 1)

            def maxima(t, n):
                need(dve, max_turned, t.times(1, 0))
                dve.wait_ge(rough_done, t.times(8, n + 1))
                nc.vector.tensor_reduce(shift_q[:, n * HC:(n + 1) * HC],
                                        chunk_bank[(n + 2) % 4].rearrange("p (h t) -> p h t", h=HC),
                                        AX.X, ALU.max, negate=True).then_inc(max_done, 1)

            def split_shift(t):
                need(dve, score_done, t.times(8, 0))
                dve.wait_ge(max_turned, t.times(1, 1))
                nc.vector.tensor_copy(shift_rows[0:2 * H, :], bank_y[0:2 * H, 0, 0:P]).then_inc(picked, 1)
                dve.wait_ge(picked, t.times(1, 2))
                nc.vector.tensor_tensor(out=shift_rows[2 * H:4 * H, :], in0=bank_y[0:2 * H, 0, 0:P],
                                        in1=shift_rows[0:2 * H, :], op=ALU.subtract).then_inc(shift_split, 1)

            def y_read_out(t, s):
                src = (bank_y, bank_t)[s][:, :, 0:2 * HC * V1].rearrange("p b (h d) -> p b h d", d=V1)
                dve.wait_ge(pv_done, t.times(8, 4 * s + 4))
                nc.vector.reciprocal(y_sum[:, s, :].rearrange("p (b h) -> p b h", b=2),
                                     src[:, :, :, DH]).then_inc(y_summed, 1)
                need(dve, y_turned, t.times(2, s - 1))
                dve.wait_ge(y_summed, t.times(2, s + 1))
                nc.vector.tensor_tensor(
                    out=y[:, s].rearrange("p (b h d) -> p b h d", b=2, d=DH), in0=src[:, :, :, 0:DH],
                    in1=y_sum[:, s, :].rearrange("p (b h) -> p b h", b=2).unsqueeze(3).broadcast_to([P, 2, H // 2, DH]),
                    op=ALU.mult).then_inc(y_read, 1)
                dve.wait_ge(y_read, t.times(2, s + 1))
                nc.vector.bn_stats(y_stats[:, s, :], y[:, s]).then_inc(y_stats_done, 1)
                dve.wait_ge(y_stats_done, t.times(2, s + 1))
                nc.vector.memset(idle[:], 0.0)
                nc.vector.bn_aggr(y_moments[:, s, :], y_stats[:, s, :]).then_inc(y_moments_done, 1)

            def y_norm(t, s):
                dve.wait_ge(y_rstd_done, t.times(2, s + 1))
                nc.vector.tensor_scalar(y[:, s], y[:, s], y_moments[:, s, 0:1], y_rstd[:, s:s + 1],
                                        ALU.subtract, ALU.mult).then_inc(y_normed, 1)

            def z_scale(t, s):
                need(dve, ulo_done, t.times(2, s - 1))
                dve.wait_ge(y_turned, t.times(2, s + 1))
                nc.vector.tensor_tensor(out=z[:, s], in0=bank_t[:, s].rearrange("p (c t) -> p c t", c=C),
                                        in1=factor[:, t.par, s, :].unsqueeze(2).broadcast_to([P, C, T]),
                                        op=ALU.mult).then_inc(z_scaled, 1)

            def u_form(t, s):
                dve.wait_ge(tanh_done, t.times(2, s + 1))
                nc.vector.scalar_tensor_tensor(out=z[:, s], in0=z_tanh[:, s], scalar=1.0, in1=z[:, s],
                                               op0=ALU.add, op1=ALU.mult).then_inc(u_done, 1)

            def u_lower(t, s):
                need(dve, out_done, t.times(2, s - 1))
                dve.wait_ge(uhi_done, t.times(2, s + 1))
                nc.vector.tensor_tensor(out=u_lo[:, s], in0=z[:, s], in1=u_hi[:, s].bitcast(F32),
                                        op=ALU.subtract).then_inc(ulo_done, 1)

            def out_add(t, s):
                dve.wait_ge(res_biased, t.times(1, 1))
                dve.wait_ge(out_done, t.times(2, s + 1))
                nc.vector.tensor_tensor(out=res[:, t.par, s, :], in0=bank_b[:, s], in1=res[:, t.par, s, :],
                                        op=ALU.add).then_inc(out_read, 1)

            def columns(t):
                need(dve, z_done, t.times(2, -2))
                need(dve, exp_done, t.times(8, -8))
                both = bass.ds(t.times(2), 2)
                nc.vector.tensor_copy(factor[:, t.par], g["film"][:, 1, 0, both, :])
                nc.vector.tensor_copy(shift[:, t.par], g["film"][:, 1, 1, both, :])
                nc.vector.tensor_copy(keep[:, t.par], g["score_keep"][:, both])
                nc.vector.tensor_copy(off[:, t.par], g["score_off"][:, both]).then_inc(columns_done, 1)

            def slot(t, first, live, more):
                before = t.plus(-1)
                if not first:
                    y_read_out(before, 1)
                if more:
                    x_stats(t.plus(1))
                if live:
                    columns(t)
                if not first:
                    y_norm(before, 1)
                if live:
                    lower(t, qT, bank_a, 0, 0, qhi_done, qlo_done)
                    lower(t, qT, bank_a, 0, 1, qhi_done, qlo_done)
                if more:
                    x_norm(t.plus(1))
                if not first:
                    z_scale(before, 0)
                    z_scale(before, 1)
                if live:
                    lower(t, kT, bank_b, 1, 0, khi_done, klo_done)
                if not first:
                    u_form(before, 0)
                    u_form(before, 1)
                if live:
                    lower(t, kT, bank_b, 1, 1, khi_done, klo_done)
                if not first:
                    u_lower(before, 0)
                    u_lower(before, 1)
                if live:
                    v_read_out(t, 0)
                    v_read_out(t, 1)
                    for n in range(2 * C):
                        maxima(t, n)
                    split_shift(t)
                if more:
                    x_lower(t.plus(1))
                if not first:
                    out_add(before, 0)
                    out_add(before, 1)
                if live:
                    y_read_out(t, 0)
                    y_norm(t, 0)

            nc.vector.tensor_tensor(out=pick_col[:], in0=ident[:, 0:2 * H], in1=ident[:, 2 * H:4 * H],
                                    op=ALU.add).then_inc(picked, 1)
            nc.vector.memset(v[:], 1.0).then_inc(ready, 1)
            nc.vector.memset(shift_rows[:], 0.0)
            dve.wait_ge(picked, 1)
            nc.vector.tensor_copy(pick[:], pick_col[:].unsqueeze(2).broadcast_to([P, 2 * H, P])).then_inc(ready, 1)
            dve.wait_ge(ready, 2)
            x_stats(at(0))
            x_norm(at(0))
            x_lower(at(0))
            slots(dve, slot)


def build(nc, a, out):
    mid = nc.dram_tensor("layer0_out", [B, T, D], F32).ap()
    with ExitStack() as ctx:
        def sb(name, shape, dt=F32, c=ctx):
            return c.enter_context(nc.sbuf_tensor(name, shape, dt))

        g = {}
        g["ident"] = sb("ident", [P, P])
        g["three"] = sb("three", [P, P], BF16)
        g["w_hi"] = sb("w_hi", [P, 4, C, D], F32R)
        g["w_lo"] = sb("w_lo", [P, 4, C, D], F32R)
        g["bv"] = sb("bv", [P, 2, D])
        g["bo"] = sb("bo", [P, 2, D])
        g["vec"] = sb("vec", [P, 2 * ROWS])
        g["film"] = sb("film", [P, 2, 2, B, C])
        g["condT"] = sb("condT", [P, EC, B])
        g["eps"] = sb("eps", [P, 2])
        g["power"] = sb("power", [P, 2])
        g["row_k"] = sb("row_k", [P, D], BF16)
        g["row_q"] = sb("row_q", [P, D], BF16)
        g["bqk"] = sb("bqk", [P, 2, C])
        g["valid"] = sb("valid", [P, B])
        g["score_keep"] = sb("score_keep", [P, B])
        g["score_off"] = sb("score_off", [P, B])
        g["mask_rows"] = sb("mask_rows", [P, B * T], BF16)
        g["off_rows"] = sb("off_rows", [P, B * T], BF16)

        prepare_shared(nc, a, g)
        prepare_layer(nc, a, g, 0)
        layer0(nc, a, g, mid)
        prepare_layer(nc, a, g, 1)
        layer1(nc, a, g, mid, out)


_L0 = ["norm_scale", "norm_bias", "film_norm_scale", "film_norm_bias", "film_emb_b"]
_L1 = ["norm_w", "norm_b", "sb_norm_w", "sb_norm_b", "emb_b"]
_W0, _W1 = ["Wq", "Wk", "Wv", "film_out_W"], ["q_w", "k_w", "v_w", "out_w"]
_B0, _B1 = ["bq", "bk", "bv", "film_out_b"], ["q_b", "k_b", "v_b", "out_b"]


def kernel(**inputs):
    import numpy as _np
    import concourse.bacc as _bacc
    from concourse import mybir as _mybir
    from concourse.bass_utils import run_bass_kernel_spmd as _run

    nc = _bacc.Bacc("TRN2", target_bir_lowering=False, num_devices=1)
    arrays, ap = {}, {}
    for name in inputs:
        x = _np.ascontiguousarray(inputs[name])
        arrays[f"in_{name}_dram"] = x
        ap[name] = nc.dram_tensor(f"in_{name}_dram", x.shape, _mybir.dt.from_np(x.dtype), kind="ExternalInput").ap()
    out = nc.dram_tensor("out_0_dram", (B, T, D), _mybir.dt.float32, kind="ExternalOutput").ap()
    names = (("L0_cond_", _L0, _W0, _B0, "film_emb_W"), ("L1_cond_", _L1, _W1, _B1, "emb_w"))
    args = {
        "x": ap["x"], "cond": ap["cond_2048"], "mask0": ap["mask_BxS_ik0"], "mask1": ap["mask_BxS_ff1"],
        "vectors": [[(ap[pre + v], r) for v, r in zip(vecs, (NS, NB, FS, FB, EB))] for pre, vecs, _, _, _ in names],
        "w": [[ap[pre + w] for w in ws] for pre, _, ws, _, _ in names],
        "b": [[ap[pre + b] for b in bs] for pre, _, _, bs, _ in names],
        "emb_w": [ap[pre + e] for pre, _, _, _, e in names],
    }
    build(nc, args, out)
    r = _run(nc, [arrays], core_ids=[0])
    return r.results[0]["out_0_dram"]
```

```python
from contextlib import ExitStack

import concourse.bass as bass
from concourse import mybir

F32 = mybir.dt.float32
F32R = mybir.dt.float32r
BF16 = mybir.dt.bfloat16
I32 = mybir.dt.int32
ALU = mybir.AluOpType
ACT = mybir.ActivationFunctionType
AX = mybir.AxisListType

P = 128
B, T, D, E = 32, 128, 512, 1024
H, DH = 16, 32
C = D // P
HC = H // C
V1 = DH + 1
EC = E // P
FC = 2 * C
NP = B // 2
EPS = 1e-5
BIG = 1e30
SCORE_OFF = -1e6

NS, NB, FS, FB, EB, QB, KB = 0, 4, 8, 12, 16, 24, 28
ROWS, ALL_ROWS = 24, 56
ORDER = (1, 0, 2, 3)
FILM1 = NP - 2


class Pair:

    def __init__(self, i, j):
        self.i, self.j = i, j
        self.par = j % 2

    def plus(self, n):
        return Pair(self.i, self.j + n)

    def times(self, n, k=0):
        return self.i * (2 * n) + (self.j * n + k)

    def use(self):
        return self.i + (self.j // 2 + 1)


def at(t):
    return Pair(t // 2, t % 2)


def is_slot(t, n):
    return isinstance(t.i, int) and t.times(1) == n


def need(eng, sem, count):
    if not isinstance(count, int) or count > 0:
        eng.wait_ge(sem, count)


def slots(eng, slot):
    slot(at(0), True, True, True)
    slot(at(1), False, True, True)
    with eng.Fori(1, NP // 2 - 1) as i:
        slot(Pair(i, 0), False, True, True)
        slot(Pair(i, 1), False, True, True)
    slot(at(NP - 2), False, True, True)
    slot(at(NP - 1), False, True, False)
    slot(at(NP), False, False, False)


def pairs_of(x):
    return x.rearrange("(g s) t d -> g t s d", s=2)


def chained(eng, sem):
    count = [0]

    def link(ins):
        count[0] += 1
        ins.then_inc(sem, 1)
        eng.wait_ge(sem, count[0])

    return link


def layer0(nc, a, g, mid):
    with ExitStack() as ctx:
        def sb(name, shape, dt=F32):
            return ctx.enter_context(nc.sbuf_tensor(name + "_l0", shape, dt))

        def ps(name, shape):
            return ctx.enter_context(nc.psum_tensor(name + "_l0", shape, F32))

        def sem(name):
            return ctx.enter_context(nc.semaphore(name + "_l0"))

        w_hi, w_lo, ident = g["w_hi"], g["w_lo"], g["ident"]
        x = sb("x", [P, 2, 2, D])
        stats = sb("stats", [P, 2, 6])
        moments = sb("moments", [P, 2, 2])
        rstd = sb("rstd", [P, 2])
        xT_hi = sb("xT_hi", [P, C, 2, T], F32R)
        xT_lo = sb("xT_lo", [P, C, 2, T], F32R)
        k_max = sb("k_max", [P, 2 * C])
        k_exp = sb("k_exp", [P, C, 2, T])
        kx = sb("kx", [P, 2, D])
        q_max = sb("q_max", [P, 2, H])
        q_exp = sb("q_exp", [P, 2, D])
        qT = sb("qT", [P, 2, C, T])
        v = sb("v", [P, 2, D])
        k_sum = sb("k_sum", [P, 2 * C])
        k_inv = sb("k_inv", [P, 2 * C])
        attn = sb("attn", [P, 2, C, HC, V1])
        q_sum = sb("q_sum", [P, 2, H])
        y = sb("y", [P, 2, D])
        y_stats = sb("y_stats", [P, 2, 6])
        y_moments = sb("y_moments", [P, 2, 2])
        y_rstd = sb("y_rstd", [P, 2])
        factor = sb("factor", [P, 2, 2, C])
        shift = sb("shift", [P, 2, 2, C])
        kept = sb("kept", [P, 2, 2])
        z = sb("z", [P, 2, C, T])
        z_tanh = sb("z_tanh", [P, 2, C, T])
        u_hi = sb("u_hi", [P, 2, C, T], F32R)
        u_lo = sb("u_lo", [P, 2, C, T], F32R)
        idle = sb("idle", [P, 1])
        res = sb("res", [P, 2, 2, D])

        stage = sb("stage", [P, 4 * C * D])
        raw = stage[:].rearrange("p (m c d) -> p m c d", m=4, c=C)
        emb_w = stage[:].rearrange("p (k e) -> p k e", k=EC)
        rows = sb("rows", [ALL_ROWS, P])
        cond = z[0:B].rearrange("b s c t -> b (s c t)")
        cond_tanh = z_tanh[0:B].rearrange("b s c t -> b (s c t)")
        full = y
        norm_bias = sb("norm_bias", [P, C, P])
        piece = sb("piece", [P, D])
        piece_b = sb("piece_b", [P, D], BF16)
        keep_mask = sb("keep_mask", [B, T], I32)
        score_mask = sb("score_mask", [B, T])
        maskf = sb("maskf", [B, T])
        mask_b = sb("mask_b", [B, T], BF16)
        off = sb("off", [B, T])
        rest = sb("rest", [B, T])
        part = sb("part", [B, 3, T], BF16)
        count = sb("count", [B, 1])
        one_plus = sb("one_plus", [P, C, B])
        film_shift = sb("film_shift", [P, C, B])

        bank_a = ps("bank_a", [P, 2, D])
        bank_b = ps("bank_b", [P, 2, D])
        bank_t = ps("bank_t", [P, 2, D])
        bank_y = ps("bank_y", [P, 2, D])
        cond_t = bank_y[:, 0, EC * B:2 * EC * B].rearrange("p (k b) -> p k b", k=EC)
        emb = bank_t[:, 0, 0:FC * B].rearrange("p (f b) -> p f b", f=FC)

        x_in = [sem("x_in0"), sem("x_in1")]
        res_in = [sem("res_in0"), sem("res_in1")]
        stored = [sem("stored0"), sem("stored1")]
        (ones_set, stats_done, moments_done, eps_added, rstd_done, x_normed, x_turned, xhi_done, xlo_done,
         kT_done, k_maxed, k_shifted, k_exped, k_scaled, k_turned, kx_done, q_done, q_maxed, q_shifted, q_exped, q_turned,
         qT_done, v_done, v_read, kv_done, k_summed, k_inverted, attn_done, y_done, q_summed, y_read, y_stats_done,
         y_moments_done, y_eps, y_rstd_done, y_normed, y_turned, z_scaled, z_done, tanh_done, u_done, uhi_done,
         ulo_done, out_done, out_read, res_biased, columns_done) = [sem(x) for x in (
             "ones_set stats_done moments_done eps_added rstd_done x_normed x_turned xhi_done xlo_done "
             "kT_done k_maxed k_shifted k_exped k_scaled k_turned kx_done q_done q_maxed q_shifted q_exped q_turned "
             "qT_done v_done v_read kv_done k_summed k_inverted attn_done y_done q_summed y_read y_stats_done "
             "y_moments_done y_eps y_rstd_done y_normed y_turned z_scaled z_done tanh_done u_done uhi_done "
             "ulo_done out_done out_read res_biased columns_done").split()]

        raw_in = [sem(f"raw_in{m}") for m in range(4)]
        (norm_rows_in, rows_in, cond_in, keep_in, masks_in, qk_bias_in, v_bias_in, bo_in, emb_in, mask_row_in,
         off_rows_in, consts_done, zero_done, ident_done, select_done, row_zero, mask_ones, norm_turned, vec_ready,
         bias_wide, through_done, full_done, rounded, piece_done, row_act, row_dve, upper_done, lower_done,
         keep_cast, parts_done, silu_tanh, silu_done, setup_turned, setup_copied, bv_done, emb_done, film_done,
         film_ready, bqk_done, chain) = [sem(x) for x in (
             "norm_rows_in rows_in cond_in keep_in masks_in qk_bias_in v_bias_in bo_in emb_in mask_row_in "
             "off_rows_in consts_done zero_done ident_done select_done row_zero mask_ones norm_turned vec_ready "
             "bias_wide through_done full_done rounded piece_done row_act row_dve upper_done lower_done "
             "keep_cast parts_done silu_tanh silu_done setup_turned setup_copied bv_done emb_done film_done "
             "film_ready bqk_done chain").split()]

        x_dram, mid_dram = pairs_of(a["x"]), pairs_of(mid)

        def wide(x):
            return x.rearrange("(a d) -> a d", a=1).broadcast_to([P, D])

        def scale_of(n, m, c):
            return 0.5 if m == 3 else g["vec"][:, n * ROWS + NS + c:n * ROWS + NS + c + 1]

        block = ctx.enter_context(nc.Block())

        @block.sync
        def _(sp):
            def load_x(t):
                need(sp, x_turned, t.times(1, -1))
                sp.dma_start(x[:, t.par], x_dram[t.times(1)]).then_inc(x_in[t.par], 16)

            def slot(t, first, live, more):
                if more:
                    load_x(t.plus(1))
                if live:
                    need(sp, stored[t.par], 16 * (t.use() - 1))
                    sp.dma_start(res[:, t.par], x_dram[t.times(1)]).then_inc(res_in[t.par], 16)
                if first:
                    load_late()
                if is_slot(t, 1):
                    sp.wait_ge(emb_done, 1)
                    load_embedding(1)
                if is_slot(t, FILM1):
                    sp.wait_ge(emb_done, 2)
                    for m in range(4):
                        load_weight(1, m)
                if not live:
                    sp.wait_ge(kT_done, 2 * NP)
                    for r in range(3):
                        sp.dma_start(g["mask_rows"][32 * r:32 * r + 1, :].rearrange("a (b t) -> a b t", b=B),
                                     part[:, r, :]).then_inc(off_rows_in, 16)
                if not first:
                    before = t.plus(-1)
                    sp.wait_ge(out_read, before.times(2, 2))
                    sp.dma_start(mid_dram[before.times(1)], res[:, before.par]).then_inc(stored[before.par], 16)

            def load_weight(n, m):
                sp.dma_start(raw[:, m], a["w"][n][m].rearrange("(c p) f -> p c f", p=P)).then_inc(raw_in[m], 16)

            def load_embedding(n):
                sp.dma_start(emb_w, a["emb_w"][n].rearrange("(k p) f -> p k f", p=P)).then_inc(emb_in, 16)

            def load_row(n, v, signal):
                x, r0 = a["vectors"][n][v]
                r = x.rearrange("(c p) -> c p", p=P)
                r0 += n * ROWS
                sp.dma_start(rows[r0:r0 + r.shape[0], :], r).then_inc(signal, 16)

            def load_late():
                sp.dma_start(cond, a["cond"]).then_inc(cond_in, 16)
                sp.dma_start(score_mask[:], a["mask1"]).then_inc(masks_in, 16)
                for v in range(2, 5):
                    load_row(0, v, rows_in)
                for v in range(7):
                    load_row(1, v, rows_in)
                sp.dma_start(g["bo"][:, 0, :], wide(a["b"][0][3])).then_inc(bo_in, 16)
                sp.dma_start(g["bv"][:, 1, :], wide(a["b"][1][2])).then_inc(v_bias_in, 16)
                sp.dma_start(g["bo"][:, 1, :], wide(a["b"][1][3])).then_inc(bo_in, 16)
                sp.wait_ge(through_done, 3)
                sp.wait_ge(lower_done, 4 * C)
                load_embedding(0)

            load_row(0, 0, norm_rows_in)
            load_row(0, 1, norm_rows_in)
            load_x(at(0))
            load_weight(0, 1)
            sp.dma_start(keep_mask[:], a["mask0"]).then_inc(keep_in, 16)
            sp.dma_start(full[:, 1, :], wide(a["b"][0][1])).then_inc(qk_bias_in, 16)
            load_weight(0, 0)
            sp.dma_start(full[:, 0, :], wide(a["b"][0][0])).then_inc(qk_bias_in, 16)
            load_weight(0, 2)
            sp.dma_start(g["bv"][:, 0, :], wide(a["b"][0][2])).then_inc(v_bias_in, 16)
            load_weight(0, 3)
            sp.wait_ge(mask_ones, 1)
            sp.wait_ge(keep_cast, 1)
            sp.dma_start(g["mask_rows"][96:97, :].rearrange("a (b t) -> a b t", b=B), mask_b[:]).then_inc(mask_row_in, 16)
            slots(sp, slot)
            sp.wait_ge(off_rows_in, 48)
            for n in range(2):
                sp.wait_ge(stored[n], 16 * NP // 2)

        @block.gpsimd
        def _(pool):
            def root(t):
                need(pool, x_normed, t.times(2, 0))
                pool.wait_ge(moments_done, t.times(1, 1))
                nc.gpsimd.tensor_tensor(out=rstd[:], in0=moments[:, :, 1], in1=g["eps"][:], op=ALU.add).then_inc(eps_added, 1)
                pool.wait_ge(eps_added, t.times(1, 1))
                nc.gpsimd.tensor_tensor(out=rstd[:], in0=rstd[:], in1=g["power"][:], op=ALU.pow).then_inc(rstd_done, 1)

            def y_root(t, s):
                need(pool, y_normed, t.times(2, s - 1))
                pool.wait_ge(y_moments_done, t.times(2, s + 1))
                nc.gpsimd.tensor_tensor(out=y_rstd[:, s:s + 1], in0=y_moments[:, s, 1:2], in1=g["eps"][:, 0:1],
                                        op=ALU.add).then_inc(y_eps, 1)
                pool.wait_ge(y_eps, t.times(2, s + 1))
                nc.gpsimd.tensor_tensor(out=y_rstd[:, s:s + 1], in0=y_rstd[:, s:s + 1], in1=g["power"][:, 0:1],
                                        op=ALU.pow).then_inc(y_rstd_done, 1)

            def z_shift(t, s):
                pool.wait_ge(z_scaled, t.times(2, s + 1))
                nc.gpsimd.tensor_tensor(out=z[:, s], in0=z[:, s],
                                        in1=shift[:, t.par, s, :].unsqueeze(2).broadcast_to([P, C, T]),
                                        op=ALU.add).then_inc(z_done, 1)

            def bias_res(t):
                pool.wait_ge(res_in[t.par], 16 * t.use())
                if is_slot(t, 0):
                    pool.wait_ge(bo_in, 32)
                nc.gpsimd.tensor_tensor(out=res[:, t.par], in0=res[:, t.par],
                                        in1=g["bo"][:, 0:1, :].broadcast_to([P, 2, D]),
                                        op=ALU.add).then_inc(res_biased, 1)

            def k_scale(t, h):
                pool.wait_ge(k_inverted, t.times(2, h + 1))
                nc.gpsimd.tensor_tensor(out=k_exp[:, 2 * h:2 * h + 2].rearrange("p c s t -> p (c s) t"),
                                        in0=k_exp[:, 2 * h:2 * h + 2].rearrange("p c s t -> p (c s) t"),
                                        in1=k_inv[:, 4 * h:4 * h + 4].unsqueeze(2).broadcast_to([P, 4, T]),
                                        op=ALU.mult).then_inc(k_scaled, 1)

            def slot(t, first, live, more):
                before = t.plus(-1)
                if more:
                    root(t.plus(1))
                if not first:
                    y_root(before, 0)
                if live:
                    k_scale(t, 0)
                if not first:
                    y_root(before, 1)
                if live:
                    k_scale(t, 1)
                if not first:
                    z_shift(before, 0)
                    z_shift(before, 1)
                if live:
                    bias_res(t)

            nc.gpsimd.memset(ident[:], 0.0).then_inc(zero_done, 1)
            pool.wait_ge(zero_done, 1)
            nc.gpsimd.affine_select(out=ident[:], in_=ident[:], compare_op=ALU.not_equal, fill=1.0,
                                    base=0, pattern=[[-1, P]], channel_multiplier=1).then_inc(ident_done, 1)
            nc.gpsimd.memset(g["eps"][:], EPS).then_inc(consts_done, 1)
            nc.gpsimd.memset(g["power"][:], -0.5).then_inc(consts_done, 1)
            nc.gpsimd.memset(g["mask_rows"][:], 1.0).then_inc(mask_ones, 1)
            pool.wait_ge(consts_done, 2)
            root(at(0))
            slots(pool, slot)

        @block.scalar
        def _(act):
            def k_expose(t, h):
                act.wait_ge(k_shifted, t.times(2, h + 1))
                nc.scalar.activation(k_exp[:, 2 * h:2 * h + 2], k_exp[:, 2 * h:2 * h + 2], ACT.Exp).then_inc(k_exped, 1)

            def q_expose(t, s):
                act.wait_ge(q_shifted, t.times(2, s + 1))
                nc.scalar.activation(q_exp[:, s], q_exp[:, s], ACT.Exp).then_inc(q_exped, 1)

            def tanh(t, s):
                act.wait_ge(z_done, t.times(2, s + 1))
                need(act, u_done, t.times(2, s - 1))
                nc.scalar.activation(z_tanh[:, s], z[:, s], ACT.Tanh, scale=0.5).then_inc(tanh_done, 1)

            def u_upper(t, s):
                need(act, out_done, t.times(2, s - 1))
                act.wait_ge(u_done, t.times(2, s + 1))
                nc.scalar.copy(u_hi[:, s], z[:, s]).then_inc(uhi_done, 1)

            def k_read(t):
                act.wait_ge(columns_done, t.times(1, 1))
                need(act, kv_done, t.times(2, 0))
                act.wait_ge(k_turned, t.times(1, 1))
                for s in range(2):
                    nc.scalar.activation(kx[:, s], bank_y[:, s], ACT.Copy,
                                         scale=kept[:, t.par, s:s + 1]).then_inc(kx_done, 1)

            def x_upper(t):
                act.wait_ge(x_turned, t.times(1, 1))
                nc.scalar.copy(xT_hi[:].rearrange("p c s t -> p s c t"),
                               bank_t[:].rearrange("p s (c t) -> p s c t", c=C)).then_inc(xhi_done, 1)

            def q_read(t):
                act.wait_ge(q_turned, t.times(1, 1))
                need(act, y_done, t.times(2, 0))
                nc.scalar.copy(qT[:].rearrange("p s c t -> p (s c t)"),
                               bank_a[:].rearrange("p s d -> p (s d)")).then_inc(qT_done, 1)

            def slot(t, first, live, more):
                before = t.plus(-1)
                if live:
                    k_expose(t, 0)
                    k_expose(t, 1)
                    if first:
                        upper_weight(0, 3)
                    q_expose(t, 0)
                    q_expose(t, 1)
                else:
                    for pos in range(3):
                        upper_weight(1, pos)
                if not first:
                    tanh(before, 0)
                    u_upper(before, 0)
                    tanh(before, 1)
                if more:
                    x_upper(t.plus(1))
                if not first:
                    u_upper(before, 1)
                if live:
                    k_read(t)
                    q_read(t)
                else:
                    upper_weight(1, 3)

            def upper_weight(n, pos):
                m = ORDER[pos]
                act.wait_ge(raw_in[m], 16 * (n + 1))
                if n == 0:
                    act.wait_ge(vec_ready, 1)
                else:
                    act.wait_ge(v_done if m < 3 else out_done, 2 * NP)
                for c in range(C):
                    nc.scalar.activation(w_hi[:, m, c, :], raw[:, m, c, :], ACT.Copy,
                                         scale=scale_of(n, m, c)).then_inc(upper_done, 1)

            def bias_rows(pos):
                row, m = (g["row_k"], 1) if pos == 0 else (g["row_q"], 0)
                act.wait_ge(row_zero, 3)
                act.wait_ge(full_done, pos + 1)
                nc.scalar.copy(row[0:1, :], full[0:1, m, :]).then_inc(row_act, 1)
                act.wait_ge(piece_done, pos + 1)
                nc.scalar.copy(row[32:33, :], piece[32:33, :]).then_inc(row_act, 1)

            upper_weight(0, 0)
            x_upper(at(0))
            upper_weight(0, 1)
            bias_rows(0)
            upper_weight(0, 2)
            bias_rows(1)
            act.wait_ge(cond_in, 16)
            nc.scalar.activation(cond_tanh, cond, ACT.Tanh, scale=0.5).then_inc(silu_tanh, 1)
            slots(act, slot)

        @block.tensor
        def _(pe):
            def project(out, m, s, row=None):
                for c in range(C):
                    for hi, lo in ((xT_hi, w_hi), (xT_hi, w_lo), (xT_lo, w_hi)):
                        last = nc.tensor.matmul(out, hi[:, c, s, :], lo[:, m, c, :],
                                                start=(c == 0 and lo is w_hi and hi is xT_hi),
                                                stop=(row is None and c == C - 1 and hi is xT_lo))
                if row is not None:
                    last = nc.tensor.matmul(out, g["three"][:], row[:], start=False, stop=True)
                return last

            def turn_x(t):
                pe.wait_ge(x_normed, t.times(2, 2))
                for s in range(2):
                    for c in range(C):
                        last = nc.tensor.transpose(bank_t[:, s, c * T:(c + 1) * T],
                                                   x[:, t.par, s, c * P:(c + 1) * P], ident[:])
                last.then_inc(x_turned, 1)

            def k_transposed(t, h):
                if h == 0:
                    pe.wait_ge(xhi_done, t.times(1, 1))
                    pe.wait_ge(xlo_done, t.times(1, 1))
                    need(pe, qT_done, t.times(1, 0))
                if is_slot(t, 0) and h == 0:
                    pe.wait_ge(lower_done, C)
                for f in (2 * h, 2 * h + 1):
                    out = bank_a[:, h, (f % 2) * 2 * T:(f % 2 + 1) * 2 * T]
                    for c in range(C):
                        for w, xs in ((w_hi, xT_hi), (w_lo, xT_hi), (w_hi, xT_lo)):
                            nc.tensor.matmul(out, w[:, 1, c, f * P:(f + 1) * P],
                                             xs[:, c].rearrange("p s t -> p (s t)"),
                                             start=(c == 0 and w is w_hi and xs is xT_hi), stop=False)
                    if is_slot(t, 0) and f == 0:
                        pe.wait_ge(row_act, 2)
                        pe.wait_ge(row_dve, 1)
                        pe.wait_ge(mask_row_in, 16)
                        pe.wait_ge(select_done, 4)
                    last = nc.tensor.matmul(out, g["row_k"][:, f * P:(f + 1) * P],
                                            g["mask_rows"][:, bass.ds(t.times(2 * T), 2 * T)],
                                            start=False, stop=True)
                last.then_inc(kT_done, 1)

            def q_rows(t, s):
                need(pe, out_read, t.times(2, -3 + s))
                if is_slot(t, 0):
                    pe.wait_ge(lower_done, 2 * C)
                    pe.wait_ge(row_act, 4)
                    pe.wait_ge(row_dve, 2)
                project(bank_b[:, s], 0, s, g["row_q"]).then_inc(q_done, 1)

            def v_rows(t, s):
                pe.wait_ge(k_shifted, t.times(2, s + 1))
                if is_slot(t, 0):
                    pe.wait_ge(lower_done, 3 * C)
                project(bank_a[:, s], 2, s).then_inc(v_done, 1)

            def turn_k(t):
                pe.wait_ge(k_scaled, t.times(2, 2))
                need(pe, y_read, t.times(2, 0))
                if is_slot(t, 0):
                    pe.wait_ge(bv_done, 1)
                    pe.wait_ge(setup_copied, 1)
                for s in range(2):
                    for c in range(C):
                        last = nc.tensor.transpose(bank_y[:, s, c * P:(c + 1) * P], k_exp[:, c, s, :], ident[:])
                last.then_inc(k_turned, 1)

            def turn_q(t):
                pe.wait_ge(q_exped, t.times(2, 2))
                pe.wait_ge(v_read, t.times(2, 2))
                for s in range(2):
                    for c in range(C):
                        last = nc.tensor.transpose(bank_a[:, s, c * T:(c + 1) * T],
                                                   q_exp[:, s, c * P:(c + 1) * P], ident[:])
                last.then_inc(q_turned, 1)

            def v_times_k(t, s):
                if s == 0:
                    pe.wait_ge(kx_done, t.times(2, 2))
                    pe.wait_ge(v_read, t.times(2, 2))
                for c in range(C):
                    last = nc.tensor.matmul(bank_y[:, s, c * P:(c + 1) * P], v[:, s, c * P:(c + 1) * P],
                                            kx[:, s, c * P:(c + 1) * P], start=True, stop=True)
                last.then_inc(kv_done, 1)

            def q_times_attn(t, s):
                pe.wait_ge(attn_done, t.times(2, 2))
                if s == 0:
                    pe.wait_ge(qT_done, t.times(1, 1))
                else:
                    pe.wait_ge(y_read, t.times(2, 1))
                for c in range(C):
                    last = nc.tensor.matmul(bank_y[:, c // 2, (c % 2) * HC * V1:(c % 2 + 1) * HC * V1],
                                            qT[:, s, c, :], attn[:, s, c].rearrange("p h d -> p (h d)"),
                                            start=True, stop=True)
                last.then_inc(y_done, 1)

            def turn_y(t, s):
                for n, used in ((0, 0), (1, FILM1 - 1)):
                    if is_slot(t, used) and s == 0:
                        pe.wait_ge(film_done, n + 1)
                pe.wait_ge(y_normed, t.times(2, s + 1))
                for c in range(C):
                    last = nc.tensor.transpose(bank_t[:, s, c * T:(c + 1) * T], y[:, s, c * P:(c + 1) * P], ident[:])
                last.then_inc(y_turned, 1)

            def out_rows(t, s, after):
                if is_slot(t, 0):
                    pe.wait_ge(lower_done, 4 * C)
                if after is not None:
                    pe.wait_ge(q_shifted, after.times(2, s + 1))
                pe.wait_ge(uhi_done, t.times(2, s + 1))
                pe.wait_ge(ulo_done, t.times(2, s + 1))
                for c in range(C):
                    for us, w in ((u_hi, w_hi), (u_hi, w_lo), (u_lo, w_hi)):
                        last = nc.tensor.matmul(bank_b[:, s], us[:, s, c, :], w[:, 3, c, :],
                                                start=(c == 0 and us is u_hi and w is w_hi),
                                                stop=(c == C - 1 and us is u_lo))
                last.then_inc(out_done, 1)

            def slot(t, first, live, more):
                before = t.plus(-1)
                if live:
                    k_transposed(t, 0)
                    k_transposed(t, 1)
                if first:
                    bias_through(1, bank_b[:, 1])
                if is_slot(t, 1):
                    embed(0)
                if is_slot(t, FILM1):
                    embed(1)
                if not first:
                    q_times_attn(before, 0)
                if live:
                    q_rows(t, 0)
                else:
                    layer1_biases()
                if not first:
                    q_times_attn(before, 1)
                if live:
                    q_rows(t, 1)
                if first:
                    pe.wait_ge(full_done, 1)
                    bias_through(2, bank_y[:, 1])
                    turn_setup()
                if not first:
                    turn_y(before, 0)
                if live:
                    v_rows(t, 0)
                    v_rows(t, 1)
                if not first:
                    turn_y(before, 1)
                if live:
                    turn_k(t)
                    turn_q(t)
                if more:
                    if not first:
                        pe.wait_ge(z_scaled, before.times(2, 2))
                    turn_x(t.plus(1))
                if not first:
                    out_rows(before, 0, t if live else None)
                    out_rows(before, 1, t if live else None)
                if live:
                    v_times_k(t, 0)
                    v_times_k(t, 1)

            def bias_through(pos, out):
                m = ORDER[pos]
                pe.wait_ge(raw_in[m], 16)
                for c in range(C):
                    last = nc.tensor.matmul(out, norm_bias[:, c, :], raw[:, m, c, :], start=(c == 0), stop=(c == C - 1))
                last.then_inc(through_done, 1)

            def turn_setup():
                pe.wait_ge(rows_in, 16 * 10)
                pe.wait_ge(parts_done, 1)
                pe.wait_ge(silu_done, 1)
                nc.tensor.transpose(bank_y[:, 0, 0:ALL_ROWS], rows[:], ident[0:ALL_ROWS, 0:ALL_ROWS])
                nc.tensor.transpose(bank_y[:, 0, 64:64 + B], maskf[:], ident[0:B, 0:B])
                nc.tensor.transpose(bank_y[:, 0, 128:128 + B], off[:], ident[0:B, 0:B])
                nc.tensor.transpose(bank_y[:, 0, 192:192 + B], score_mask[:], ident[0:B, 0:B])
                for k in range(EC):
                    last = nc.tensor.transpose(cond_t[:, k, :], cond[:, k * P:(k + 1) * P], ident[0:B, 0:B])
                last.then_inc(setup_turned, 1)

            def embed(n):
                pe.wait_ge(emb_in, 16 * (n + 1))
                for f in range(FC):
                    for k in range(EC):
                        last = nc.tensor.matmul(emb[:, f, :], emb_w[:, k, f * P:(f + 1) * P], g["condT"][:, k, :],
                                                start=(k == 0), stop=(k == EC - 1))
                last.then_inc(emb_done, 1)

            def layer1_biases():
                pe.wait_ge(bias_wide, 2)
                pe.wait_ge(qT_done, NP)
                for m in range(2):
                    pe.wait_ge(raw_in[m], 32)
                    for f in range(C):
                        for c in range(C):
                            nb = ROWS + NB + c
                            last = nc.tensor.matmul(bank_a[:, 0, m * C + f:m * C + f + 1],
                                                    raw[:, m, c, f * P:(f + 1) * P], g["vec"][:, nb:nb + 1],
                                                    start=(c == 0), stop=(c == C - 1))
                last.then_inc(through_done, 1)
                pe.wait_ge(raw_in[2], 32)
                for c in range(C):
                    last = nc.tensor.matmul(bank_a[:, 1], norm_bias[:, c, :], raw[:, 2, c, :],
                                            start=(c == 0), stop=(c == C - 1))
                last.then_inc(through_done, 1)

            pe.wait_ge(ident_done, 1)
            pe.wait_ge(norm_rows_in, 32)
            nc.tensor.transpose(bank_b[:, 0, 0:FS], rows[0:FS, :], ident[0:FS, 0:FS]).then_inc(norm_turned, 1)
            turn_x(at(0))
            pe.wait_ge(bias_wide, 1)
            bias_through(0, bank_y[:, 1])
            slots(pe, slot)

        @block.vector
        def _(dve):
            def x_stats(t):
                dve.wait_ge(x_in[t.par], 16 * t.use())
                for s in range(2):
                    nc.vector.bn_stats(stats[:, s, :], x[:, t.par, s, :]).then_inc(stats_done, 1)
                dve.wait_ge(stats_done, t.times(2, 2))
                nc.vector.memset(idle[:], 0.0)
                for s in range(2):
                    last = nc.vector.bn_aggr(moments[:, s, :], stats[:, s, :])
                last.then_inc(moments_done, 1)

            def x_norm(t):
                dve.wait_ge(rstd_done, t.times(1, 1))
                for s in range(2):
                    nc.vector.tensor_scalar(x[:, t.par, s, :], x[:, t.par, s, :], moments[:, s, 0:1], rstd[:, s:s + 1],
                                            ALU.subtract, ALU.mult).then_inc(x_normed, 1)

            def x_lower(t):
                dve.wait_ge(xhi_done, t.times(1, 1))
                nc.vector.tensor_tensor(out=xT_lo[:].rearrange("p c s t -> p s c t"),
                                        in0=bank_t[:].rearrange("p s (c t) -> p s c t", c=C),
                                        in1=xT_hi[:].bitcast(F32).rearrange("p c s t -> p s c t"),
                                        op=ALU.subtract).then_inc(xlo_done, 1)

            def k_shift(t, h):
                src = bank_a[:, h].rearrange("p (f t) -> p f t", t=T)
                dve.wait_ge(kT_done, t.times(2, h + 1))
                nc.vector.tensor_reduce(k_max[:, 4 * h:4 * h + 4], src, AX.X, ALU.max).then_inc(k_maxed, 1)
                need(dve, k_turned, t.times(1, 0))
                dve.wait_ge(k_maxed, t.times(2, h + 1))
                nc.vector.tensor_tensor(out=k_exp[:, 2 * h:2 * h + 2].rearrange("p c s t -> p (c s) t"), in0=src,
                                        in1=k_max[:, 4 * h:4 * h + 4].unsqueeze(2).broadcast_to([P, 4, T]),
                                        op=ALU.subtract).then_inc(k_shifted, 1)

            def q_shift(t, s):
                src = bank_b[:, s].rearrange("p (h d) -> p h d", h=H)
                dve.wait_ge(q_done, t.times(2, s + 1))
                nc.vector.tensor_reduce(q_max[:, s, :], src, AX.X, ALU.max).then_inc(q_maxed, 1)
                need(dve, q_turned, t.times(1, 0))
                dve.wait_ge(q_maxed, t.times(2, s + 1))
                nc.vector.tensor_tensor(out=q_exp[:, s].rearrange("p (h d) -> p h d", h=H), in0=src,
                                        in1=q_max[:, s, :].unsqueeze(2).broadcast_to([P, H, DH]),
                                        op=ALU.subtract).then_inc(q_shifted, 1)

            def v_read_out(t, s):
                need(dve, kv_done, t.times(2, s - 1))
                dve.wait_ge(v_done, t.times(2, s + 1))
                nc.vector.tensor_tensor(out=v[:, s], in0=bank_a[:, s], in1=g["bv"][:, 0, :],
                                        op=ALU.add).then_inc(v_read, 1)

            def k_sums(t, h):
                dve.wait_ge(k_exped, t.times(2, h + 1))
                nc.vector.tensor_reduce(k_sum[:, 4 * h:4 * h + 4],
                                        k_exp[:, 2 * h:2 * h + 2].rearrange("p c s t -> p (c s) t"),
                                        AX.X, ALU.add).then_inc(k_summed, 1)
                need(dve, k_scaled, t.times(2, h - 1))
                dve.wait_ge(k_summed, t.times(2, h + 1))
                nc.vector.reciprocal(k_inv[:, 4 * h:4 * h + 4], k_sum[:, 4 * h:4 * h + 4]).then_inc(k_inverted, 1)

            def attn_blocks(t, s):
                dve.wait_ge(kv_done, t.times(2, s + 1))
                need(dve, y_done, t.times(2, s - 1))
                for j in range(HC):
                    rows = slice(DH * j, DH * j + DH)
                    last = nc.vector.tensor_copy(
                        attn[rows, s, :, j, 0:DH],
                        bank_y[rows, s].rearrange("p (c h e) -> p c h e", c=C, h=HC)[:, :, j, :])
                last.then_inc(attn_done, 1)

            def y_read_out(t, s):
                src = bank_y[:, :, 0:2 * HC * V1].rearrange("p b (h d) -> p b h d", d=V1)
                dve.wait_ge(y_done, t.times(2, s + 1))
                nc.vector.reciprocal(q_sum[:, s, :].rearrange("p (b h) -> p b h", b=2),
                                     src[:, :, :, DH]).then_inc(q_summed, 1)
                need(dve, y_turned, t.times(2, s - 1))
                dve.wait_ge(q_summed, t.times(2, s + 1))
                nc.vector.tensor_tensor(
                    out=y[:, s].rearrange("p (b h d) -> p b h d", b=2, d=DH), in0=src[:, :, :, 0:DH],
                    in1=q_sum[:, s, :].rearrange("p (b h) -> p b h", b=2).unsqueeze(3).broadcast_to([P, 2, H // 2, DH]),
                    op=ALU.mult).then_inc(y_read, 1)
                dve.wait_ge(y_read, t.times(2, s + 1))
                nc.vector.bn_stats(y_stats[:, s, :], y[:, s]).then_inc(y_stats_done, 1)
                dve.wait_ge(y_stats_done, t.times(2, s + 1))
                nc.vector.memset(idle[:], 0.0)
                nc.vector.bn_aggr(y_moments[:, s, :], y_stats[:, s, :]).then_inc(y_moments_done, 1)

            def y_norm(t, s):
                dve.wait_ge(y_rstd_done, t.times(2, s + 1))
                nc.vector.tensor_scalar(y[:, s], y[:, s], y_moments[:, s, 0:1], y_rstd[:, s:s + 1],
                                        ALU.subtract, ALU.mult).then_inc(y_normed, 1)

            def z_scale(t, s):
                need(dve, ulo_done, t.times(2, s - 1))
                need(dve, uhi_done, t.times(2, s - 1))
                dve.wait_ge(film_ready, t.times(2, 2))
                dve.wait_ge(y_turned, t.times(2, s + 1))
                nc.vector.tensor_tensor(out=z[:, s], in0=bank_t[:, s].rearrange("p (c t) -> p c t", c=C),
                                        in1=factor[:, t.par, s, :].unsqueeze(2).broadcast_to([P, C, T]),
                                        op=ALU.mult).then_inc(z_scaled, 1)

            def u_form(t, s):
                dve.wait_ge(tanh_done, t.times(2, s + 1))
                nc.vector.scalar_tensor_tensor(out=z[:, s], in0=z_tanh[:, s], scalar=1.0, in1=z[:, s],
                                               op0=ALU.add, op1=ALU.mult).then_inc(u_done, 1)

            def u_lower(t, s):
                need(dve, out_done, t.times(2, s - 1))
                dve.wait_ge(uhi_done, t.times(2, s + 1))
                nc.vector.tensor_tensor(out=u_lo[:, s], in0=z[:, s], in1=u_hi[:, s].bitcast(F32),
                                        op=ALU.subtract).then_inc(ulo_done, 1)

            def out_add(t, s):
                dve.wait_ge(res_biased, t.times(1, 1))
                dve.wait_ge(out_done, t.times(2, s + 1))
                nc.vector.tensor_tensor(out=res[:, t.par, s, :], in0=bank_b[:, s], in1=res[:, t.par, s, :],
                                        op=ALU.add).then_inc(out_read, 1)

            def columns(t):
                need(dve, kx_done, t.times(2, -2))
                if is_slot(t, 0):
                    dve.wait_ge(vec_ready, 5)
                nc.vector.tensor_copy(kept[:, t.par], g["valid"][:, bass.ds(t.times(2), 2)]).then_inc(columns_done, 1)

            def film_columns(t):
                need(dve, z_done, t.times(2, -2))
                both = bass.ds(t.times(2), 2)
                nc.vector.tensor_copy(factor[:, t.par], g["film"][:, 0, 0, both, :]).then_inc(film_ready, 1)
                nc.vector.tensor_copy(shift[:, t.par], g["film"][:, 0, 1, both, :]).then_inc(film_ready, 1)

            def lower_weight(n, pos):
                m = ORDER[pos]
                for c in range(C):
                    dve.wait_ge(upper_done, (4 * n + pos) * C + c + 1)
                    nc.vector.scalar_tensor_tensor(out=w_lo[:, m, c, :], in0=raw[:, m, c, :], scalar=scale_of(n, m, c),
                                                   in1=w_hi[:, m, c, :].bitcast(F32),
                                                   op0=ALU.mult, op1=ALU.subtract).then_inc(lower_done, 1)

            def bias_parts(pos):
                row, m = (g["row_k"], 1) if pos == 0 else (g["row_q"], 0)
                dve.wait_ge(qk_bias_in, 32)
                dve.wait_ge(through_done, pos + 1)
                nc.vector.tensor_tensor(out=full[:, m, :], in0=(bank_y if pos == 0 else bank_b)[:, 1],
                                        in1=full[:, m, :], op=ALU.add).then_inc(full_done, 1)
                dve.wait_ge(full_done, pos + 1)
                link(nc.vector.tensor_copy(piece_b[:], full[:, m, :]))
                if pos == 1:
                    dve.wait_ge(row_act, 2)
                nc.vector.tensor_tensor(out=piece[:], in0=full[:, m, :], in1=piece_b[:],
                                        op=ALU.subtract).then_inc(piece_done, 1)
                dve.wait_ge(piece_done, pos + 1)
                link(nc.vector.tensor_copy(piece_b[:], piece[:]))
                dve.wait_ge(row_zero, 3)
                nc.vector.tensor_tensor(out=row[64:65, :], in0=piece[64:65, :], in1=piece_b[64:65, :],
                                        op=ALU.subtract).then_inc(row_dve, 1)

            def v_bias(n, bank):
                dve.wait_ge(v_bias_in, 32)
                dve.wait_ge(through_done, 3 + 2 * n)
                nc.vector.tensor_tensor(out=g["bv"][:, n, :], in0=bank, in1=g["bv"][:, n, :],
                                        op=ALU.add).then_inc(bv_done, 1)

            def masks():
                dve.wait_ge(masks_in, 16)
                link(nc.vector.tensor_scalar(maskf[:], maskf[:], -1.0, 1.0, ALU.mult, ALU.add))
                link(nc.vector.tensor_reduce(count[:], maskf[:], AX.X, ALU.add))
                link(nc.vector.reciprocal(count[:], count[:]))
                link(nc.vector.tensor_scalar(count[:], count[:], 0.0, None, ALU.mult))
                link(nc.vector.tensor_scalar(maskf[:], maskf[:], count[:, 0:1], None, ALU.add))
                nc.vector.tensor_scalar(off[:], score_mask[:], 1.0, -SCORE_OFF, ALU.subtract, ALU.mult).then_inc(parts_done, 1)
                dve.wait_ge(silu_tanh, 1)
                nc.vector.scalar_tensor_tensor(out=cond, in0=cond_tanh, scalar=1.0, in1=cond,
                                               op0=ALU.add, op1=ALU.mult).then_inc(silu_done, 1)

            def offset_parts():
                dve.wait_ge(parts_done, 1)
                link(nc.vector.tensor_copy(rest[:], off[:]))
                for r in range(3):
                    link(nc.vector.tensor_copy(part[:, r, :], rest[:]))
                    if r < 2:
                        link(nc.vector.tensor_tensor(out=rest[:], in0=rest[:], in1=part[:, r, :], op=ALU.subtract))

            def setup_columns():
                dve.wait_ge(setup_turned, 1)
                nc.vector.tensor_copy(g["valid"][:], bank_y[:, 0, 64:64 + B]).then_inc(vec_ready, 1)
                nc.vector.tensor_copy(g["vec"][:, FS:ALL_ROWS], bank_y[:, 0, FS:ALL_ROWS]).then_inc(vec_ready, 1)
                nc.vector.tensor_copy(g["score_keep"][:], bank_y[:, 0, 192:192 + B]).then_inc(vec_ready, 1)
                nc.vector.tensor_copy(g["score_off"][:], bank_y[:, 0, 128:128 + B]).then_inc(vec_ready, 1)
                nc.vector.tensor_scalar(g["condT"][:], cond_t, 0.5, None, ALU.mult).then_inc(setup_copied, 1)

            def film(n):
                v, f = n * ROWS, g["film"]

                def col(r):
                    return g["vec"][:, v + r:v + r + C].unsqueeze(2).broadcast_to([P, C, B])

                def by_sequence(k):
                    return f[:, n, k].rearrange("p b c -> p c b")

                dve.wait_ge(emb_done, n + 1)
                link(nc.vector.tensor_tensor(out=one_plus[:], in0=emb[:, 0:C, :], in1=col(EB), op=ALU.add))
                nc.vector.tensor_tensor(out=film_shift[:], in0=emb[:, C:FC, :], in1=col(EB + C),
                                        op=ALU.add).then_inc(film_done, 1)
                dve.wait_ge(film_done, n + 1)
                link(nc.vector.tensor_scalar(one_plus[:], one_plus[:], 1.0, None, ALU.add))
                link(nc.vector.tensor_tensor(out=by_sequence(0), in0=one_plus[:], in1=col(FS), op=ALU.mult))
                link(nc.vector.tensor_tensor(out=one_plus[:], in0=one_plus[:], in1=col(FB), op=ALU.mult))
                link(nc.vector.tensor_tensor(out=by_sequence(1), in0=one_plus[:], in1=film_shift[:], op=ALU.add))

            def spread_norm_bias(n):
                nb = n * ROWS + NB
                nc.vector.tensor_copy(norm_bias[:], g["vec"][:, nb:nb + C].unsqueeze(2).broadcast_to([P, C, P])
                                      ).then_inc(bias_wide, 1)

            def first_slot(t):
                k_shift(t, 0)
                lower_weight(0, 2)
                k_shift(t, 1)
                masks()
                k_sums(t, 0)
                q_shift(t, 0)
                x_stats(t.plus(1))
                k_sums(t, 1)
                q_shift(t, 1)
                v_bias(0, bank_y[:, 1])
                setup_columns()
                columns(t)
                v_read_out(t, 0)
                x_norm(t.plus(1))
                v_read_out(t, 1)
                lower_weight(0, 3)
                offset_parts()
                x_lower(t.plus(1))

            def last_slot(before):
                attn_blocks(before, 0)
                attn_blocks(before, 1)
                spread_norm_bias(1)
                lower_weight(1, 0)
                y_read_out(before, 0)
                lower_weight(1, 1)
                y_norm(before, 0)
                y_read_out(before, 1)
                film_columns(before)
                y_norm(before, 1)
                z_scale(before, 0)
                z_scale(before, 1)
                dve.wait_ge(through_done, 4)
                nc.vector.tensor_tensor(out=g["bqk"][:].rearrange("p m c -> p (m c)"), in0=bank_a[:, 0, 0:2 * C],
                                        in1=g["vec"][:, ROWS + QB:ROWS + QB + 2 * C], op=ALU.add).then_inc(bqk_done, 1)
                v_bias(1, bank_a[:, 1])
                lower_weight(1, 2)
                u_form(before, 0)
                u_lower(before, 0)
                u_form(before, 1)
                u_lower(before, 1)
                out_add(before, 0)
                out_add(before, 1)
                lower_weight(1, 3)
                dve.wait_ge(lower_done, 8 * C)

            def slot(t, first, live, more):
                before = t.plus(-1)
                if first:
                    first_slot(t)
                    return
                if not live:
                    last_slot(before)
                    return
                attn_blocks(before, 0)
                attn_blocks(before, 1)
                k_shift(t, 0)
                columns(t)
                if more:
                    x_stats(t.plus(1))
                k_shift(t, 1)
                if is_slot(t, 1):
                    film(0)
                if is_slot(t, FILM1):
                    film(1)
                y_read_out(before, 0)
                k_sums(t, 0)
                q_shift(t, 0)
                y_norm(before, 0)
                film_columns(before)
                y_read_out(before, 1)
                k_sums(t, 1)
                q_shift(t, 1)
                y_norm(before, 1)
                z_scale(before, 0)
                if more:
                    x_norm(t.plus(1))
                v_read_out(t, 0)
                v_read_out(t, 1)
                z_scale(before, 1)
                u_form(before, 0)
                u_lower(before, 0)
                u_form(before, 1)
                if more:
                    x_lower(t.plus(1))
                u_lower(before, 1)
                out_add(before, 0)
                out_add(before, 1)

            link = chained(dve, chain)
            nc.vector.memset(attn[:], 0.0).then_inc(ones_set, 1)
            dve.wait_ge(ones_set, 1)
            for j in range(HC):
                nc.vector.memset(attn[DH * j:DH * j + DH, :, :, j, DH:V1], 1.0).then_inc(ones_set, 1)
            dve.wait_ge(ones_set, 1 + HC)
            nc.vector.memset(g["three"][:], 0.0).then_inc(row_zero, 1)
            nc.vector.memset(g["row_k"][:], 0.0).then_inc(row_zero, 1)
            nc.vector.memset(g["row_q"][:], 0.0).then_inc(row_zero, 1)
            dve.wait_ge(row_zero, 3)
            for r in range(3):
                nc.vector.memset(g["three"][32 * r:32 * r + 1, :], 1.0).then_inc(select_done, 1)
            nc.vector.memset(g["row_k"][96:97, :], -BIG).then_inc(select_done, 1)
            dve.wait_ge(norm_turned, 1)
            nc.vector.tensor_copy(g["vec"][:, 0:FS], bank_b[:, 0, 0:FS]).then_inc(vec_ready, 1)
            dve.wait_ge(vec_ready, 1)
            spread_norm_bias(0)
            x_stats(at(0))
            dve.wait_ge(keep_in, 16)
            link(nc.vector.tensor_scalar(maskf[:], keep_mask[:], 1.0, None, ALU.is_equal))
            nc.vector.tensor_copy(mask_b[:], maskf[:]).then_inc(keep_cast, 1)
            x_norm(at(0))
            lower_weight(0, 0)
            x_lower(at(0))
            bias_parts(0)
            lower_weight(0, 1)
            bias_parts(1)
            slots(dve, slot)


def layer1(nc, a, g, mid, out):
    with ExitStack() as ctx:
        def sb(name, shape, dt=F32):
            return ctx.enter_context(nc.sbuf_tensor(name + "_l1", shape, dt))

        def ps(name, shape):
            return ctx.enter_context(nc.psum_tensor(name + "_l1", shape, F32))

        def sem(name):
            return ctx.enter_context(nc.semaphore(name + "_l1"))

        w_hi, w_lo, ident = g["w_hi"], g["w_lo"], g["ident"]
        x = sb("x", [P, 2, 2, D])
        stats = sb("stats", [P, 2, 6])
        moments = sb("moments", [P, 2, 2])
        rstd = sb("rstd", [P, 2])
        xT_hi = sb("xT_hi", [P, C, 2, T], F32R)
        xT_lo = sb("xT_lo", [P, C, 2, T], F32R)
        qT = sb("qT", [P, 2, C, 2, T], F32R)
        kT = sb("kT", [P, 2, C, 2, T], F32R)
        q_wide = sb("q_wide", [P, 2, C, 2, HC, T], F32R)
        v = sb("v", [P, 2, H, V1])
        shift_q = sb("shift_q", [P, 2 * H])
        shift_rows = sb("shift_rows", [P, P], BF16)
        pick = sb("pick", [P, 2 * H, P], BF16)
        pick_col = sb("pick_col", [P, 2 * H])
        prob = sb("prob", [P, 4, HC, T])
        y_sum = sb("y_sum", [P, 2, H])
        y = sb("y", [P, 2, D])
        y_stats = sb("y_stats", [P, 2, 6])
        y_moments = sb("y_moments", [P, 2, 2])
        y_rstd = sb("y_rstd", [P, 2])
        factor = sb("factor", [P, 2, 2, C])
        shift = sb("shift", [P, 2, 2, C])
        off = sb("off", [P, 2, 2])
        keep = sb("keep", [P, 2, 2])
        z = sb("z", [P, 2, C, T])
        z_tanh = sb("z_tanh", [P, 2, C, T])
        u_hi = sb("u_hi", [P, 2, C, T], F32R)
        u_lo = sb("u_lo", [P, 2, C, T], F32R)
        idle = sb("idle", [P, 1])
        res = sb("res", [P, 2, 2, D])

        bank_a = ps("bank_a", [P, 2, D])
        bank_b = ps("bank_b", [P, 2, D])
        bank_t = ps("bank_t", [P, 2, D])
        bank_y = ps("bank_y", [P, 2, D])
        chunk_bank = [bank_a[:, 0], bank_a[:, 1], bank_b[:, 0], bank_b[:, 1]]

        x_in = [sem("x_in0"), sem("x_in1")]
        res_in = [sem("res_in0"), sem("res_in1")]
        stored = [sem("stored0"), sem("stored1")]
        names = ("ready wide_cleared stats_done moments_done eps_added rstd_done x_normed x_turned xhi_done xlo_done "
                 "q_done qhi_done qlo_done spread_in k_done khi_done klo_done v_done v_read v_masked "
                 "rough_done max_done max_turned shift_split score_done exp_done pv_done "
                 "y_summed y_read y_stats_done y_moments_done y_eps y_rstd_done y_normed y_turned "
                 "z_scaled z_done tanh_done u_done uhi_done ulo_done out_done out_read res_biased columns_done picked")
        (ready, wide_cleared, stats_done, moments_done, eps_added, rstd_done, x_normed, x_turned, xhi_done, xlo_done,
         q_done, qhi_done, qlo_done, spread_in, k_done, khi_done, klo_done, v_done, v_read, v_masked,
         rough_done, max_done, max_turned, shift_split, score_done, exp_done, pv_done,
         y_summed, y_read, y_stats_done, y_moments_done, y_eps, y_rstd_done, y_normed, y_turned,
         z_scaled, z_done, tanh_done, u_done, uhi_done, ulo_done, out_done, out_read, res_biased,
         columns_done, picked) = [sem(n) for n in names.split()]

        mid_dram, out_dram = pairs_of(mid), pairs_of(out)
        block = ctx.enter_context(nc.Block())

        @block.sync
        def _(sp):
            def load_x(t):
                need(sp, x_turned, t.times(1, -1))
                sp.dma_start(x[:, t.par], mid_dram[t.times(1)]).then_inc(x_in[t.par], 16)

            def slot(t, first, live, more):
                if more:
                    load_x(t.plus(1))
                if live:
                    need(sp, stored[t.par], 16 * (t.use() - 1))
                    sp.dma_start(res[:, t.par], mid_dram[t.times(1)]).then_inc(res_in[t.par], 16)
                    if first:
                        sp.wait_ge(wide_cleared, 1)
                    sp.wait_ge(qlo_done, t.times(C, C))
                    for j in range(HC):
                        rows = slice(DH * j, DH * j + DH)
                        sp.dma_start(q_wide[rows, :, :, :, j, :].bitcast(F32).rearrange("p a c s t -> p (a c s) t"),
                                     qT[rows].bitcast(F32).rearrange("p a c s t -> p (a c s) t")).then_inc(spread_in, 16)
                if not first:
                    before = t.plus(-1)
                    sp.wait_ge(out_read, before.times(2, 2))
                    sp.dma_start(out_dram[before.times(1)], res[:, before.par]).then_inc(stored[before.par], 16)

            load_x(at(0))
            slots(sp, slot)
            for n in range(2):
                sp.wait_ge(stored[n], 16 * NP // 2)

        @block.gpsimd
        def _(pool):
            def root(t):
                need(pool, x_normed, t.times(2, 0))
                pool.wait_ge(moments_done, t.times(1, 1))
                nc.gpsimd.tensor_tensor(out=rstd[:], in0=moments[:, :, 1], in1=g["eps"][:], op=ALU.add).then_inc(eps_added, 1)
                pool.wait_ge(eps_added, t.times(1, 1))
                nc.gpsimd.tensor_tensor(out=rstd[:], in0=rstd[:], in1=g["power"][:], op=ALU.pow).then_inc(rstd_done, 1)

            def y_root(t, s):
                need(pool, y_normed, t.times(2, s - 1))
                pool.wait_ge(y_moments_done, t.times(2, s + 1))
                nc.gpsimd.tensor_tensor(out=y_rstd[:, s:s + 1], in0=y_moments[:, s, 1:2], in1=g["eps"][:, 0:1],
                                        op=ALU.add).then_inc(y_eps, 1)
                pool.wait_ge(y_eps, t.times(2, s + 1))
                nc.gpsimd.tensor_tensor(out=y_rstd[:, s:s + 1], in0=y_rstd[:, s:s + 1], in1=g["power"][:, 0:1],
                                        op=ALU.pow).then_inc(y_rstd_done, 1)

            def z_shift(t, s):
                pool.wait_ge(z_scaled, t.times(2, s + 1))
                nc.gpsimd.tensor_tensor(out=z[:, s], in0=z[:, s],
                                        in1=shift[:, t.par, s, :].unsqueeze(2).broadcast_to([P, C, T]),
                                        op=ALU.add).then_inc(z_done, 1)

            def v_mask(t, s):
                pool.wait_ge(v_read, t.times(2, s + 1))
                nc.gpsimd.tensor_tensor(out=v[:, s, :, 0:DH], in0=v[:, s, :, 0:DH],
                                        in1=keep[:, t.par, s:s + 1].unsqueeze(2).broadcast_to([P, H, DH]),
                                        op=ALU.mult).then_inc(v_masked, 1)

            def bias_res(t):
                pool.wait_ge(res_in[t.par], 16 * t.use())
                nc.gpsimd.tensor_tensor(out=res[:, t.par], in0=res[:, t.par],
                                        in1=g["bo"][:, 1:2, :].broadcast_to([P, 2, D]),
                                        op=ALU.add).then_inc(res_biased, 1)

            def slot(t, first, live, more):
                before = t.plus(-1)
                if not first:
                    y_root(before, 1)
                if more:
                    root(t.plus(1))
                if not first:
                    z_shift(before, 0)
                    z_shift(before, 1)
                if live:
                    v_mask(t, 0)
                    v_mask(t, 1)
                    bias_res(t)
                    y_root(t, 0)

            root(at(0))
            nc.gpsimd.memset(q_wide[:].bitcast(F32), 0.0).then_inc(wide_cleared, 1)
            slots(pool, slot)

        @block.scalar
        def _(act):
            def upper(t, dst, banks, m, h, done, signal):
                act.wait_ge(done, t.times(2, h + 1))
                for f in (2 * h, 2 * h + 1):
                    nc.scalar.activation(dst[:, 0, f].rearrange("p s t -> p (s t)"),
                                         banks[:, f // 2, (f % 2) * 2 * T:(f % 2 + 1) * 2 * T], ACT.Identity,
                                         bias=g["bqk"][:, m, f:f + 1]).then_inc(signal, 1)

            def tanh(t, s):
                act.wait_ge(z_done, t.times(2, s + 1))
                need(act, u_done, t.times(2, s - 1))
                nc.scalar.activation(z_tanh[:, s], z[:, s], ACT.Tanh, scale=0.5).then_inc(tanh_done, 1)

            def u_upper(t, s):
                need(act, out_done, t.times(2, s - 1))
                act.wait_ge(u_done, t.times(2, s + 1))
                nc.scalar.copy(u_hi[:, s], z[:, s]).then_inc(uhi_done, 1)

            def x_upper(t):
                act.wait_ge(x_turned, t.times(1, 1))
                nc.scalar.copy(xT_hi[:].rearrange("p c s t -> p s c t"),
                               bank_t[:].rearrange("p s (c t) -> p s c t", c=C)).then_inc(xhi_done, 1)

            def expose(t, n):
                need(act, pv_done, t.times(8, n - 3))
                act.wait_ge(score_done, t.times(8, n + 1))
                nc.scalar.activation(prob[:, n % 4].rearrange("p h t -> p (h t)"), chunk_bank[n % 4], ACT.Exp,
                                     bias=off[:, t.par, n // C:n // C + 1]).then_inc(exp_done, 1)

            def slot(t, first, live, more):
                before = t.plus(-1)
                if live:
                    need(act, spread_in, t.times(64, 0))
                    upper(t, qT, bank_a, 0, 0, q_done, qhi_done)
                    upper(t, qT, bank_a, 0, 1, q_done, qhi_done)
                    need(act, score_done, t.times(8, 0))
                    upper(t, kT, bank_b, 1, 0, k_done, khi_done)
                if not first:
                    tanh(before, 0)
                    tanh(before, 1)
                if live:
                    upper(t, kT, bank_b, 1, 1, k_done, khi_done)
                if not first:
                    u_upper(before, 0)
                    u_upper(before, 1)
                if more:
                    x_upper(t.plus(1))
                if live:
                    act.wait_ge(columns_done, t.times(1, 1))
                    for n in range(2 * C):
                        expose(t, n)

            x_upper(at(0))
            slots(act, slot)

        @block.tensor
        def _(pe):
            def turn_x(t):
                pe.wait_ge(x_normed, t.times(2, 2))
                for s in range(2):
                    for c in range(C):
                        last = nc.tensor.transpose(bank_t[:, s, c * T:(c + 1) * T],
                                                   x[:, t.par, s, c * P:(c + 1) * P], ident[:])
                last.then_inc(x_turned, 1)

            def transposed(bank, m, h, signal):
                for f in (2 * h, 2 * h + 1):
                    for c in range(C):
                        for w, xs in ((w_hi, xT_hi), (w_lo, xT_hi), (w_hi, xT_lo)):
                            last = nc.tensor.matmul(bank[:, h, (f % 2) * 2 * T:(f % 2 + 1) * 2 * T],
                                                    w[:, m, c, f * P:(f + 1) * P],
                                                    xs[:, c].rearrange("p s t -> p (s t)"),
                                                    start=(c == 0 and w is w_hi and xs is xT_hi),
                                                    stop=(c == C - 1 and xs is xT_lo))
                last.then_inc(signal, 1)

            def q_transposed(t, h):
                if h == 0:
                    pe.wait_ge(xhi_done, t.times(1, 1))
                    pe.wait_ge(xlo_done, t.times(1, 1))
                need(pe, exp_done, t.times(8, h - 3))
                transposed(bank_a, 0, h, q_done)

            def k_transposed(t, h):
                need(pe, exp_done, t.times(8, h - 1))
                transposed(bank_b, 1, h, k_done)

            def v_rows(t, s):
                pe.wait_ge(qlo_done, t.times(C, 2 * s + 2))
                for c in range(C):
                    for xs, w in ((xT_hi, w_hi), (xT_hi, w_lo), (xT_lo, w_hi)):
                        last = nc.tensor.matmul(bank_a[:, s], xs[:, c, s, :], w[:, 2, c, :],
                                                start=(c == 0 and w is w_hi and xs is xT_hi),
                                                stop=(c == C - 1 and xs is xT_lo))
                last.then_inc(v_done, 1)

            def turn_y(t, s):
                pe.wait_ge(y_normed, t.times(2, 2))
                for c in range(C):
                    last = nc.tensor.transpose(bank_t[:, s, c * T:(c + 1) * T], y[:, s, c * P:(c + 1) * P], ident[:])
                last.then_inc(y_turned, 1)

            def rough(t, n):
                s, c, bank = n // C, n % C, chunk_bank[(n + 2) % 4]
                if n == 0:
                    pe.wait_ge(spread_in, t.times(64, 64))
                if n < 2:
                    pe.wait_ge(klo_done, t.times(C, 2 * n + 2))
                elif n < 4:
                    if n == 2:
                        pe.wait_ge(klo_done, t.times(C, C))
                    pe.wait_ge(v_read, t.times(2, n - 1))
                else:
                    pe.wait_ge(max_done, t.times(8, n - 3))
                nc.tensor.matmul(bank, g["three"][:],
                                 g["mask_rows"][:, bass.ds(t.times(2 * T, s * T), T)].unsqueeze(1).broadcast_to([P, HC, T]),
                                 start=True, stop=False)
                for h in range(HC):
                    last = nc.tensor.matmul(bank[:, h * T:(h + 1) * T], q_wide[:, 0, c, s, h, :], kT[:, 0, c, s, :],
                                            start=False, stop=(h == HC - 1))
                last.then_inc(rough_done, 1)

            def turn_max(t):
                pe.wait_ge(max_done, t.times(8, 8))
                need(pe, y_read, t.times(2, 0))
                nc.tensor.transpose(bank_y[0:2 * H, 0, 0:P], shift_q[:], ident[:]).then_inc(max_turned, 1)

            def scores(t, n):
                s, c, bank = n // C, n % C, chunk_bank[n % 4]
                if n < 2:
                    if n == 0:
                        pe.wait_ge(shift_split, t.times(1, 1))
                elif n < 4:
                    need(pe, out_read, t.times(2, n - 3))
                else:
                    pe.wait_ge(exp_done, t.times(8, n - 3))
                for k, (ks, qs) in enumerate(((0, 0), (0, 1), (1, 0))):
                    nc.tensor.matmul(bank, kT[:, ks, c, s, :], q_wide[:, qs, c, s].rearrange("p h t -> p (h t)"),
                                     start=(k == 0), stop=False)
                for h in range(HC):
                    last = nc.tensor.matmul(bank[:, h * T:(h + 1) * T], pick[:, s * H + c * HC + h, :], shift_rows[:],
                                            start=False, stop=(h == HC - 1))
                last.then_inc(score_done, 1)

            def times_v(t, n, more=True):
                s, c = n // C, n % C
                bank = (bank_y, bank_t)[s]
                if n == 0:
                    pe.wait_ge(v_masked, t.times(2, 2))
                if n == C:
                    if more:
                        pe.wait_ge(xhi_done, t.times(1, 2))
                        pe.wait_ge(xlo_done, t.times(1, 2))
                    else:
                        pe.wait_ge(z_scaled, t.times(2, 0))
                pe.wait_ge(exp_done, t.times(8, n + 1))
                for h in range(HC):
                    k = (c % 2) * HC + h
                    last = nc.tensor.matmul(bank[:, c // 2, k * V1:(k + 1) * V1], prob[:, n % 4, h, :],
                                            v[:, s, c * HC + h, :], start=True, stop=True)
                last.then_inc(pv_done, 1)

            def out_rows(t, s, after):
                if after is not None:
                    pe.wait_ge(max_done, after.times(8, C + s + 1))
                pe.wait_ge(uhi_done, t.times(2, s + 1))
                pe.wait_ge(ulo_done, t.times(2, s + 1))
                for c in range(C):
                    for us, w in ((u_hi, w_hi), (u_hi, w_lo), (u_lo, w_hi)):
                        last = nc.tensor.matmul(bank_b[:, s], us[:, s, c, :], w[:, 3, c, :],
                                                start=(c == 0 and us is u_hi and w is w_hi),
                                                stop=(c == C - 1 and us is u_lo))
                last.then_inc(out_done, 1)

            def slot(t, first, live, more):
                before = t.plus(-1)
                if live:
                    q_transposed(t, 0)
                if not first:
                    times_v(before, 2 * C - 2)
                    times_v(before, 2 * C - 1)
                if live:
                    q_transposed(t, 1)
                    k_transposed(t, 0)
                if not first:
                    turn_y(before, 0)
                    turn_y(before, 1)
                if live:
                    k_transposed(t, 1)
                    v_rows(t, 0)
                    v_rows(t, 1)
                    for n in range(C):
                        rough(t, n)
                if more:
                    if not first:
                        pe.wait_ge(z_scaled, before.times(2, 2))
                    turn_x(t.plus(1))
                if live:
                    for n in range(C, 2 * C):
                        rough(t, n)
                if not first:
                    out_rows(before, 0, t if live else None)
                if live:
                    turn_max(t)
                if not first:
                    out_rows(before, 1, t if live else None)
                if live:
                    for n in range(2 * C):
                        scores(t, n)
                        if n >= 2:
                            times_v(t, n - 2, more)

            pe.wait_ge(ready, 2)
            turn_x(at(0))
            slots(pe, slot)

        @block.vector
        def _(dve):
            def x_stats(t):
                dve.wait_ge(x_in[t.par], 16 * t.use())
                for s in range(2):
                    nc.vector.bn_stats(stats[:, s, :], x[:, t.par, s, :]).then_inc(stats_done, 1)
                dve.wait_ge(stats_done, t.times(2, 2))
                nc.vector.memset(idle[:], 0.0)
                for s in range(2):
                    last = nc.vector.bn_aggr(moments[:, s, :], stats[:, s, :])
                last.then_inc(moments_done, 1)

            def x_norm(t):
                dve.wait_ge(rstd_done, t.times(1, 1))
                for s in range(2):
                    nc.vector.tensor_scalar(x[:, t.par, s, :], x[:, t.par, s, :], moments[:, s, 0:1], rstd[:, s:s + 1],
                                            ALU.subtract, ALU.mult).then_inc(x_normed, 1)

            def x_lower(t):
                dve.wait_ge(xhi_done, t.times(1, 1))
                nc.vector.tensor_tensor(out=xT_lo[:].rearrange("p c s t -> p s c t"),
                                        in0=bank_t[:].rearrange("p s (c t) -> p s c t", c=C),
                                        in1=xT_hi[:].bitcast(F32).rearrange("p c s t -> p s c t"),
                                        op=ALU.subtract).then_inc(xlo_done, 1)

            def lower(t, dst, banks, m, h, hi_done, signal):
                dve.wait_ge(hi_done, t.times(C, 2 * h + 2))
                for f in (2 * h, 2 * h + 1):
                    nc.vector.scalar_tensor_tensor(
                        out=dst[:, 1, f].rearrange("p s t -> p (s t)"),
                        in0=banks[:, f // 2, (f % 2) * 2 * T:(f % 2 + 1) * 2 * T], scalar=g["bqk"][:, m, f:f + 1],
                        in1=dst[:, 0, f].bitcast(F32).rearrange("p s t -> p (s t)"),
                        op0=ALU.add, op1=ALU.subtract).then_inc(signal, 1)

            def v_read_out(t, s):
                need(dve, pv_done, t.times(8, 0))
                dve.wait_ge(v_done, t.times(2, s + 1))
                nc.vector.tensor_tensor(out=v[:, s, :, 0:DH], in0=bank_a[:, s].rearrange("p (h d) -> p h d", h=H),
                                        in1=g["bv"][:, 1, :].rearrange("p (h d) -> p h d", h=H),
                                        op=ALU.add).then_inc(v_read, 1)

            def maxima(t, n):
                need(dve, max_turned, t.times(1, 0))
                dve.wait_ge(rough_done, t.times(8, n + 1))
                nc.vector.tensor_reduce(shift_q[:, n * HC:(n + 1) * HC],
                                        chunk_bank[(n + 2) % 4].rearrange("p (h t) -> p h t", h=HC),
                                        AX.X, ALU.max, negate=True).then_inc(max_done, 1)

            def split_shift(t):
                need(dve, score_done, t.times(8, 0))
                dve.wait_ge(max_turned, t.times(1, 1))
                nc.vector.tensor_copy(shift_rows[0:2 * H, :], bank_y[0:2 * H, 0, 0:P]).then_inc(picked, 1)
                dve.wait_ge(picked, t.times(1, 2))
                nc.vector.tensor_tensor(out=shift_rows[2 * H:4 * H, :], in0=bank_y[0:2 * H, 0, 0:P],
                                        in1=shift_rows[0:2 * H, :], op=ALU.subtract).then_inc(shift_split, 1)

            def y_read_out(t, s):
                src = (bank_y, bank_t)[s][:, :, 0:2 * HC * V1].rearrange("p b (h d) -> p b h d", d=V1)
                dve.wait_ge(pv_done, t.times(8, 4 * s + 4))
                nc.vector.reciprocal(y_sum[:, s, :].rearrange("p (b h) -> p b h", b=2),
                                     src[:, :, :, DH]).then_inc(y_summed, 1)
                need(dve, y_turned, t.times(2, s - 1))
                dve.wait_ge(y_summed, t.times(2, s + 1))
                nc.vector.tensor_tensor(
                    out=y[:, s].rearrange("p (b h d) -> p b h d", b=2, d=DH), in0=src[:, :, :, 0:DH],
                    in1=y_sum[:, s, :].rearrange("p (b h) -> p b h", b=2).unsqueeze(3).broadcast_to([P, 2, H // 2, DH]),
                    op=ALU.mult).then_inc(y_read, 1)
                dve.wait_ge(y_read, t.times(2, s + 1))
                nc.vector.bn_stats(y_stats[:, s, :], y[:, s]).then_inc(y_stats_done, 1)
                dve.wait_ge(y_stats_done, t.times(2, s + 1))
                nc.vector.memset(idle[:], 0.0)
                nc.vector.bn_aggr(y_moments[:, s, :], y_stats[:, s, :]).then_inc(y_moments_done, 1)

            def y_norm(t, s):
                dve.wait_ge(y_rstd_done, t.times(2, s + 1))
                nc.vector.tensor_scalar(y[:, s], y[:, s], y_moments[:, s, 0:1], y_rstd[:, s:s + 1],
                                        ALU.subtract, ALU.mult).then_inc(y_normed, 1)

            def z_scale(t, s):
                need(dve, ulo_done, t.times(2, s - 1))
                dve.wait_ge(y_turned, t.times(2, s + 1))
                nc.vector.tensor_tensor(out=z[:, s], in0=bank_t[:, s].rearrange("p (c t) -> p c t", c=C),
                                        in1=factor[:, t.par, s, :].unsqueeze(2).broadcast_to([P, C, T]),
                                        op=ALU.mult).then_inc(z_scaled, 1)

            def u_form(t, s):
                dve.wait_ge(tanh_done, t.times(2, s + 1))
                nc.vector.scalar_tensor_tensor(out=z[:, s], in0=z_tanh[:, s], scalar=1.0, in1=z[:, s],
                                               op0=ALU.add, op1=ALU.mult).then_inc(u_done, 1)

            def u_lower(t, s):
                need(dve, out_done, t.times(2, s - 1))
                dve.wait_ge(uhi_done, t.times(2, s + 1))
                nc.vector.tensor_tensor(out=u_lo[:, s], in0=z[:, s], in1=u_hi[:, s].bitcast(F32),
                                        op=ALU.subtract).then_inc(ulo_done, 1)

            def out_add(t, s):
                dve.wait_ge(res_biased, t.times(1, 1))
                dve.wait_ge(out_done, t.times(2, s + 1))
                nc.vector.tensor_tensor(out=res[:, t.par, s, :], in0=bank_b[:, s], in1=res[:, t.par, s, :],
                                        op=ALU.add).then_inc(out_read, 1)

            def columns(t):
                need(dve, z_done, t.times(2, -2))
                need(dve, exp_done, t.times(8, -8))
                both = bass.ds(t.times(2), 2)
                nc.vector.tensor_copy(factor[:, t.par], g["film"][:, 1, 0, both, :])
                nc.vector.tensor_copy(shift[:, t.par], g["film"][:, 1, 1, both, :])
                nc.vector.tensor_copy(keep[:, t.par], g["score_keep"][:, both])
                nc.vector.tensor_copy(off[:, t.par], g["score_off"][:, both]).then_inc(columns_done, 1)

            def slot(t, first, live, more):
                before = t.plus(-1)
                if not first:
                    y_read_out(before, 1)
                if more:
                    x_stats(t.plus(1))
                if live:
                    columns(t)
                if not first:
                    y_norm(before, 1)
                if live:
                    lower(t, qT, bank_a, 0, 0, qhi_done, qlo_done)
                    lower(t, qT, bank_a, 0, 1, qhi_done, qlo_done)
                if more:
                    x_norm(t.plus(1))
                if not first:
                    z_scale(before, 0)
                    z_scale(before, 1)
                if live:
                    lower(t, kT, bank_b, 1, 0, khi_done, klo_done)
                if not first:
                    u_form(before, 0)
                    u_form(before, 1)
                if live:
                    lower(t, kT, bank_b, 1, 1, khi_done, klo_done)
                if not first:
                    u_lower(before, 0)
                    u_lower(before, 1)
                if live:
                    v_read_out(t, 0)
                    v_read_out(t, 1)
                    for n in range(2 * C):
                        maxima(t, n)
                    split_shift(t)
                if more:
                    x_lower(t.plus(1))
                if not first:
                    out_add(before, 0)
                    out_add(before, 1)
                if live:
                    y_read_out(t, 0)
                    y_norm(t, 0)

            nc.vector.tensor_tensor(out=pick_col[:], in0=ident[:, 0:2 * H], in1=ident[:, 2 * H:4 * H],
                                    op=ALU.add).then_inc(picked, 1)
            nc.vector.memset(v[:], 1.0).then_inc(ready, 1)
            nc.vector.memset(shift_rows[:], 0.0)
            dve.wait_ge(picked, 1)
            nc.vector.tensor_copy(pick[:], pick_col[:].unsqueeze(2).broadcast_to([P, 2 * H, P])).then_inc(ready, 1)
            dve.wait_ge(ready, 2)
            x_stats(at(0))
            x_norm(at(0))
            x_lower(at(0))
            slots(dve, slot)


def build(nc, a, out):
    mid = nc.dram_tensor("layer0_out", [B, T, D], F32).ap()
    with ExitStack() as ctx:
        def sb(name, shape, dt=F32, c=ctx):
            return c.enter_context(nc.sbuf_tensor(name, shape, dt))

        g = {}
        g["ident"] = sb("ident", [P, P])
        g["three"] = sb("three", [P, P], BF16)
        g["w_hi"] = sb("w_hi", [P, 4, C, D], F32R)
        g["w_lo"] = sb("w_lo", [P, 4, C, D], F32R)
        g["bv"] = sb("bv", [P, 2, D])
        g["bo"] = sb("bo", [P, 2, D])
        g["vec"] = sb("vec", [P, ALL_ROWS])
        g["film"] = sb("film", [P, 2, 2, B, C])
        g["condT"] = sb("condT", [P, EC, B])
        g["eps"] = sb("eps", [P, 2])
        g["power"] = sb("power", [P, 2])
        g["row_k"] = sb("row_k", [P, D], BF16)
        g["row_q"] = sb("row_q", [P, D], BF16)
        g["bqk"] = sb("bqk", [P, 2, C])
        g["valid"] = sb("valid", [P, B])
        g["score_keep"] = sb("score_keep", [P, B])
        g["score_off"] = sb("score_off", [P, B])
        g["mask_rows"] = sb("mask_rows", [P, B * T], BF16)

        layer0(nc, a, g, mid)
        layer1(nc, a, g, mid, out)


_L0 = ["norm_scale", "norm_bias", "film_norm_scale", "film_norm_bias", "film_emb_b"]
_L1 = ["norm_w", "norm_b", "sb_norm_w", "sb_norm_b", "emb_b", "q_b", "k_b"]
_W0, _W1 = ["Wq", "Wk", "Wv", "film_out_W"], ["q_w", "k_w", "v_w", "out_w"]
_B0, _B1 = ["bq", "bk", "bv", "film_out_b"], ["q_b", "k_b", "v_b", "out_b"]


def kernel(**inputs):
    import numpy as _np
    import concourse.bacc as _bacc
    from concourse import mybir as _mybir
    from concourse.bass_utils import run_bass_kernel_spmd as _run

    nc = _bacc.Bacc("TRN2", target_bir_lowering=False, num_devices=1)
    arrays, ap = {}, {}
    for name in inputs:
        x = _np.ascontiguousarray(inputs[name])
        arrays[f"in_{name}_dram"] = x
        ap[name] = nc.dram_tensor(f"in_{name}_dram", x.shape, _mybir.dt.from_np(x.dtype), kind="ExternalInput").ap()
    out = nc.dram_tensor("out_0_dram", (B, T, D), _mybir.dt.float32, kind="ExternalOutput").ap()
    names = (("L0_cond_", _L0, _W0, _B0, "film_emb_W"), ("L1_cond_", _L1, _W1, _B1, "emb_w"))
    args = {
        "x": ap["x"], "cond": ap["cond_2048"], "mask0": ap["mask_BxS_ik0"], "mask1": ap["mask_BxS_ff1"],
        "vectors": [[(ap[pre + v], r) for v, r in zip(vecs, (NS, NB, FS, FB, EB, QB, KB))] for pre, vecs, _, _, _ in names],
        "w": [[ap[pre + w] for w in ws] for pre, _, ws, _, _ in names],
        "b": [[ap[pre + b] for b in bs] for pre, _, _, bs, _ in names],
        "emb_w": [ap[pre + e] for pre, _, _, _, e in names],
    }
    build(nc, args, out)
    r = _run(nc, [arrays], core_ids=[0])
    return r.results[0]["out_0_dram"]
```

```python
from contextlib import ExitStack

import concourse.bass as bass
from concourse import mybir

F32 = mybir.dt.float32
F32R = mybir.dt.float32r
BF16 = mybir.dt.bfloat16
I32 = mybir.dt.int32
ALU = mybir.AluOpType
ACT = mybir.ActivationFunctionType
AX = mybir.AxisListType

P = 128
B, T, D, E = 32, 128, 512, 1024
H, DH = 16, 32
C = D // P
HC = H // C
V1 = DH + 1
EC = E // P
FC = 2 * C
NP = B // 2
EPS = 1e-5
BIG = 1e30
SCORE_OFF = -1e6

NS, NB, FS, FB, EB, QB, KB = 0, 4, 8, 12, 16, 24, 28
ROWS, ALL_ROWS = 24, 56
ORDER = (1, 0, 2, 3)
FILM1 = NP - 2


class Pair:

    def __init__(self, i, j):
        self.i, self.j = i, j
        self.par = j % 2

    def plus(self, n):
        return Pair(self.i, self.j + n)

    def times(self, n, k=0):
        return self.i * (2 * n) + (self.j * n + k)

    def use(self):
        return self.i + (self.j // 2 + 1)


def at(t):
    return Pair(t // 2, t % 2)


def is_slot(t, n):
    return isinstance(t.i, int) and t.times(1) == n


def need(eng, sem, count):
    if not isinstance(count, int) or count > 0:
        eng.wait_ge(sem, count)


def slots(eng, slot, more_last=False):
    slot(at(0), True, True, True)
    slot(at(1), False, True, True)
    with eng.Fori(1, NP // 2 - 1) as i:
        slot(Pair(i, 0), False, True, True)
        slot(Pair(i, 1), False, True, True)
    slot(at(NP - 2), False, True, True)
    slot(at(NP - 1), False, True, more_last)
    slot(at(NP), False, False, False)


def pairs_of(x):
    return x.rearrange("(g s) t d -> g t s d", s=2)


def chained(eng, sem):
    count = [0]

    def link(ins):
        count[0] += 1
        ins.then_inc(sem, 1)
        eng.wait_ge(sem, count[0])

    return link


def layer0(nc, a, g, mid):
    with ExitStack() as ctx:
        def sb(name, shape, dt=F32):
            return ctx.enter_context(nc.sbuf_tensor(name + "_l0", shape, dt))

        def ps(name, shape):
            return ctx.enter_context(nc.psum_tensor(name + "_l0", shape, F32))

        def sem(name):
            return ctx.enter_context(nc.semaphore(name + "_l0"))

        w_hi, w_lo, ident = g["w_hi"], g["w_lo"], g["ident"]
        x, stats, moments, rstd, xT_hi, xT_lo = (g[k] for k in ("x", "stats", "moments", "rstd", "xT_hi", "xT_lo"))
        k_max = sb("k_max", [P, 2 * C])
        k_exp = sb("k_exp", [P, C, 2, T])
        kx = sb("kx", [P, 2, D])
        q_max = sb("q_max", [P, 2, H])
        q_exp = sb("q_exp", [P, 2, D])
        qT = sb("qT", [P, 2, C, T])
        v = sb("v", [P, 2, D])
        k_sum = sb("k_sum", [P, 2 * C])
        k_inv = sb("k_inv", [P, 2 * C])
        attn = sb("attn", [P, 2, C, HC, V1])
        q_sum = sb("q_sum", [P, 2, H])
        y = sb("y", [P, 2, D])
        y_stats = sb("y_stats", [P, 2, 6])
        y_moments = sb("y_moments", [P, 2, 2])
        y_rstd = sb("y_rstd", [P, 2])
        factor = sb("factor", [P, 2, 2, C])
        shift = sb("shift", [P, 2, 2, C])
        kept = sb("kept", [P, 2, 2])
        z = sb("z", [P, 2, C, T])
        z_tanh = sb("z_tanh", [P, 2, C, T])
        u_hi = sb("u_hi", [P, 2, C, T], F32R)
        u_lo = sb("u_lo", [P, 2, C, T], F32R)
        idle = sb("idle", [P, 1])
        res = g["res"]

        stage = sb("stage", [P, 4 * C * D])
        raw = stage[:].rearrange("p (m c d) -> p m c d", m=4, c=C)
        emb_w = stage[:].rearrange("p (k e) -> p k e", k=EC)
        rows = sb("rows", [ALL_ROWS, P])
        cond = z[0:B].rearrange("b s c t -> b (s c t)")
        cond_tanh = z_tanh[0:B].rearrange("b s c t -> b (s c t)")
        full = y
        row_k = sb("row_k", [P, D], BF16)
        row_q = sb("row_q", [P, D], BF16)
        condT = sb("condT", [P, EC, B])
        norm_bias = sb("norm_bias", [P, C, P])
        piece = sb("piece", [P, D])
        piece_b = sb("piece_b", [P, D], BF16)
        keep_mask = sb("keep_mask", [B, T], I32)
        score_mask = sb("score_mask", [B, T])
        maskf = sb("maskf", [B, T])
        mask_b = sb("mask_b", [B, T], BF16)
        off = sb("off", [B, T])
        rest = sb("rest", [B, T])
        part = sb("part", [B, 3, T], BF16)
        count = sb("count", [B, 1])
        emb_rows = sb("emb_rows", [4 * B, D])
        emb = sb("emb", [P, FC, B])
        one_plus = sb("one_plus", [P, C, B])
        film_shift = sb("film_shift", [P, C, B])

        bank_a = ps("bank_a", [P, 2, D])
        bank_b = ps("bank_b", [P, 2, D])
        bank_t = ps("bank_t", [P, 2, D])
        bank_y = ps("bank_y", [P, 2, D])
        cond_t = bank_y[:, 0, EC * B:2 * EC * B].rearrange("p (k b) -> p k b", k=EC)

        res_in = [sem("res_in0"), sem("res_in1")]
        stored = g["mid_stored"]
        x_in = g["x_in"]
        (stats_done, moments_done, eps_added, rstd_done, x_normed, x_turned, xhi_done, xlo_done) = g["x_chain"]
        (ones_set, kT_done, k_maxed, k_shifted, k_exped, k_scaled, k_turned, kx_done,
         q_done, q_maxed, q_shifted, q_exped, q_turned,
         qT_done, v_done, v_read, kv_done, k_summed, k_inverted, attn_done, y_done, q_summed, y_read, y_stats_done,
         y_moments_done, y_eps, y_rstd_done, y_normed, y_turned, z_scaled, z_done, tanh_done, u_done, uhi_done,
         ulo_done, out_done, out_read, res_biased, columns_done) = [sem(x) for x in (
             "ones_set kT_done k_maxed k_shifted k_exped k_scaled k_turned kx_done q_done q_maxed q_shifted q_exped q_turned "
             "qT_done v_done v_read kv_done k_summed k_inverted attn_done y_done q_summed y_read y_stats_done "
             "y_moments_done y_eps y_rstd_done y_normed y_turned z_scaled z_done tanh_done u_done uhi_done "
             "ulo_done out_done out_read res_biased columns_done").split()]

        raw_in = [sem(f"raw_in{m}") for m in range(4)]
        (norm_rows_in, rows_in, cond_in, keep_in, masks_in, qk_bias_in, v_bias_in, bo_in, emb_in, mask_row_in,
         off_rows_in, consts_done, zero_done, ident_done, select_done, row_zero, mask_ones, norm_turned, vec_ready,
         bias_wide, through_done, full_done, piece_done, row_act, row_dve, upper_done, lower_done,
         out_lower_done, keep_cast, parts_done, silu_tanh, silu_done, setup_turned, setup_copied, bv_done,
         emb_done, emb_copied, emb_turned, emb_moved, film_done,
         film_ready, bqk_turned, bqk_done, chain) = [sem(x) for x in (
             "norm_rows_in rows_in cond_in keep_in masks_in qk_bias_in v_bias_in bo_in emb_in mask_row_in "
             "off_rows_in consts_done zero_done ident_done select_done row_zero mask_ones norm_turned vec_ready "
             "bias_wide through_done full_done piece_done row_act row_dve upper_done lower_done "
             "out_lower_done keep_cast parts_done silu_tanh silu_done setup_turned setup_copied bv_done "
             "emb_done emb_copied emb_turned emb_moved film_done "
             "film_ready bqk_turned bqk_done chain").split()]

        x_dram, mid_dram = pairs_of(a["x"]), pairs_of(mid)

        def wide(x):
            return x.rearrange("(a d) -> a d", a=1).broadcast_to([P, D])

        def scale_of(n, m, c):
            return 1.0 if m == 3 else g["vec"][:, n * ROWS + NS + c:n * ROWS + NS + c + 1]

        block = ctx.enter_context(nc.Block())

        @block.sync
        def _(sp):
            def load_x(t):
                need(sp, x_turned, t.times(1, -1))
                src = mid_dram[0] if is_slot(t, NP) else x_dram[t.times(1)]
                sp.dma_start(x[:, t.par], src).then_inc(x_in[t.par], 16)

            def slot(t, first, live, more):
                if live and not is_slot(t, NP - 1):
                    load_x(t.plus(2))
                if live:
                    need(sp, stored[t.par], 16 * (t.use() - 1))
                    sp.dma_start(res[:, t.par], x_dram[t.times(1)]).then_inc(res_in[t.par], 16)
                if first:
                    load_late()
                if is_slot(t, 1):
                    sp.wait_ge(emb_done, 1)
                    for m in range(4):
                        load_embedding(1, m)
                if is_slot(t, FILM1):
                    sp.wait_ge(emb_done, 2)
                    for m in range(4):
                        load_weight(1, m)
                if not live:
                    sp.wait_ge(kT_done, 2 * NP)
                    for r in range(3):
                        sp.dma_start(g["mask_rows"][32 * r:32 * r + 1, :].rearrange("a (b t) -> a b t", b=B),
                                     part[:, r, :]).then_inc(off_rows_in, 16)
                if not first:
                    before = t.plus(-1)
                    sp.wait_ge(out_read, before.times(2, 2))
                    sp.dma_start(mid_dram[before.times(1)], res[:, before.par]).then_inc(stored[before.par], 16)

            def load_weight(n, m):
                sp.dma_start(raw[:, m], a["w"][n][m].rearrange("(c p) f -> p c f", p=P)).then_inc(raw_in[m], 16)

            def load_embedding(n, m):
                src = a["emb_w"][n].rearrange("(k p) f -> p k f", p=P)
                sp.dma_start(emb_w[:, 2 * m:2 * m + 2], src[:, 2 * m:2 * m + 2]).then_inc(emb_in, 16)

            def load_row(n, v, signal):
                x, r0 = a["vectors"][n][v]
                r = x.rearrange("(c p) -> c p", p=P)
                r0 += n * ROWS
                sp.dma_start(rows[r0:r0 + r.shape[0], :], r).then_inc(signal, 16)

            def load_late():
                sp.dma_start(cond, a["cond"]).then_inc(cond_in, 16)
                sp.dma_start(score_mask[:], a["mask1"]).then_inc(masks_in, 16)
                for v in range(2, 5):
                    load_row(0, v, rows_in)
                for v in range(7):
                    load_row(1, v, rows_in)
                sp.dma_start(g["bo"][:, 0, :], wide(a["b"][0][3])).then_inc(bo_in, 16)
                sp.dma_start(g["bv"][:, 1, :], wide(a["b"][1][2])).then_inc(v_bias_in, 16)
                sp.dma_start(g["bo"][:, 1, :], wide(a["b"][1][3])).then_inc(bo_in, 16)
                for pos in range(4):
                    sp.wait_ge(through_done, min(pos + 1, 3))
                    if pos < 3:
                        sp.wait_ge(lower_done, (pos + 1) * C)
                    else:
                        sp.wait_ge(out_lower_done, C)
                    load_embedding(0, ORDER[pos])

            load_x(at(0))
            load_row(0, 0, norm_rows_in)
            load_row(0, 1, norm_rows_in)
            load_weight(0, 1)
            sp.dma_start(keep_mask[:], a["mask0"]).then_inc(keep_in, 16)
            sp.dma_start(full[:, 1, :], wide(a["b"][0][1])).then_inc(qk_bias_in, 16)
            load_weight(0, 0)
            sp.dma_start(full[:, 0, :], wide(a["b"][0][0])).then_inc(qk_bias_in, 16)
            load_weight(0, 2)
            sp.dma_start(g["bv"][:, 0, :], wide(a["b"][0][2])).then_inc(v_bias_in, 16)
            load_weight(0, 3)
            load_x(at(1))
            sp.wait_ge(mask_ones, 1)
            sp.wait_ge(keep_cast, 1)
            sp.dma_start(g["mask_rows"][96:97, :].rearrange("a (b t) -> a b t", b=B), mask_b[:]).then_inc(mask_row_in, 16)
            slots(sp, slot, more_last=True)
            sp.wait_ge(off_rows_in, 48)

        @block.gpsimd
        def _(pool):
            def root(t):
                need(pool, x_normed, t.times(2, 0))
                pool.wait_ge(moments_done, t.times(1, 1))
                nc.gpsimd.tensor_tensor(out=rstd[:], in0=moments[:, :, 1], in1=g["eps"][:], op=ALU.add).then_inc(eps_added, 1)
                pool.wait_ge(eps_added, t.times(1, 1))
                nc.gpsimd.tensor_tensor(out=rstd[:], in0=rstd[:], in1=g["power"][:], op=ALU.pow).then_inc(rstd_done, 1)

            def y_root(t, s):
                need(pool, y_normed, t.times(2, s - 1))
                pool.wait_ge(y_moments_done, t.times(2, s + 1))
                nc.gpsimd.tensor_tensor(out=y_rstd[:, s:s + 1], in0=y_moments[:, s, 1:2], in1=g["eps"][:, 0:1],
                                        op=ALU.add).then_inc(y_eps, 1)
                pool.wait_ge(y_eps, t.times(2, s + 1))
                nc.gpsimd.tensor_tensor(out=y_rstd[:, s:s + 1], in0=y_rstd[:, s:s + 1], in1=g["power"][:, 0:1],
                                        op=ALU.pow).then_inc(y_rstd_done, 1)

            def z_shift(t, s):
                pool.wait_ge(z_scaled, t.times(2, s + 1))
                nc.gpsimd.tensor_tensor(out=z[:, s], in0=z[:, s],
                                        in1=shift[:, t.par, s, :].unsqueeze(2).broadcast_to([P, C, T]),
                                        op=ALU.add).then_inc(z_done, 1)

            def bias_res(t):
                pool.wait_ge(res_in[t.par], 16 * t.use())
                if is_slot(t, 0):
                    pool.wait_ge(bo_in, 32)
                nc.gpsimd.tensor_tensor(out=res[:, t.par], in0=res[:, t.par],
                                        in1=g["bo"][:, 0:1, :].broadcast_to([P, 2, D]),
                                        op=ALU.add).then_inc(res_biased, 1)

            def k_scale(t, h):
                pool.wait_ge(k_inverted, t.times(2, h + 1))
                nc.gpsimd.tensor_tensor(out=k_exp[:, 2 * h:2 * h + 2].rearrange("p c s t -> p (c s) t"),
                                        in0=k_exp[:, 2 * h:2 * h + 2].rearrange("p c s t -> p (c s) t"),
                                        in1=k_inv[:, 4 * h:4 * h + 4].unsqueeze(2).broadcast_to([P, 4, T]),
                                        op=ALU.mult).then_inc(k_scaled, 1)

            def slot(t, first, live, more):
                before = t.plus(-1)
                if more and not first:
                    root(t.plus(1))
                if not first:
                    y_root(before, 0)
                if live:
                    k_scale(t, 0)
                if not first:
                    y_root(before, 1)
                if live:
                    k_scale(t, 1)
                if first:
                    root(t.plus(1))
                if not first:
                    z_shift(before, 0)
                    z_shift(before, 1)
                if live:
                    bias_res(t)

            def lower_out_weight(n, chunks):
                for c in chunks:
                    pool.wait_ge(upper_done, (4 * n + 3) * C + c + 1)
                    nc.gpsimd.tensor_tensor(out=w_lo[:, 3, c, :], in0=raw[:, 3, c, :],
                                            in1=w_hi[:, 3, c, :].bitcast(F32), op=ALU.subtract).then_inc(out_lower_done, 1)

            nc.gpsimd.memset(ident[:], 0.0).then_inc(zero_done, 1)
            pool.wait_ge(zero_done, 1)
            nc.gpsimd.affine_select(out=ident[:], in_=ident[:], compare_op=ALU.not_equal, fill=1.0,
                                    base=0, pattern=[[-1, P]], channel_multiplier=1).then_inc(ident_done, 1)
            nc.gpsimd.memset(g["eps"][:], EPS).then_inc(consts_done, 1)
            nc.gpsimd.memset(g["power"][:], -0.5).then_inc(consts_done, 1)
            nc.gpsimd.memset(g["mask_rows"][:], 1.0).then_inc(mask_ones, 1)
            pool.wait_ge(consts_done, 2)
            root(at(0))
            lower_out_weight(0, range(C))
            slots(pool, slot, more_last=True)
            lower_out_weight(1, range(C // 2))
            pool.wait_ge(out_lower_done, 2 * C - C // 2)

        @block.scalar
        def _(act):
            def k_expose(t, h):
                act.wait_ge(k_shifted, t.times(2, h + 1))
                nc.scalar.activation(k_exp[:, 2 * h:2 * h + 2], k_exp[:, 2 * h:2 * h + 2], ACT.Exp).then_inc(k_exped, 1)

            def q_expose(t, s):
                act.wait_ge(q_shifted, t.times(2, s + 1))
                nc.scalar.activation(q_exp[:, s], q_exp[:, s], ACT.Exp).then_inc(q_exped, 1)

            def tanh(t, s):
                act.wait_ge(z_done, t.times(2, s + 1))
                need(act, u_done, t.times(2, s - 1))
                nc.scalar.activation(z_tanh[:, s], z[:, s], ACT.Tanh).then_inc(tanh_done, 1)

            def u_upper(t, s):
                need(act, out_done, t.times(2, s - 1))
                act.wait_ge(u_done, t.times(2, s + 1))
                nc.scalar.copy(u_hi[:, s], z[:, s]).then_inc(uhi_done, 1)

            def k_read(t, s):
                act.wait_ge(columns_done, t.times(1, 1))
                need(act, kv_done, t.times(2, 0))
                act.wait_ge(k_turned, t.times(1, 1))
                nc.scalar.activation(kx[:, s], bank_y[:, s], ACT.Copy,
                                     scale=kept[:, t.par, s:s + 1]).then_inc(kx_done, 1)

            def x_upper(t):
                act.wait_ge(x_turned, t.times(1, 1))
                nc.scalar.copy(xT_hi[:].rearrange("p c s t -> p s c t"),
                               bank_t[:].rearrange("p s (c t) -> p s c t", c=C)).then_inc(xhi_done, 1)

            def q_read(t):
                act.wait_ge(q_turned, t.times(1, 1))
                need(act, y_done, t.times(2, 0))
                nc.scalar.copy(qT[:].rearrange("p s c t -> p (s c t)"),
                               bank_a[:].rearrange("p s d -> p (s d)")).then_inc(qT_done, 1)

            def slot(t, first, live, more):
                before = t.plus(-1)
                if live:
                    k_expose(t, 0)
                    if is_slot(t, 1):
                        copy_embedding(0)
                    if is_slot(t, FILM1):
                        copy_embedding(1)
                    k_expose(t, 1)
                    q_expose(t, 0)
                    if is_slot(t, NP - 1):
                        upper_weight(1, 0)
                    q_expose(t, 1)
                    if is_slot(t, NP - 1):
                        upper_weight(1, 1)
                else:
                    upper_weight(1, 2)
                if not first:
                    tanh(before, 0)
                if live:
                    k_read(t, 0)
                    k_read(t, 1)
                if not first:
                    u_upper(before, 0)
                    tanh(before, 1)
                if more:
                    x_upper(t.plus(1))
                if not first:
                    u_upper(before, 1)
                if live:
                    q_read(t)
                else:
                    upper_weight(1, 3)

            def copy_embedding(n):
                act.wait_ge(emb_done, n + 1)
                need(act, emb_turned, n)
                nc.scalar.copy(emb_rows[:], bank_t[:, 0]).then_inc(emb_copied, 1)

            def upper_weight(n, pos):
                m = ORDER[pos]
                act.wait_ge(raw_in[m], 16 * (n + 1))
                if n == 0:
                    act.wait_ge(vec_ready, 1)
                else:
                    act.wait_ge((q_done, kT_done, v_done, out_done)[m], 2 * NP)
                for c in range(C):
                    nc.scalar.activation(w_hi[:, m, c, :], raw[:, m, c, :], ACT.Copy,
                                         scale=scale_of(n, m, c)).then_inc(upper_done, 1)

            def bias_rows(pos):
                row, m = (row_k, 1) if pos == 0 else (row_q, 0)
                act.wait_ge(row_zero, 3)
                act.wait_ge(full_done, pos + 1)
                nc.scalar.copy(row[0:1, :], full[0:1, m, :]).then_inc(row_act, 1)
                act.wait_ge(piece_done, pos + 1)
                nc.scalar.copy(row[32:33, :], piece[32:33, :]).then_inc(row_act, 1)

            upper_weight(0, 0)
            x_upper(at(0))
            upper_weight(0, 1)
            bias_rows(0)
            bias_rows(1)
            upper_weight(0, 2)
            upper_weight(0, 3)
            act.wait_ge(cond_in, 16)
            nc.scalar.activation(cond_tanh, cond, ACT.Tanh, scale=0.5).then_inc(silu_tanh, 1)
            slots(act, slot, more_last=True)

        @block.tensor
        def _(pe):
            def project(out, m, s, row=None):
                for c in range(C):
                    for hi, lo in ((xT_hi, w_hi), (xT_hi, w_lo), (xT_lo, w_hi)):
                        last = nc.tensor.matmul(out, hi[:, c, s, :], lo[:, m, c, :],
                                                start=(c == 0 and lo is w_hi and hi is xT_hi),
                                                stop=(row is None and c == C - 1 and hi is xT_lo))
                if row is not None:
                    last = nc.tensor.matmul(out, g["three"][:], row[:], start=False, stop=True)
                return last

            def turn_x(t):
                pe.wait_ge(x_normed, t.times(2, 2))
                for s in range(2):
                    for c in range(C):
                        last = nc.tensor.transpose(bank_t[:, s, c * T:(c + 1) * T],
                                                   x[:, t.par, s, c * P:(c + 1) * P], ident[:])
                last.then_inc(x_turned, 1)

            def k_transposed(t, h):
                if h == 0:
                    pe.wait_ge(xhi_done, t.times(1, 1))
                    pe.wait_ge(xlo_done, t.times(1, 1))
                    need(pe, qT_done, t.times(1, 0))
                if is_slot(t, 0) and h == 0:
                    pe.wait_ge(lower_done, C)
                for f in (2 * h, 2 * h + 1):
                    out = bank_a[:, h, (f % 2) * 2 * T:(f % 2 + 1) * 2 * T]
                    for c in range(C):
                        for w, xs in ((w_hi, xT_hi), (w_lo, xT_hi), (w_hi, xT_lo)):
                            nc.tensor.matmul(out, w[:, 1, c, f * P:(f + 1) * P],
                                             xs[:, c].rearrange("p s t -> p (s t)"),
                                             start=(c == 0 and w is w_hi and xs is xT_hi), stop=False)
                    if is_slot(t, 0) and f == 0:
                        pe.wait_ge(row_act, 2)
                        pe.wait_ge(row_dve, 1)
                        pe.wait_ge(mask_row_in, 16)
                        pe.wait_ge(select_done, 4)
                    last = nc.tensor.matmul(out, row_k[:, f * P:(f + 1) * P],
                                            g["mask_rows"][:, bass.ds(t.times(2 * T), 2 * T)],
                                            start=False, stop=True)
                last.then_inc(kT_done, 1)

            def q_rows(t, s):
                need(pe, out_read, t.times(2, -3 + s))
                if is_slot(t, 0):
                    pe.wait_ge(lower_done, 2 * C)
                    pe.wait_ge(row_act, 4)
                    pe.wait_ge(row_dve, 2)
                project(bank_b[:, s], 0, s, row_q).then_inc(q_done, 1)

            def v_rows(t, s):
                pe.wait_ge(k_shifted, t.times(2, s + 1))
                if is_slot(t, 0):
                    pe.wait_ge(lower_done, 3 * C)
                project(bank_a[:, s], 2, s).then_inc(v_done, 1)

            def turn_k(t):
                pe.wait_ge(k_scaled, t.times(2, 2))
                need(pe, y_read, t.times(2, 0))
                if is_slot(t, 0):
                    pe.wait_ge(bv_done, 1)
                    pe.wait_ge(setup_copied, 1)
                for s in range(2):
                    for c in range(C):
                        last = nc.tensor.transpose(bank_y[:, s, c * P:(c + 1) * P], k_exp[:, c, s, :], ident[:])
                last.then_inc(k_turned, 1)

            def turn_q(t):
                pe.wait_ge(q_exped, t.times(2, 2))
                pe.wait_ge(v_read, t.times(2, 2))
                for s in range(2):
                    for c in range(C):
                        last = nc.tensor.transpose(bank_a[:, s, c * T:(c + 1) * T],
                                                   q_exp[:, s, c * P:(c + 1) * P], ident[:])
                last.then_inc(q_turned, 1)

            def v_times_k(t, s):
                pe.wait_ge(kx_done, t.times(2, s + 1))
                pe.wait_ge(v_read, t.times(2, s + 1))
                for c in range(C):
                    last = nc.tensor.matmul(bank_y[:, s, c * P:(c + 1) * P], v[:, s, c * P:(c + 1) * P],
                                            kx[:, s, c * P:(c + 1) * P], start=True, stop=True)
                last.then_inc(kv_done, 1)

            def q_times_attn(t, s):
                pe.wait_ge(attn_done, t.times(2, 2))
                if s == 0:
                    pe.wait_ge(qT_done, t.times(1, 1))
                else:
                    pe.wait_ge(y_read, t.times(2, 1))
                for c in range(C):
                    last = nc.tensor.matmul(bank_y[:, c // 2, (c % 2) * HC * V1:(c % 2 + 1) * HC * V1],
                                            qT[:, s, c, :], attn[:, s, c].rearrange("p h d -> p (h d)"),
                                            start=True, stop=True)
                last.then_inc(y_done, 1)

            def turn_y(t, s):
                for n, used in ((0, 0), (1, FILM1 - 1)):
                    if is_slot(t, used) and s == 0:
                        pe.wait_ge(film_done, 2 * n + 2)
                pe.wait_ge(y_normed, t.times(2, s + 1))
                for c in range(C):
                    last = nc.tensor.transpose(bank_t[:, s, c * T:(c + 1) * T], y[:, s, c * P:(c + 1) * P], ident[:])
                last.then_inc(y_turned, 1)

            def out_rows(t, s, after):
                if is_slot(t, 0):
                    pe.wait_ge(out_lower_done, C)
                if after is not None:
                    pe.wait_ge(q_shifted, after.times(2, s + 1))
                pe.wait_ge(uhi_done, t.times(2, s + 1))
                pe.wait_ge(ulo_done, t.times(2, s + 1))
                for c in range(C):
                    for us, w in ((u_hi, w_hi), (u_hi, w_lo), (u_lo, w_hi)):
                        last = nc.tensor.matmul(bank_b[:, s], us[:, s, c, :], w[:, 3, c, :],
                                                start=(c == 0 and us is u_hi and w is w_hi),
                                                stop=(c == C - 1 and us is u_lo))
                last.then_inc(out_done, 1)

            def slot(t, first, live, more):
                before = t.plus(-1)
                if live:
                    k_transposed(t, 0)
                    k_transposed(t, 1)
                if is_slot(t, 1):
                    embed(0)
                if is_slot(t, FILM1):
                    embed(1)
                if not first:
                    q_times_attn(before, 0)
                if live:
                    q_rows(t, 0)
                    if is_slot(t, 1):
                        turn_embedding(0)
                    if is_slot(t, FILM1):
                        turn_embedding(1)
                else:
                    layer1_bias(0, bank_a[:, 0])
                if not first:
                    q_times_attn(before, 1)
                if live:
                    q_rows(t, 1)
                if first:
                    pe.wait_ge(full_done, 1)
                    bias_through(2, bank_y[:, 1])
                if not first:
                    turn_y(before, 0)
                if live:
                    v_rows(t, 0)
                    v_rows(t, 1)
                else:
                    layer1_bias(1, bank_a[:, 1])
                if not first:
                    turn_y(before, 1)
                if not live:
                    pe.wait_ge(full_done, 3)
                    layer1_bias(2, bank_a[:, 0])
                if first:
                    turn_setup()
                    turn_q(t)
                    turn_k(t)
                elif live:
                    turn_k(t)
                    turn_q(t)
                if more:
                    if not first:
                        pe.wait_ge(z_scaled, before.times(2, 2))
                    turn_x(t.plus(1))
                if live:
                    v_times_k(t, 0)
                    v_times_k(t, 1)
                if not first:
                    out_rows(before, 0, t if live else None)
                    out_rows(before, 1, t if live else None)
                if not live:
                    turn_layer1_biases()

            def bias_through(pos, out):
                m = ORDER[pos]
                pe.wait_ge(raw_in[m], 16)
                for c in range(C):
                    last = nc.tensor.matmul(out, norm_bias[:, c, :], raw[:, m, c, :], start=(c == 0), stop=(c == C - 1))
                last.then_inc(through_done, 1)

            def turn_setup():
                pe.wait_ge(rows_in, 16 * 10)
                pe.wait_ge(parts_done, 1)
                pe.wait_ge(silu_done, 1)
                nc.tensor.transpose(bank_y[:, 0, 0:ALL_ROWS], rows[:], ident[0:ALL_ROWS, 0:ALL_ROWS])
                nc.tensor.transpose(bank_y[:, 0, 64:64 + B], maskf[:], ident[0:B, 0:B])
                nc.tensor.transpose(bank_y[:, 0, 128:128 + B], off[:], ident[0:B, 0:B])
                nc.tensor.transpose(bank_y[:, 0, 192:192 + B], score_mask[:], ident[0:B, 0:B])
                for k in range(EC):
                    last = nc.tensor.transpose(cond_t[:, k, :], cond[:, k * P:(k + 1) * P], ident[0:B, 0:B])
                last.then_inc(setup_turned, 1)

            def embed(n):
                pe.wait_ge(emb_in, 64 * (n + 1))
                for k in range(EC // 2):
                    for tile in range(4):
                        h, kk = tile // 2, (tile % 2) * (EC // 2) + k
                        last = nc.tensor.matmul(bank_t[tile * B:(tile + 1) * B, 0], condT[:, kk, :],
                                                emb_w[:, kk, h * D:(h + 1) * D],
                                                start=(k == 0), stop=(k == EC // 2 - 1))
                last.then_inc(emb_done, 1)

            def turn_embedding(n):
                pe.wait_ge(emb_copied, n + 1)
                for c in range(C):
                    last = nc.tensor.transpose(bank_t[:, 1, c * P:(c + 1) * P], emb_rows[:, c * P:(c + 1) * P], ident[:])
                last.then_inc(emb_turned, 1)

            def layer1_bias(m, bank):
                if m == 0:
                    pe.wait_ge(bias_wide, 2)
                    pe.wait_ge(qT_done, NP)
                pe.wait_ge(raw_in[m], 32)
                for c in range(C):
                    last = nc.tensor.matmul(bank, norm_bias[:, c, :], raw[:, m, c, :], start=(c == 0), stop=(c == C - 1))
                last.then_inc(through_done, 1)

            def turn_layer1_biases():
                pe.wait_ge(full_done, 4)
                for m in range(2):
                    for f in range(C):
                        n = m * C + f
                        last = nc.tensor.transpose(bank_y[:, 0, n * B:(n + 1) * B],
                                                   q_exp[0:B, m, f * P:(f + 1) * P], ident[0:B, 0:B])
                last.then_inc(bqk_turned, 1)

            pe.wait_ge(ident_done, 1)
            pe.wait_ge(norm_rows_in, 32)
            nc.tensor.transpose(bank_b[:, 0, 0:FS], rows[0:FS, :], ident[0:FS, 0:FS]).then_inc(norm_turned, 1)
            turn_x(at(0))
            pe.wait_ge(bias_wide, 1)
            bias_through(0, bank_y[:, 1])
            bias_through(1, bank_b[:, 1])
            slots(pe, slot, more_last=True)

        @block.vector
        def _(dve):
            def x_stats(t):
                dve.wait_ge(x_in[t.par], 16 * t.use())
                for s in range(2):
                    nc.vector.bn_stats(stats[:, s, :], x[:, t.par, s, :]).then_inc(stats_done, 1)
                dve.wait_ge(stats_done, t.times(2, 2))
                nc.vector.memset(idle[:], 0.0)
                for s in range(2):
                    last = nc.vector.bn_aggr(moments[:, s, :], stats[:, s, :])
                last.then_inc(moments_done, 1)

            def x_norm(t, sequences=(0, 1)):
                dve.wait_ge(rstd_done, t.times(1, 1))
                for s in sequences:
                    nc.vector.tensor_scalar(x[:, t.par, s, :], x[:, t.par, s, :], moments[:, s, 0:1], rstd[:, s:s + 1],
                                            ALU.subtract, ALU.mult).then_inc(x_normed, 1)

            def x_lower(t):
                dve.wait_ge(xhi_done, t.times(1, 1))
                nc.vector.tensor_tensor(out=xT_lo[:].rearrange("p c s t -> p s c t"),
                                        in0=bank_t[:].rearrange("p s (c t) -> p s c t", c=C),
                                        in1=xT_hi[:].bitcast(F32).rearrange("p c s t -> p s c t"),
                                        op=ALU.subtract).then_inc(xlo_done, 1)

            def k_shift(t, h):
                src = bank_a[:, h].rearrange("p (f t) -> p f t", t=T)
                dve.wait_ge(kT_done, t.times(2, h + 1))
                nc.vector.tensor_reduce(k_max[:, 4 * h:4 * h + 4], src, AX.X, ALU.max).then_inc(k_maxed, 1)
                need(dve, k_turned, t.times(1, 0))
                dve.wait_ge(k_maxed, t.times(2, h + 1))
                nc.vector.tensor_tensor(out=k_exp[:, 2 * h:2 * h + 2].rearrange("p c s t -> p (c s) t"), in0=src,
                                        in1=k_max[:, 4 * h:4 * h + 4].unsqueeze(2).broadcast_to([P, 4, T]),
                                        op=ALU.subtract).then_inc(k_shifted, 1)

            def q_shift(t, s):
                src = bank_b[:, s].rearrange("p (h d) -> p h d", h=H)
                dve.wait_ge(q_done, t.times(2, s + 1))
                nc.vector.tensor_reduce(q_max[:, s, :], src, AX.X, ALU.max).then_inc(q_maxed, 1)
                need(dve, q_turned, t.times(1, 0))
                dve.wait_ge(q_maxed, t.times(2, s + 1))
                nc.vector.tensor_tensor(out=q_exp[:, s].rearrange("p (h d) -> p h d", h=H), in0=src,
                                        in1=q_max[:, s, :].unsqueeze(2).broadcast_to([P, H, DH]),
                                        op=ALU.subtract).then_inc(q_shifted, 1)

            def v_read_out(t, s):
                need(dve, kv_done, t.times(2, s - 1))
                dve.wait_ge(v_done, t.times(2, s + 1))
                nc.vector.tensor_tensor(out=v[:, s], in0=bank_a[:, s], in1=g["bv"][:, 0, :],
                                        op=ALU.add).then_inc(v_read, 1)

            def k_sums(t, h):
                dve.wait_ge(k_exped, t.times(2, h + 1))
                nc.vector.tensor_reduce(k_sum[:, 4 * h:4 * h + 4],
                                        k_exp[:, 2 * h:2 * h + 2].rearrange("p c s t -> p (c s) t"),
                                        AX.X, ALU.add).then_inc(k_summed, 1)
                need(dve, k_scaled, t.times(2, h - 1))
                dve.wait_ge(k_summed, t.times(2, h + 1))
                nc.vector.reciprocal(k_inv[:, 4 * h:4 * h + 4], k_sum[:, 4 * h:4 * h + 4]).then_inc(k_inverted, 1)

            def attn_blocks(t, s):
                dve.wait_ge(kv_done, t.times(2, s + 1))
                need(dve, y_done, t.times(2, s - 1))
                for j in range(HC):
                    rows = slice(DH * j, DH * j + DH)
                    last = nc.vector.tensor_copy(
                        attn[rows, s, :, j, 0:DH],
                        bank_y[rows, s].rearrange("p (c h e) -> p c h e", c=C, h=HC)[:, :, j, :])
                last.then_inc(attn_done, 1)

            def y_read_out(t, s):
                src = bank_y[:, :, 0:2 * HC * V1].rearrange("p b (h d) -> p b h d", d=V1)
                dve.wait_ge(y_done, t.times(2, s + 1))
                nc.vector.reciprocal(q_sum[:, s, :].rearrange("p (b h) -> p b h", b=2),
                                     src[:, :, :, DH]).then_inc(q_summed, 1)
                need(dve, y_turned, t.times(2, s - 1))
                dve.wait_ge(q_summed, t.times(2, s + 1))
                nc.vector.tensor_tensor(
                    out=y[:, s].rearrange("p (b h d) -> p b h d", b=2, d=DH), in0=src[:, :, :, 0:DH],
                    in1=q_sum[:, s, :].rearrange("p (b h) -> p b h", b=2).unsqueeze(3).broadcast_to([P, 2, H // 2, DH]),
                    op=ALU.mult).then_inc(y_read, 1)
                dve.wait_ge(y_read, t.times(2, s + 1))
                nc.vector.bn_stats(y_stats[:, s, :], y[:, s]).then_inc(y_stats_done, 1)
                dve.wait_ge(y_stats_done, t.times(2, s + 1))
                nc.vector.memset(idle[:], 0.0)
                nc.vector.bn_aggr(y_moments[:, s, :], y_stats[:, s, :]).then_inc(y_moments_done, 1)

            def y_norm(t, s):
                dve.wait_ge(y_rstd_done, t.times(2, s + 1))
                nc.vector.tensor_scalar(y[:, s], y[:, s], y_moments[:, s, 0:1], y_rstd[:, s:s + 1],
                                        ALU.subtract, ALU.mult).then_inc(y_normed, 1)

            def z_scale(t, s):
                need(dve, ulo_done, t.times(2, s - 1))
                need(dve, uhi_done, t.times(2, s - 1))
                dve.wait_ge(film_ready, t.times(2, 2))
                dve.wait_ge(y_turned, t.times(2, s + 1))
                nc.vector.tensor_tensor(out=z[:, s], in0=bank_t[:, s].rearrange("p (c t) -> p c t", c=C),
                                        in1=factor[:, t.par, s, :].unsqueeze(2).broadcast_to([P, C, T]),
                                        op=ALU.mult).then_inc(z_scaled, 1)

            def u_form(t, s):
                dve.wait_ge(tanh_done, t.times(2, s + 1))
                nc.vector.scalar_tensor_tensor(out=z[:, s], in0=z_tanh[:, s], scalar=1.0, in1=z[:, s],
                                               op0=ALU.add, op1=ALU.mult).then_inc(u_done, 1)

            def u_lower(t, s):
                need(dve, out_done, t.times(2, s - 1))
                dve.wait_ge(uhi_done, t.times(2, s + 1))
                nc.vector.tensor_tensor(out=u_lo[:, s], in0=z[:, s], in1=u_hi[:, s].bitcast(F32),
                                        op=ALU.subtract).then_inc(ulo_done, 1)

            def out_add(t, s):
                dve.wait_ge(res_biased, t.times(1, 1))
                dve.wait_ge(out_done, t.times(2, s + 1))
                nc.vector.tensor_tensor(out=res[:, t.par, s, :], in0=bank_b[:, s], in1=res[:, t.par, s, :],
                                        op=ALU.add).then_inc(out_read, 1)

            def columns(t):
                need(dve, kx_done, t.times(2, -2))
                if is_slot(t, 0):
                    dve.wait_ge(vec_ready, 5)
                nc.vector.tensor_copy(kept[:, t.par], g["valid"][:, bass.ds(t.times(2), 2)]).then_inc(columns_done, 1)

            def film_columns(t):
                need(dve, z_done, t.times(2, -2))
                both = bass.ds(t.times(2), 2)
                nc.vector.tensor_copy(factor[:, t.par], g["film"][:, 0, 0, both, :]).then_inc(film_ready, 1)
                nc.vector.tensor_copy(shift[:, t.par], g["film"][:, 0, 1, both, :]).then_inc(film_ready, 1)

            def lower_weight(n, pos, chunks=range(C)):
                m = ORDER[pos]
                for c in chunks:
                    dve.wait_ge(upper_done, (4 * n + pos) * C + c + 1)
                    nc.vector.scalar_tensor_tensor(out=w_lo[:, m, c, :], in0=raw[:, m, c, :], scalar=scale_of(n, m, c),
                                                   in1=w_hi[:, m, c, :].bitcast(F32),
                                                   op0=ALU.mult, op1=ALU.subtract).then_inc(lower_done, 1)

            def bias_parts(pos):
                row, m = (row_k, 1) if pos == 0 else (row_q, 0)
                dve.wait_ge(qk_bias_in, 32)
                dve.wait_ge(through_done, pos + 1)
                nc.vector.tensor_tensor(out=full[:, m, :], in0=(bank_y if pos == 0 else bank_b)[:, 1],
                                        in1=full[:, m, :], op=ALU.add).then_inc(full_done, 1)
                dve.wait_ge(full_done, pos + 1)
                link(nc.vector.tensor_copy(piece_b[:], full[:, m, :]))
                if pos == 1:
                    dve.wait_ge(row_act, 2)
                nc.vector.tensor_tensor(out=piece[:], in0=full[:, m, :], in1=piece_b[:],
                                        op=ALU.subtract).then_inc(piece_done, 1)
                dve.wait_ge(piece_done, pos + 1)
                link(nc.vector.tensor_copy(piece_b[:], piece[:]))
                dve.wait_ge(row_zero, 3)
                nc.vector.tensor_tensor(out=row[64:65, :], in0=piece[64:65, :], in1=piece_b[64:65, :],
                                        op=ALU.subtract).then_inc(row_dve, 1)

            def v_bias(n, bank):
                dve.wait_ge(v_bias_in, 32)
                dve.wait_ge(through_done, 3 + 3 * n)
                nc.vector.tensor_tensor(out=g["bv"][:, n, :], in0=bank, in1=g["bv"][:, n, :],
                                        op=ALU.add).then_inc(bv_done, 1)

            def masks():
                dve.wait_ge(masks_in, 16)
                link(nc.vector.tensor_scalar(maskf[:], maskf[:], -1.0, 1.0, ALU.mult, ALU.add))
                link(nc.vector.tensor_reduce(count[:], maskf[:], AX.X, ALU.add))
                link(nc.vector.reciprocal(count[:], count[:]))
                link(nc.vector.tensor_scalar(count[:], count[:], 0.0, None, ALU.mult))
                link(nc.vector.tensor_scalar(maskf[:], maskf[:], count[:, 0:1], None, ALU.add))
                nc.vector.tensor_scalar(off[:], score_mask[:], 1.0, -SCORE_OFF, ALU.subtract, ALU.mult).then_inc(parts_done, 1)
                dve.wait_ge(silu_tanh, 1)
                nc.vector.scalar_tensor_tensor(out=cond, in0=cond_tanh, scalar=1.0, in1=cond,
                                               op0=ALU.add, op1=ALU.mult).then_inc(silu_done, 1)

            def offset_parts():
                dve.wait_ge(parts_done, 1)
                link(nc.vector.tensor_copy(rest[:], off[:]))
                for r in range(3):
                    link(nc.vector.tensor_copy(part[:, r, :], rest[:]))
                    if r < 2:
                        link(nc.vector.tensor_tensor(out=rest[:], in0=rest[:], in1=part[:, r, :], op=ALU.subtract))

            def setup_columns():
                dve.wait_ge(setup_turned, 1)
                nc.vector.tensor_copy(g["valid"][:], bank_y[:, 0, 64:64 + B]).then_inc(vec_ready, 1)
                nc.vector.tensor_copy(g["vec"][:, FS:ALL_ROWS], bank_y[:, 0, FS:ALL_ROWS]).then_inc(vec_ready, 1)
                nc.vector.tensor_copy(g["score_keep"][:], bank_y[:, 0, 192:192 + B]).then_inc(vec_ready, 1)
                nc.vector.tensor_copy(g["score_off"][:], bank_y[:, 0, 128:128 + B]).then_inc(vec_ready, 1)
                nc.vector.tensor_scalar(condT[:], cond_t, 0.5, None, ALU.mult).then_inc(setup_copied, 1)

            def film(n):
                v, f = n * ROWS, g["film"]

                def col(r):
                    return g["vec"][:, v + r:v + r + C].unsqueeze(2).broadcast_to([P, C, B])

                def by_sequence(k):
                    return f[:, n, k].rearrange("p b c -> p c b")

                dve.wait_ge(emb_turned, n + 1)
                halves = bank_t[:, 1].rearrange("p (c h k b) -> p h c k b", c=C, h=2, k=2)
                for h in range(2):
                    nc.vector.tensor_copy(emb[:, h * C:(h + 1) * C, :], halves[:, h, :, 0, :]).then_inc(emb_moved, 1)
                dve.wait_ge(emb_moved, 2 * n + 2)
                for h in range(2):
                    nc.vector.tensor_tensor(out=emb[:, h * C:(h + 1) * C, :], in0=halves[:, h, :, 1, :],
                                            in1=emb[:, h * C:(h + 1) * C, :], op=ALU.add).then_inc(film_done, 1)
                dve.wait_ge(film_done, 2 * n + 2)
                link(nc.vector.tensor_tensor(out=one_plus[:], in0=emb[:, 0:C, :], in1=col(EB), op=ALU.add))
                link(nc.vector.tensor_tensor(out=film_shift[:], in0=emb[:, C:FC, :], in1=col(EB + C), op=ALU.add))
                link(nc.vector.tensor_scalar(one_plus[:], one_plus[:], 1.0, 0.5, ALU.add, ALU.mult))
                link(nc.vector.tensor_scalar(film_shift[:], film_shift[:], 0.5, None, ALU.mult))
                link(nc.vector.tensor_tensor(out=by_sequence(0), in0=one_plus[:], in1=col(FS), op=ALU.mult))
                link(nc.vector.tensor_tensor(out=one_plus[:], in0=one_plus[:], in1=col(FB), op=ALU.mult))
                link(nc.vector.tensor_tensor(out=by_sequence(1), in0=one_plus[:], in1=film_shift[:], op=ALU.add))

            def spread_norm_bias(n):
                nb = n * ROWS + NB
                nc.vector.tensor_copy(norm_bias[:], g["vec"][:, nb:nb + C].unsqueeze(2).broadcast_to([P, C, P])
                                      ).then_inc(bias_wide, 1)

            def first_slot(t):
                k_shift(t, 0)
                lower_weight(0, 2)
                k_shift(t, 1)
                k_sums(t, 0)
                q_shift(t, 0)
                k_sums(t, 1)
                q_shift(t, 1)
                masks()
                v_bias(0, bank_y[:, 1])
                x_stats(t.plus(1))
                v_read_out(t, 0)
                v_read_out(t, 1)
                setup_columns()
                columns(t)
                x_norm(t.plus(1))
                x_lower(t.plus(1))
                offset_parts()

            def layer1_bias_copy(m):
                dve.wait_ge(through_done, 4 + m)
                nc.vector.tensor_copy(q_exp[0:B, m], bank_a[0:B, m]).then_inc(full_done, 1)

            def last_slot(before):
                attn_blocks(before, 0)
                attn_blocks(before, 1)
                spread_norm_bias(1)
                y_read_out(before, 0)
                film_columns(before)
                lower_weight(1, 1, (0,))
                y_norm(before, 0)
                lower_weight(1, 1, (1, 2))
                y_read_out(before, 1)
                z_scale(before, 0)
                layer1_bias_copy(0)
                y_norm(before, 1)
                layer1_bias_copy(1)
                u_form(before, 0)
                z_scale(before, 1)
                u_lower(before, 0)
                lower_weight(1, 1, (3,))
                u_form(before, 1)
                u_lower(before, 1)
                lower_weight(1, 2)
                out_add(before, 0)
                v_bias(1, bank_a[:, 0])
                out_add(before, 1)
                dve.wait_ge(bqk_turned, 1)
                nc.vector.tensor_tensor(out=g["bqk"][:].rearrange("p m c -> p (m c)"),
                                        in0=bank_y[:, 0, 0:2 * C * B].rearrange("p (k b) -> p k b", b=B)[:, :, 0],
                                        in1=g["vec"][:, ROWS + QB:ROWS + QB + 2 * C], op=ALU.add).then_inc(bqk_done, 1)
                lower_weight(1, 3, range(C // 2, C))
                dve.wait_ge(lower_done, 6 * C + C // 2)
                dve.wait_ge(bqk_done, 1)

            def slot(t, first, live, more):
                before = t.plus(-1)
                if first:
                    first_slot(t)
                    return
                if not live:
                    last_slot(before)
                    return
                attn_blocks(before, 0)
                attn_blocks(before, 1)
                k_shift(t, 0)
                columns(t)
                if more:
                    x_stats(t.plus(1))
                y_read_out(before, 0)
                k_shift(t, 1)
                k_sums(t, 0)
                q_shift(t, 0)
                if is_slot(t, 1):
                    film(0)
                if is_slot(t, FILM1):
                    film(1)
                y_norm(before, 0)
                film_columns(before)
                y_read_out(before, 1)
                k_sums(t, 1)
                q_shift(t, 1)
                y_norm(before, 1)
                z_scale(before, 0)
                v_read_out(t, 0)
                if more:
                    x_norm(t.plus(1), (0,))
                v_read_out(t, 1)
                if more:
                    x_norm(t.plus(1), (1,))
                z_scale(before, 1)
                u_form(before, 0)
                u_lower(before, 0)
                u_form(before, 1)
                if more:
                    x_lower(t.plus(1))
                u_lower(before, 1)
                if is_slot(t, NP - 1):
                    lower_weight(1, 0)
                out_add(before, 0)
                out_add(before, 1)

            link = chained(dve, chain)
            nc.vector.memset(attn[:], 0.0).then_inc(ones_set, 1)
            dve.wait_ge(ones_set, 1)
            for j in range(HC):
                nc.vector.memset(attn[DH * j:DH * j + DH, :, :, j, DH:V1], 1.0).then_inc(ones_set, 1)
            dve.wait_ge(ones_set, 1 + HC)
            nc.vector.memset(g["three"][:], 0.0).then_inc(row_zero, 1)
            nc.vector.memset(row_k[:], 0.0).then_inc(row_zero, 1)
            nc.vector.memset(row_q[:], 0.0).then_inc(row_zero, 1)
            dve.wait_ge(row_zero, 3)
            for r in range(3):
                nc.vector.memset(g["three"][32 * r:32 * r + 1, :], 1.0).then_inc(select_done, 1)
            nc.vector.memset(row_k[96:97, :], -BIG).then_inc(select_done, 1)
            dve.wait_ge(norm_turned, 1)
            nc.vector.tensor_copy(g["vec"][:, 0:FS], bank_b[:, 0, 0:FS]).then_inc(vec_ready, 1)
            dve.wait_ge(vec_ready, 1)
            spread_norm_bias(0)
            x_stats(at(0))
            x_norm(at(0))
            dve.wait_ge(keep_in, 16)
            link(nc.vector.tensor_scalar(maskf[:], keep_mask[:], 1.0, None, ALU.is_equal))
            nc.vector.tensor_copy(mask_b[:], maskf[:]).then_inc(keep_cast, 1)
            lower_weight(0, 0)
            x_lower(at(0))
            bias_parts(0)
            lower_weight(0, 1)
            bias_parts(1)
            slots(dve, slot, more_last=True)


def layer1(nc, a, g, mid, out):
    with ExitStack() as ctx:
        def sb(name, shape, dt=F32):
            return ctx.enter_context(nc.sbuf_tensor(name + "_l1", shape, dt))

        def ps(name, shape):
            return ctx.enter_context(nc.psum_tensor(name + "_l1", shape, F32))

        def sem(name):
            return ctx.enter_context(nc.semaphore(name + "_l1"))

        w_hi, w_lo, ident = g["w_hi"], g["w_lo"], g["ident"]
        x, stats, moments, rstd, xT_hi, xT_lo = (g[k] for k in ("x", "stats", "moments", "rstd", "xT_hi", "xT_lo"))
        qT = sb("qT", [P, 2, C, 2, T], F32R)
        kT = sb("kT", [P, 2, C, 2, T], F32R)
        q_wide = sb("q_wide", [P, 2, C, 2, HC, T], F32R)
        k_wide = sb("k_wide", [P, C, 2, HC, T], F32R)
        v = sb("v", [P, 2, H, V1])
        shift_q = sb("shift_q", [P, 2 * H])
        shift_rows = sb("shift_rows", [P, P], BF16)
        pick = sb("pick", [P, 2 * H], BF16)
        prob = sb("prob", [P, 4, HC, T])
        y_sum = sb("y_sum", [P, 2, H])
        y = sb("y", [P, 2, D])
        y_stats = sb("y_stats", [P, 2, 6])
        y_moments = sb("y_moments", [P, 2, 2])
        y_rstd = sb("y_rstd", [P, 2])
        factor = sb("factor", [P, 2, 2, C])
        shift = sb("shift", [P, 2, 2, C])
        off = sb("off", [P, 2, 2])
        keep = sb("keep", [P, 2, 2])
        z = sb("z", [P, 2, C, T])
        z_tanh = sb("z_tanh", [P, 2, C, T])
        u_hi = sb("u_hi", [P, 2, C, T], F32R)
        u_lo = sb("u_lo", [P, 2, C, T], F32R)
        idle = sb("idle", [P, 1])
        res = g["res"]

        bank_a = ps("bank_a", [P, 2, D])
        bank_b = ps("bank_b", [P, 2, D])
        bank_t = ps("bank_t", [P, 2, D])
        bank_y = ps("bank_y", [P, 2, D])
        chunk_bank = [bank_a[:, 0], bank_a[:, 1], bank_b[:, 0], bank_b[:, 1]]

        res_in = [sem("res_in0"), sem("res_in1")]
        stored = [sem("stored0"), sem("stored1")]
        x_in = g["x_in"]
        (stats_done, moments_done, eps_added, rstd_done, x_normed, x_turned, xhi_done, xlo_done) = g["x_chain"]
        names = ("ready wide_cleared q_done qhi_done qlo_done spread_in k_spread_in k_done khi_done klo_done v_done v_read v_masked "
                 "rough_done max_done max_turned shift_split score_done exp_done pv_done "
                 "y_summed y_read y_stats_done y_moments_done y_eps y_rstd_done y_normed y_turned "
                 "z_scaled z_done tanh_done u_done uhi_done ulo_done out_done out_read res_biased columns_done picked")
        (ready, wide_cleared,
         q_done, qhi_done, qlo_done, spread_in, k_spread_in, k_done, khi_done, klo_done, v_done, v_read, v_masked,
         rough_done, max_done, max_turned, shift_split, score_done, exp_done, pv_done,
         y_summed, y_read, y_stats_done, y_moments_done, y_eps, y_rstd_done, y_normed, y_turned,
         z_scaled, z_done, tanh_done, u_done, uhi_done, ulo_done, out_done, out_read, res_biased,
         columns_done, picked) = [sem(n) for n in names.split()]

        mid_dram, out_dram = pairs_of(mid), pairs_of(out)

        def early(t, s):
            return is_slot(t, NP - 1) and s == 0

        def z_bank(t, s):
            return bank_y[:, 0] if early(t, s) else bank_t[:, s]

        def out_bank(t, s):
            return bank_y[:, 1] if early(t, s) else bank_b[:, s]

        block = ctx.enter_context(nc.Block())

        @block.sync
        def _(sp):
            def load_x(t):
                sp.wait_ge(x_turned, t.times(1, NP - 1))
                sp.dma_start(x[:, t.par], mid_dram[t.times(1)]).then_inc(x_in[t.par], 16)

            def slot(t, first, live, more):
                if more and not is_slot(t, NP - 2):
                    load_x(t.plus(2))
                if first:
                    for n in range(2):
                        sp.wait_ge(g["mid_stored"][n], 16 * NP // 2)
                if live:
                    need(sp, stored[t.par], 16 * (t.use() - 1))
                    sp.dma_start(res[:, t.par], mid_dram[t.times(1)]).then_inc(res_in[t.par], 16)
                    if first:
                        sp.wait_ge(wide_cleared, 1)
                    sp.wait_ge(khi_done, t.times(C, C))
                    for j in range(HC):
                        rows = slice(DH * j, DH * j + DH)
                        sp.dma_start(k_wide[rows, :, :, j, :].bitcast(F32).rearrange("p c s t -> p (c s) t"),
                                     kT[rows, 0].bitcast(F32).rearrange("p c s t -> p (c s) t")).then_inc(k_spread_in, 16)
                    if first:
                        sp.wait_ge(wide_cleared, 2)
                    sp.wait_ge(qlo_done, t.times(C, C))
                    for j in range(HC):
                        rows = slice(DH * j, DH * j + DH)
                        sp.dma_start(q_wide[rows, :, :, :, j, :].bitcast(F32).rearrange("p a c s t -> p (a c s) t"),
                                     qT[rows].bitcast(F32).rearrange("p a c s t -> p (a c s) t")).then_inc(spread_in, 16)
                if not first:
                    before = t.plus(-1)
                    sp.wait_ge(out_read, before.times(2, 2))
                    sp.dma_start(out_dram[before.times(1)], res[:, before.par]).then_inc(stored[before.par], 16)

            load_x(at(1))
            slots(sp, slot)
            for n in range(2):
                sp.wait_ge(stored[n], 16 * NP // 2)

        @block.gpsimd
        def _(pool):
            def root(t):
                u = t.plus(NP)
                need(pool, x_normed, u.times(2, 0))
                pool.wait_ge(moments_done, u.times(1, 1))
                nc.gpsimd.tensor_tensor(out=rstd[:], in0=moments[:, :, 1], in1=g["eps"][:], op=ALU.add).then_inc(eps_added, 1)
                pool.wait_ge(eps_added, u.times(1, 1))
                nc.gpsimd.tensor_tensor(out=rstd[:], in0=rstd[:], in1=g["power"][:], op=ALU.pow).then_inc(rstd_done, 1)

            def y_root(t, s):
                need(pool, y_normed, t.times(2, s - 1))
                pool.wait_ge(y_moments_done, t.times(2, s + 1))
                nc.gpsimd.tensor_tensor(out=y_rstd[:, s:s + 1], in0=y_moments[:, s, 1:2], in1=g["eps"][:, 0:1],
                                        op=ALU.add).then_inc(y_eps, 1)
                pool.wait_ge(y_eps, t.times(2, s + 1))
                nc.gpsimd.tensor_tensor(out=y_rstd[:, s:s + 1], in0=y_rstd[:, s:s + 1], in1=g["power"][:, 0:1],
                                        op=ALU.pow).then_inc(y_rstd_done, 1)

            def z_shift(t, s):
                pool.wait_ge(z_scaled, t.times(2, s + 1))
                nc.gpsimd.tensor_tensor(out=z[:, s], in0=z[:, s],
                                        in1=shift[:, t.par, s, :].unsqueeze(2).broadcast_to([P, C, T]),
                                        op=ALU.add).then_inc(z_done, 1)

            def v_mask(t, s):
                pool.wait_ge(v_read, t.times(2, s + 1))
                nc.gpsimd.tensor_tensor(out=v[:, s, :, 0:DH], in0=v[:, s, :, 0:DH],
                                        in1=keep[:, t.par, s:s + 1].unsqueeze(2).broadcast_to([P, H, DH]),
                                        op=ALU.mult).then_inc(v_masked, 1)

            def bias_res(t):
                pool.wait_ge(res_in[t.par], 16 * t.use())
                nc.gpsimd.tensor_tensor(out=res[:, t.par], in0=res[:, t.par],
                                        in1=g["bo"][:, 1:2, :].broadcast_to([P, 2, D]),
                                        op=ALU.add).then_inc(res_biased, 1)

            def slot(t, first, live, more):
                before = t.plus(-1)
                if not first:
                    y_root(before, 1)
                if more:
                    root(t.plus(1))
                if not first:
                    if live:
                        z_shift(before, 0)
                    z_shift(before, 1)
                if live:
                    v_mask(t, 0)
                    v_mask(t, 1)
                    bias_res(t)
                    y_root(t, 0)
                    if not more:
                        z_shift(t, 0)

            nc.gpsimd.memset(k_wide[:].bitcast(F32), 0.0).then_inc(wide_cleared, 1)
            nc.gpsimd.memset(q_wide[:].bitcast(F32), 0.0).then_inc(wide_cleared, 1)
            slots(pool, slot)

        @block.scalar
        def _(act):
            def upper(t, dst, banks, m, h, done, signal):
                act.wait_ge(done, t.times(2, h + 1))
                for f in (2 * h, 2 * h + 1):
                    nc.scalar.activation(dst[:, 0, f].rearrange("p s t -> p (s t)"),
                                         banks[:, f // 2, (f % 2) * 2 * T:(f % 2 + 1) * 2 * T], ACT.Identity,
                                         bias=g["bqk"][:, m, f:f + 1]).then_inc(signal, 1)

            def tanh(t, s):
                act.wait_ge(z_done, t.times(2, s + 1))
                need(act, u_done, t.times(2, s - 1))
                nc.scalar.activation(z_tanh[:, s], z[:, s], ACT.Tanh).then_inc(tanh_done, 1)

            def u_upper(t, s):
                need(act, out_done, t.times(2, s - 1))
                act.wait_ge(u_done, t.times(2, s + 1))
                nc.scalar.copy(u_hi[:, s], z[:, s]).then_inc(uhi_done, 1)

            def x_upper(t):
                u = t.plus(NP)
                act.wait_ge(x_turned, u.times(1, 1))
                nc.scalar.copy(xT_hi[:].rearrange("p c s t -> p s c t"),
                               bank_t[:].rearrange("p s (c t) -> p s c t", c=C)).then_inc(xhi_done, 1)

            def expose(t, n):
                need(act, pv_done, t.times(8, n - 3))
                act.wait_ge(score_done, t.times(8, n + 1))
                nc.scalar.activation(prob[:, n % 4].rearrange("p h t -> p (h t)"), chunk_bank[n % 4], ACT.Exp,
                                     bias=off[:, t.par, n // C:n // C + 1]).then_inc(exp_done, 1)

            def slot(t, first, live, more):
                before = t.plus(-1)
                if live:
                    need(act, score_done, t.times(8, 0))
                    need(act, k_spread_in, t.times(64, 0))
                    upper(t, kT, bank_a, 1, 0, k_done, khi_done)
                    upper(t, kT, bank_a, 1, 1, k_done, khi_done)
                    need(act, spread_in, t.times(64, 0))
                    upper(t, qT, bank_b, 0, 0, q_done, qhi_done)
                if not first:
                    if live:
                        tanh(before, 0)
                    tanh(before, 1)
                if live:
                    upper(t, qT, bank_b, 0, 1, q_done, qhi_done)
                if not first:
                    if live:
                        u_upper(before, 0)
                    u_upper(before, 1)
                if more:
                    x_upper(t.plus(1))
                if live:
                    act.wait_ge(columns_done, t.times(1, 1))
                    for n in range(2 * C):
                        expose(t, n)
                    if not more:
                        tanh(t, 0)
                        u_upper(t, 0)

            slots(act, slot)

        @block.tensor
        def _(pe):
            def turn_x(t):
                u = t.plus(NP)
                pe.wait_ge(x_normed, u.times(2, 2))
                for s in range(2):
                    for c in range(C):
                        last = nc.tensor.transpose(bank_t[:, s, c * T:(c + 1) * T],
                                                   x[:, t.par, s, c * P:(c + 1) * P], ident[:])
                last.then_inc(x_turned, 1)

            def transposed(bank, m, h, signal):
                for f in (2 * h, 2 * h + 1):
                    for c in range(C):
                        for w, xs in ((w_hi, xT_hi), (w_lo, xT_hi), (w_hi, xT_lo)):
                            last = nc.tensor.matmul(bank[:, h, (f % 2) * 2 * T:(f % 2 + 1) * 2 * T],
                                                    w[:, m, c, f * P:(f + 1) * P],
                                                    xs[:, c].rearrange("p s t -> p (s t)"),
                                                    start=(c == 0 and w is w_hi and xs is xT_hi),
                                                    stop=(c == C - 1 and xs is xT_lo))
                last.then_inc(signal, 1)

            def k_transposed(t, h):
                if h == 0:
                    pe.wait_ge(xhi_done, t.times(1, NP + 1))
                    pe.wait_ge(xlo_done, t.times(1, NP + 1))
                need(pe, exp_done, t.times(8, h - 3))
                transposed(bank_a, 1, h, k_done)

            def q_transposed(t, h):
                need(pe, exp_done, t.times(8, h - 1))
                transposed(bank_b, 0, h, q_done)

            def v_rows(t, s):
                pe.wait_ge(klo_done, t.times(C, 2 * s + 2))
                for c in range(C):
                    for xs, w in ((xT_hi, w_hi), (xT_hi, w_lo), (xT_lo, w_hi)):
                        last = nc.tensor.matmul(bank_a[:, s], xs[:, c, s, :], w[:, 2, c, :],
                                                start=(c == 0 and w is w_hi and xs is xT_hi),
                                                stop=(c == C - 1 and xs is xT_lo))
                last.then_inc(v_done, 1)

            def turn_y(t, s):
                if early(t, s):
                    pe.wait_ge(y_normed, t.times(2, 1))
                else:
                    pe.wait_ge(y_normed, t.times(2, 2))
                for c in range(C):
                    last = nc.tensor.transpose(z_bank(t, s)[:, c * T:(c + 1) * T], y[:, s, c * P:(c + 1) * P], ident[:])
                last.then_inc(y_turned, 1)

            def rough(t, n):
                s, c, bank = n // C, n % C, chunk_bank[(n + 2) % 4]
                if n == 0:
                    pe.wait_ge(k_spread_in, t.times(64, 64))
                if n < 2:
                    pe.wait_ge(qlo_done, t.times(C, 2 * n + 2))
                    pe.wait_ge(qhi_done, t.times(C, C))
                elif n < 4:
                    if n == 2:
                        pe.wait_ge(qlo_done, t.times(C, C))
                    pe.wait_ge(v_read, t.times(2, n - 1))
                else:
                    pe.wait_ge(max_done, t.times(8, n - 3))
                nc.tensor.matmul(bank, g["three"][:],
                                 g["mask_rows"][:, bass.ds(t.times(2 * T, s * T), T)].unsqueeze(1).broadcast_to([P, HC, T]),
                                 start=True, stop=False)
                nc.tensor.matmul(bank, qT[:, 0, c, s, :], k_wide[:, c, s].rearrange("p h t -> p (h t)"),
                                 start=False, stop=True).then_inc(rough_done, 1)

            def turn_max(t):
                pe.wait_ge(max_done, t.times(8, 8))
                need(pe, y_read, t.times(2, 0))
                nc.tensor.transpose(bank_y[0:2 * H, 0, 0:P], shift_q[:], ident[:]).then_inc(max_turned, 1)

            def scores(t, n):
                s, c, bank = n // C, n % C, chunk_bank[n % 4]
                if n < 2:
                    if n == 0:
                        pe.wait_ge(shift_split, t.times(1, 1))
                        pe.wait_ge(spread_in, t.times(64, 64))
                        if is_slot(t, 0):
                            pe.wait_ge(ready, 2)
                            pe.wait_ge(picked, 1)
                elif n < 4:
                    need(pe, out_read, t.times(2, n - 3))
                else:
                    pe.wait_ge(exp_done, t.times(8, n - 3))
                for k, (ks, qs) in enumerate(((0, 0), (0, 1), (1, 0))):
                    nc.tensor.matmul(bank, kT[:, ks, c, s, :], q_wide[:, qs, c, s].rearrange("p h t -> p (h t)"),
                                     start=(k == 0), stop=False)
                for h in range(HC):
                    r = s * H + c * HC + h
                    last = nc.tensor.matmul(bank[:, h * T:(h + 1) * T], pick[:, r:r + 1].broadcast_to([P, T]), shift_rows[:],
                                            start=False, stop=(h == HC - 1))
                last.then_inc(score_done, 1)

            def times_v(t, n, more=True):
                s, c = n // C, n % C
                bank = (bank_y, bank_t)[s]
                if n == 0:
                    pe.wait_ge(v_masked, t.times(2, 2))
                if n == C:
                    if more:
                        pe.wait_ge(xhi_done, t.times(1, NP + 2))
                        pe.wait_ge(xlo_done, t.times(1, NP + 2))
                    else:
                        pe.wait_ge(z_scaled, t.times(2, 0))
                pe.wait_ge(exp_done, t.times(8, n + 1))
                for h in range(HC):
                    k = (c % 2) * HC + h
                    last = nc.tensor.matmul(bank[:, c // 2, k * V1:(k + 1) * V1], prob[:, n % 4, h, :],
                                            v[:, s, c * HC + h, :], start=True, stop=True)
                last.then_inc(pv_done, 1)

            def out_rows(t, s, after):
                if after is not None:
                    pe.wait_ge(max_done, after.times(8, C + s + 1))
                pe.wait_ge(uhi_done, t.times(2, s + 1))
                pe.wait_ge(ulo_done, t.times(2, s + 1))
                for c in range(C):
                    for us, w in ((u_hi, w_hi), (u_hi, w_lo), (u_lo, w_hi)):
                        last = nc.tensor.matmul(out_bank(t, s), us[:, s, c, :], w[:, 3, c, :],
                                                start=(c == 0 and us is u_hi and w is w_hi),
                                                stop=(c == C - 1 and us is u_lo))
                last.then_inc(out_done, 1)

            def slot(t, first, live, more):
                before = t.plus(-1)
                if live:
                    k_transposed(t, 0)
                if not first:
                    times_v(before, 2 * C - 2)
                    times_v(before, 2 * C - 1)
                if live:
                    k_transposed(t, 1)
                    q_transposed(t, 0)
                if not first:
                    if live:
                        turn_y(before, 0)
                    turn_y(before, 1)
                if not live:
                    out_rows(before, 0, None)
                if live:
                    q_transposed(t, 1)
                    v_rows(t, 0)
                    v_rows(t, 1)
                    for n in range(C):
                        rough(t, n)
                if more:
                    if not first:
                        pe.wait_ge(z_scaled, before.times(2, 2))
                    turn_x(t.plus(1))
                if live:
                    for n in range(C, 2 * C):
                        rough(t, n)
                if not first and live:
                    out_rows(before, 0, t)
                if live:
                    turn_max(t)
                if not first:
                    out_rows(before, 1, t if live else None)
                if live:
                    for n in range(2 * C):
                        scores(t, n)
                        if n >= 2:
                            times_v(t, n - 2, more)
                        if n == 2 * C - 1 and not more:
                            turn_y(t, 0)

            slots(pe, slot)

        @block.vector
        def _(dve):
            def x_stats(t):
                u = t.plus(NP)
                dve.wait_ge(x_in[t.par], 16 * u.use())
                for s in range(2):
                    nc.vector.bn_stats(stats[:, s, :], x[:, t.par, s, :]).then_inc(stats_done, 1)
                dve.wait_ge(stats_done, u.times(2, 2))
                nc.vector.memset(idle[:], 0.0)
                for s in range(2):
                    last = nc.vector.bn_aggr(moments[:, s, :], stats[:, s, :])
                last.then_inc(moments_done, 1)

            def x_norm(t):
                u = t.plus(NP)
                dve.wait_ge(rstd_done, u.times(1, 1))
                for s in range(2):
                    nc.vector.tensor_scalar(x[:, t.par, s, :], x[:, t.par, s, :], moments[:, s, 0:1], rstd[:, s:s + 1],
                                            ALU.subtract, ALU.mult).then_inc(x_normed, 1)

            def x_lower(t):
                u = t.plus(NP)
                dve.wait_ge(xhi_done, u.times(1, 1))
                nc.vector.tensor_tensor(out=xT_lo[:].rearrange("p c s t -> p s c t"),
                                        in0=bank_t[:].rearrange("p s (c t) -> p s c t", c=C),
                                        in1=xT_hi[:].bitcast(F32).rearrange("p c s t -> p s c t"),
                                        op=ALU.subtract).then_inc(xlo_done, 1)

            def lower(t, dst, banks, m, h, hi_done, signal):
                dve.wait_ge(hi_done, t.times(C, 2 * h + 2))
                for f in (2 * h, 2 * h + 1):
                    nc.vector.scalar_tensor_tensor(
                        out=dst[:, 1, f].rearrange("p s t -> p (s t)"),
                        in0=banks[:, f // 2, (f % 2) * 2 * T:(f % 2 + 1) * 2 * T], scalar=g["bqk"][:, m, f:f + 1],
                        in1=dst[:, 0, f].bitcast(F32).rearrange("p s t -> p (s t)"),
                        op0=ALU.add, op1=ALU.subtract).then_inc(signal, 1)

            def v_read_out(t, s):
                need(dve, pv_done, t.times(8, 0))
                dve.wait_ge(v_done, t.times(2, s + 1))
                nc.vector.tensor_tensor(out=v[:, s, :, 0:DH], in0=bank_a[:, s].rearrange("p (h d) -> p h d", h=H),
                                        in1=g["bv"][:, 1, :].rearrange("p (h d) -> p h d", h=H),
                                        op=ALU.add).then_inc(v_read, 1)

            def maxima(t, n):
                need(dve, max_turned, t.times(1, 0))
                dve.wait_ge(rough_done, t.times(8, n + 1))
                nc.vector.tensor_reduce(shift_q[:, n * HC:(n + 1) * HC],
                                        chunk_bank[(n + 2) % 4].rearrange("p (h t) -> p h t", h=HC),
                                        AX.X, ALU.max, negate=True).then_inc(max_done, 1)

            def split_shift(t):
                need(dve, score_done, t.times(8, 0))
                dve.wait_ge(max_turned, t.times(1, 1))
                nc.vector.tensor_copy(shift_rows[0:2 * H, :], bank_y[0:2 * H, 0, 0:P]).then_inc(picked, 1)
                dve.wait_ge(picked, t.times(1, 2))
                nc.vector.tensor_tensor(out=shift_rows[2 * H:4 * H, :], in0=bank_y[0:2 * H, 0, 0:P],
                                        in1=shift_rows[0:2 * H, :], op=ALU.subtract).then_inc(shift_split, 1)

            def y_read_out(t, s):
                src = (bank_y, bank_t)[s][:, :, 0:2 * HC * V1].rearrange("p b (h d) -> p b h d", d=V1)
                dve.wait_ge(pv_done, t.times(8, 4 * s + 4))
                nc.vector.reciprocal(y_sum[:, s, :].rearrange("p (b h) -> p b h", b=2),
                                     src[:, :, :, DH]).then_inc(y_summed, 1)
                need(dve, y_turned, t.times(2, s - 1))
                dve.wait_ge(y_summed, t.times(2, s + 1))
                nc.vector.tensor_tensor(
                    out=y[:, s].rearrange("p (b h d) -> p b h d", b=2, d=DH), in0=src[:, :, :, 0:DH],
                    in1=y_sum[:, s, :].rearrange("p (b h) -> p b h", b=2).unsqueeze(3).broadcast_to([P, 2, H // 2, DH]),
                    op=ALU.mult).then_inc(y_read, 1)
                dve.wait_ge(y_read, t.times(2, s + 1))
                nc.vector.bn_stats(y_stats[:, s, :], y[:, s]).then_inc(y_stats_done, 1)
                dve.wait_ge(y_stats_done, t.times(2, s + 1))
                nc.vector.memset(idle[:], 0.0)
                nc.vector.bn_aggr(y_moments[:, s, :], y_stats[:, s, :]).then_inc(y_moments_done, 1)

            def y_norm(t, s):
                dve.wait_ge(y_rstd_done, t.times(2, s + 1))
                nc.vector.tensor_scalar(y[:, s], y[:, s], y_moments[:, s, 0:1], y_rstd[:, s:s + 1],
                                        ALU.subtract, ALU.mult).then_inc(y_normed, 1)

            def z_scale(t, s):
                need(dve, ulo_done, t.times(2, s - 1))
                dve.wait_ge(y_turned, t.times(2, s + 1))
                nc.vector.tensor_tensor(out=z[:, s], in0=z_bank(t, s).rearrange("p (c t) -> p c t", c=C),
                                        in1=factor[:, t.par, s, :].unsqueeze(2).broadcast_to([P, C, T]),
                                        op=ALU.mult).then_inc(z_scaled, 1)

            def u_form(t, s):
                dve.wait_ge(tanh_done, t.times(2, s + 1))
                nc.vector.scalar_tensor_tensor(out=z[:, s], in0=z_tanh[:, s], scalar=1.0, in1=z[:, s],
                                               op0=ALU.add, op1=ALU.mult).then_inc(u_done, 1)

            def u_lower(t, s):
                need(dve, out_done, t.times(2, s - 1))
                dve.wait_ge(uhi_done, t.times(2, s + 1))
                nc.vector.tensor_tensor(out=u_lo[:, s], in0=z[:, s], in1=u_hi[:, s].bitcast(F32),
                                        op=ALU.subtract).then_inc(ulo_done, 1)

            def out_add(t, s):
                dve.wait_ge(res_biased, t.times(1, 1))
                dve.wait_ge(out_done, t.times(2, s + 1))
                nc.vector.tensor_tensor(out=res[:, t.par, s, :], in0=out_bank(t, s), in1=res[:, t.par, s, :],
                                        op=ALU.add).then_inc(out_read, 1)

            def columns(t):
                need(dve, z_done, t.times(2, -2))
                need(dve, exp_done, t.times(8, -8))
                both = bass.ds(t.times(2), 2)
                nc.vector.tensor_copy(factor[:, t.par], g["film"][:, 1, 0, both, :])
                nc.vector.tensor_copy(shift[:, t.par], g["film"][:, 1, 1, both, :])
                nc.vector.tensor_copy(keep[:, t.par], g["score_keep"][:, both])
                nc.vector.tensor_copy(off[:, t.par], g["score_off"][:, both]).then_inc(columns_done, 1)

            def slot(t, first, live, more):
                before = t.plus(-1)
                if not first:
                    y_read_out(before, 1)
                if not live:
                    u_form(before, 0)
                    u_lower(before, 0)
                if more:
                    x_stats(t.plus(1))
                if live:
                    columns(t)
                if not first:
                    y_norm(before, 1)
                if live:
                    lower(t, kT, bank_a, 1, 0, khi_done, klo_done)
                    lower(t, kT, bank_a, 1, 1, khi_done, klo_done)
                if more:
                    x_norm(t.plus(1))
                if not first:
                    if live:
                        z_scale(before, 0)
                    z_scale(before, 1)
                if live:
                    lower(t, qT, bank_b, 0, 0, qhi_done, qlo_done)
                if not first:
                    if live:
                        u_form(before, 0)
                    u_form(before, 1)
                if live:
                    lower(t, qT, bank_b, 0, 1, qhi_done, qlo_done)
                if not first:
                    if live:
                        u_lower(before, 0)
                    u_lower(before, 1)
                if live:
                    v_read_out(t, 0)
                    v_read_out(t, 1)
                    for n in range(2 * C):
                        maxima(t, n)
                    split_shift(t)
                if more:
                    x_lower(t.plus(1))
                if not first:
                    out_add(before, 0)
                    out_add(before, 1)
                if live:
                    y_read_out(t, 0)
                    y_norm(t, 0)
                    if not more:
                        z_scale(t, 0)

            nc.vector.tensor_tensor(out=pick[:], in0=ident[:, 0:2 * H], in1=ident[:, 2 * H:4 * H],
                                    op=ALU.add).then_inc(picked, 1)
            nc.vector.memset(v[:], 1.0).then_inc(ready, 1)
            nc.vector.memset(shift_rows[:], 0.0).then_inc(ready, 1)
            dve.wait_ge(ready, 2)
            dve.wait_ge(picked, 1)
            slots(dve, slot)


def build(nc, a, out):
    mid = nc.dram_tensor("layer0_out", [B, T, D], F32).ap()
    with ExitStack() as ctx:
        def sb(name, shape, dt=F32, c=ctx):
            return c.enter_context(nc.sbuf_tensor(name, shape, dt))

        g = {}
        g["ident"] = sb("ident", [P, P])
        g["three"] = sb("three", [P, P], BF16)
        g["w_hi"] = sb("w_hi", [P, 4, C, D], F32R)
        g["w_lo"] = sb("w_lo", [P, 4, C, D], F32R)
        g["bv"] = sb("bv", [P, 2, D])
        g["bo"] = sb("bo", [P, 2, D])
        g["vec"] = sb("vec", [P, ALL_ROWS])
        g["film"] = sb("film", [P, 2, 2, B, C])
        g["eps"] = sb("eps", [P, 2])
        g["power"] = sb("power", [P, 2])
        g["bqk"] = sb("bqk", [P, 2, C])
        g["valid"] = sb("valid", [P, B])
        g["score_keep"] = sb("score_keep", [P, B])
        g["score_off"] = sb("score_off", [P, B])
        g["x"] = sb("x", [P, 2, 2, D])
        g["stats"] = sb("stats", [P, 2, 6])
        g["moments"] = sb("moments", [P, 2, 2])
        g["rstd"] = sb("rstd", [P, 2])
        g["xT_hi"] = sb("xT_hi", [P, C, 2, T], F32R)
        g["xT_lo"] = sb("xT_lo", [P, C, 2, T], F32R)
        g["res"] = sb("res", [P, 2, 2, D])
        g["mid_stored"] = [ctx.enter_context(nc.semaphore(f"mid_stored{n}")) for n in range(2)]
        g["x_in"] = [ctx.enter_context(nc.semaphore(f"x_in{n}")) for n in range(2)]
        g["x_chain"] = [ctx.enter_context(nc.semaphore(n)) for n in (
            "stats_done moments_done eps_added rstd_done x_normed x_turned xhi_done xlo_done").split()]
        g["mask_rows"] = sb("mask_rows", [P, B * T], BF16)

        layer0(nc, a, g, mid)
        layer1(nc, a, g, mid, out)


_L0 = ["norm_scale", "norm_bias", "film_norm_scale", "film_norm_bias", "film_emb_b"]
_L1 = ["norm_w", "norm_b", "sb_norm_w", "sb_norm_b", "emb_b", "q_b", "k_b"]
_W0, _W1 = ["Wq", "Wk", "Wv", "film_out_W"], ["q_w", "k_w", "v_w", "out_w"]
_B0, _B1 = ["bq", "bk", "bv", "film_out_b"], ["q_b", "k_b", "v_b", "out_b"]


def kernel(**inputs):
    import numpy as _np
    import concourse.bacc as _bacc
    from concourse import mybir as _mybir
    from concourse.bass_utils import run_bass_kernel_spmd as _run

    nc = _bacc.Bacc("TRN2", target_bir_lowering=False, num_devices=1)
    arrays, ap = {}, {}
    for name in inputs:
        x = _np.ascontiguousarray(inputs[name])
        arrays[f"in_{name}_dram"] = x
        ap[name] = nc.dram_tensor(f"in_{name}_dram", x.shape, _mybir.dt.from_np(x.dtype), kind="ExternalInput").ap()
    out = nc.dram_tensor("out_0_dram", (B, T, D), _mybir.dt.float32, kind="ExternalOutput").ap()
    names = (("L0_cond_", _L0, _W0, _B0, "film_emb_W"), ("L1_cond_", _L1, _W1, _B1, "emb_w"))
    args = {
        "x": ap["x"], "cond": ap["cond_2048"], "mask0": ap["mask_BxS_ik0"], "mask1": ap["mask_BxS_ff1"],
        "vectors": [[(ap[pre + v], r) for v, r in zip(vecs, (NS, NB, FS, FB, EB, QB, KB))] for pre, vecs, _, _, _ in names],
        "w": [[ap[pre + w] for w in ws] for pre, _, ws, _, _ in names],
        "b": [[ap[pre + b] for b in bs] for pre, _, _, bs, _ in names],
        "emb_w": [ap[pre + e] for pre, _, _, _, e in names],
    }
    build(nc, args, out)
    r = _run(nc, [arrays], core_ids=[0])
    return r.results[0]["out_0_dram"]
```
